# Optimizing a Trainium2 kernel written in Bass

```python
import numpy as np
import jax
import jax.numpy as jnp

def _softmax(x, axis=-1):
    return jax.nn.softmax(x, axis=axis)

def _gelu(x):
    return jax.nn.gelu(x, approximate=True)

def _silu(x):
    return jax.nn.silu(x)

def _sigmoid(x):
    return jax.nn.sigmoid(x)

def _layernorm(x, axis=-1, eps=1e-05):
    m = jnp.mean(x, axis=axis, keepdims=True)
    v = jnp.var(x, axis=axis, keepdims=True)
    return (x - m) / jnp.sqrt(v + eps)

def _scatter_add(tgt, idx, src, axis=0):
    return tgt.at[idx].add(src)

def _segment_sum(src, seg, n):
    return jax.ops.segment_sum(src, seg, n)
kernel_name = 'mk_macaron_d2_jaxref_r8_9ac717'

def setup_inputs(seed: int=0):
    np.random.seed(seed)
    _w = jnp.asarray

    def _L0_attn_setup():
        import jax, jax.numpy as jnp
        import numpy as np
        EPS = 1e-06
        NUM_HEADS = 16

        def _split_heads(t, b, s, h, hd):
            return t.reshape(b, s, h, hd).transpose(0, 2, 1, 3)
        key = jax.random.key(seed)
        ks = jax.random.split(key, 6)
        B, S, D = (8, 128, 128)
        scale = 1.0 / np.sqrt(D)
        x = jax.random.normal(ks[0], (B, S, D), dtype=jnp.float32)
        Wq = jax.random.normal(ks[1], (D, D), dtype=jnp.float32) * scale
        Wk = jax.random.normal(ks[2], (D, D), dtype=jnp.float32) * scale
        Wv = jax.random.normal(ks[3], (D, D), dtype=jnp.float32) * scale
        Wo = jax.random.normal(ks[4], (D, D), dtype=jnp.float32) * scale
        bq = jnp.zeros((D,), jnp.float32)
        bk = jnp.zeros((D,), jnp.float32)
        bv = jnp.zeros((D,), jnp.float32)
        bo = jnp.zeros((D,), jnp.float32)
        qk_scale = jnp.full((1, 1, 1, 1), np.log2(S ** 2 - S + EPS), dtype=jnp.float32)
        return {'x': x, 'Wq': Wq, 'bq': bq, 'Wk': Wk, 'bk': bk, 'Wv': Wv, 'bv': bv, 'Wo': Wo, 'bo': bo, 'qk_scale': qk_scale}
    _L0_attn_in = _L0_attn_setup()

    def _L0_ffn_setup():
        import jax, jax.numpy as jnp
        import numpy as np
        TOP_P = 0.3
        key = jax.random.key(seed)
        k1, k2, k3, k4 = jax.random.split(key, 4)
        B, S, D, H, E = (4, 512, 128, 128, 8)
        x = jax.random.normal(k1, (B, S, D), dtype=jnp.float32)
        gate_W = jax.random.normal(k2, (E, D), dtype=jnp.float32) / np.float32(np.sqrt(D))
        expert_W = jax.random.normal(k3, (E, H, D), dtype=jnp.float32) / np.float32(np.sqrt(D))
        out_W = jax.random.normal(k4, (D, H), dtype=jnp.float32) / np.float32(np.sqrt(H))
        return {'x': x, 'gate_W': gate_W, 'expert_W': expert_W, 'out_W': out_W}
    _L0_ffn_in = _L0_ffn_setup()

    def _L1_attn_setup():
        import jax, jax.numpy as jnp
        import numpy as np
        B, T, D = (4, 256, 128)
        NHEAD = 16
        HEAD_DIM = D // NHEAD

        def _rope_cache(seq_len, dim):
            inv_freq = 1.0 / 10000.0 ** (jnp.arange(0, dim, 2, dtype=jnp.float32) / dim)
            t = jnp.arange(seq_len, dtype=jnp.float32)
            freqs = jnp.outer(t, inv_freq)
            return (jnp.cos(freqs), jnp.sin(freqs))

        def _apply_rope(x, cos, sin):
            d2 = x.shape[-1] // 2
            x1, x2 = (x[..., :d2], x[..., d2:])
            cos = cos[None, None]
            sin = sin[None, None]
            return jnp.concatenate([x1 * cos - x2 * sin, x2 * cos + x1 * sin], axis=-1)
        key = jax.random.key(seed)
        ks = jax.random.split(key, 5)
        s = 1.0 / np.sqrt(D)
        x = jax.random.normal(ks[0], (B, T, D), dtype=jnp.float32)
        Wqkv = jax.random.uniform(ks[1], (3 * D, D), jnp.float32, -s, s)
        bqkv = jax.random.uniform(ks[2], (3 * D,), jnp.float32, -s, s)
        Wout = jax.random.uniform(ks[3], (D, D), jnp.float32, -s, s)
        bout = jax.random.uniform(ks[4], (D,), jnp.float32, -s, s)
        return {'x': x, 'Wqkv': Wqkv, 'bqkv': bqkv, 'Wout': Wout, 'bout': bout}
    _L1_attn_in = _L1_attn_setup()

    def _L1_ffn_setup():
        import jax, jax.numpy as jnp
        import numpy as np
        B, S, D = (2, 256, 128)
        E, G, K = (32, 8, 4)
        H, SH = (256, 256)
        CAP_FACTOR = 1.25

        def _l2norm(v):
            n = jnp.linalg.norm(v, axis=-1, keepdims=True)
            return v / jnp.maximum(n, 1e-12)
        key = jax.random.key(seed)
        ks = jax.random.split(key, 10)
        x = jax.random.normal(ks[0], (B, S, D), jnp.float32)
        group_centroids = jax.random.normal(ks[1], (G, D), jnp.float32) * 0.02
        expert_centroids = jax.random.normal(ks[2], (E, D), jnp.float32) * 0.02
        bias = jnp.zeros((E,), jnp.float32)
        sd_in = 1.0 / np.sqrt(D).astype(np.float32)
        sd_h = 1.0 / np.sqrt(H).astype(np.float32)
        wg = jax.random.normal(ks[3], (E, D, H), jnp.float32) * sd_in
        wu = jax.random.normal(ks[4], (E, D, H), jnp.float32) * sd_in
        wd = jax.random.normal(ks[5], (E, H, D), jnp.float32) * sd_h
        sg = jax.random.normal(ks[6], (D, SH), jnp.float32) * sd_in
        su = jax.random.normal(ks[7], (D, SH), jnp.float32) * sd_in
        sd_w = jax.random.normal(ks[8], (SH, D), jnp.float32) * sd_h
        return dict(x=x, group_centroids=group_centroids, expert_centroids=expert_centroids, bias=bias, wg=wg, wu=wu, wd=wd, sg=sg, su=su, sd=sd_w)
    _L1_ffn_in = _L1_ffn_setup()
    _d = {'L0_attn_x': _L0_attn_in['x'], 'L0_attn_Wq': _L0_attn_in['Wq'], 'L0_attn_bq': _L0_attn_in['bq'], 'L0_attn_Wk': _L0_attn_in['Wk'], 'L0_attn_bk': _L0_attn_in['bk'], 'L0_attn_Wv': _L0_attn_in['Wv'], 'L0_attn_bv': _L0_attn_in['bv'], 'L0_attn_Wo': _L0_attn_in['Wo'], 'L0_attn_bo': _L0_attn_in['bo'], 'L0_attn_qk_scale': _L0_attn_in['qk_scale'], 'L0_ffn_gate_W': _L0_ffn_in['gate_W'], 'L0_ffn_expert_W': _L0_ffn_in['expert_W'], 'L0_ffn_out_W': _L0_ffn_in['out_W'], 'L1_attn_Wqkv': _L1_attn_in['Wqkv'], 'L1_attn_bqkv': _L1_attn_in['bqkv'], 'L1_attn_Wout': _L1_attn_in['Wout'], 'L1_attn_bout': _L1_attn_in['bout'], 'L1_ffn_group_centroids': _L1_ffn_in['group_centroids'], 'L1_ffn_expert_centroids': _L1_ffn_in['expert_centroids'], 'L1_ffn_bias': _L1_ffn_in['bias'], 'L1_ffn_wg': _L1_ffn_in['wg'], 'L1_ffn_wu': _L1_ffn_in['wu'], 'L1_ffn_wd': _L1_ffn_in['wd'], 'L1_ffn_sg': _L1_ffn_in['sg'], 'L1_ffn_su': _L1_ffn_in['su'], 'L1_ffn_sd': _L1_ffn_in['sd']}
    _x0 = _d['L0_attn_x']
    _d['L0_attn_x'] = jax.random.normal(jax.random.fold_in(jax.random.key(seed), 1), (1, 2048, 128), dtype=_x0.dtype)
    del _x0
    return _d

def reference(L0_attn_x, L0_attn_Wq, L0_attn_bq, L0_attn_Wk, L0_attn_bk, L0_attn_Wv, L0_attn_bv, L0_attn_Wo, L0_attn_bo, L0_attn_qk_scale, L0_ffn_gate_W, L0_ffn_expert_W, L0_ffn_out_W, L1_attn_Wqkv, L1_attn_bqkv, L1_attn_Wout, L1_attn_bout, L1_ffn_group_centroids, L1_ffn_expert_centroids, L1_ffn_bias, L1_ffn_wg, L1_ffn_wu, L1_ffn_wd, L1_ffn_sg, L1_ffn_su, L1_ffn_sd):

    def _L0_attn_ref(x, Wq, bq, Wk, bk, Wv, bv, Wo, bo, qk_scale):
        import jax, jax.numpy as jnp
        import numpy as np
        EPS = 1e-06
        NUM_HEADS = 16

        def _split_heads(t, b, s, h, hd):
            return t.reshape(b, s, h, hd).transpose(0, 2, 1, 3)
        b, s, d = x.shape
        h = NUM_HEADS
        hd = d // h
        q = _split_heads(x @ Wq + bq, b, s, h, hd)
        k = _split_heads(x @ Wk + bk, b, s, h, hd)
        v = _split_heads(x @ Wv + bv, b, s, h, hd)
        q = q / (jnp.linalg.norm(q, axis=-1, keepdims=True) + EPS)
        k = k / (jnp.linalg.norm(k, axis=-1, keepdims=True) + EPS)
        logits = jnp.einsum('bhtd,bhsd->bhts', q, k) * qk_scale
        weights = jax.nn.softmax(logits, axis=-1)
        out = jnp.einsum('bhts,bhsd->bhtd', weights, v)
        out = out.transpose(0, 2, 1, 3).reshape(b, s, d)
        return out @ Wo + bo

    def _L0_ffn_ref(x, gate_W, expert_W, out_W):
        import jax, jax.numpy as jnp
        import numpy as np
        TOP_P = 0.3
        B, S, D = x.shape
        E = gate_W.shape[0]
        N = B * S
        p = jax.nn.softmax(jnp.einsum('bsd,ed->bse', x, gate_W), axis=-1).reshape(N, E)
        tpi = (p > TOP_P).astype(jnp.int32)
        cnt = jnp.sum(tpi[:, :, None] == jnp.arange(E)[None, None, :], axis=1)
        scale = cnt.astype(x.dtype) * p
        x2 = x.reshape(N, D)
        h = jnp.einsum('nd,ehd->neh', x2, expert_W)
        final = jnp.einsum('neh,ne->nh', h, scale)
        out = jnp.einsum('nh,dh->nd', final, out_W).reshape(B, S, D)
        return out

    def _L1_attn_ref(x, Wqkv, bqkv, Wout, bout):
        import jax, jax.numpy as jnp
        import numpy as np
        B, T, D = (4, 256, 128)
        NHEAD = 16
        HEAD_DIM = D // NHEAD

        def _rope_cache(seq_len, dim):
            inv_freq = 1.0 / 10000.0 ** (jnp.arange(0, dim, 2, dtype=jnp.float32) / dim)
            t = jnp.arange(seq_len, dtype=jnp.float32)
            freqs = jnp.outer(t, inv_freq)
            return (jnp.cos(freqs), jnp.sin(freqs))

        def _apply_rope(x, cos, sin):
            d2 = x.shape[-1] // 2
            x1, x2 = (x[..., :d2], x[..., d2:])
            cos = cos[None, None]
            sin = sin[None, None]
            return jnp.concatenate([x1 * cos - x2 * sin, x2 * cos + x1 * sin], axis=-1)
        b, t, d = x.shape
        qkv = x @ Wqkv.T + bqkv
        qkv = qkv.reshape(b, t, 3, NHEAD, HEAD_DIM).transpose(2, 0, 3, 1, 4)
        q, k, v = (qkv[0], qkv[1], qkv[2])
        cos, sin = _rope_cache(t, HEAD_DIM)
        q = _apply_rope(q, cos, sin)
        k = _apply_rope(k, cos, sin)
        scale = jnp.sqrt(jnp.float32(HEAD_DIM))
        attn = jnp.einsum('bhqd,bhkd->bhqk', q, k) / scale
        attn = jax.nn.softmax(attn, axis=-1)
        out = jnp.einsum('bhqk,bhkd->bhqd', attn, v)
        out = out.transpose(0, 2, 1, 3).reshape(b, t, d)
        return out @ Wout.T + bout

    def _L1_ffn_ref(x, group_centroids, expert_centroids, bias, wg, wu, wd, sg, su, sd):
        import jax, jax.numpy as jnp
        import numpy as np
        B, S, D = (2, 256, 128)
        E, G, K = (32, 8, 4)
        H, SH = (256, 256)
        CAP_FACTOR = 1.25

        def _l2norm(v):
            n = jnp.linalg.norm(v, axis=-1, keepdims=True)
            return v / jnp.maximum(n, 1e-12)
        b, s, d = x.shape
        xf = x.reshape(-1, d)
        N = xf.shape[0]
        shared = jax.nn.silu(xf @ sg) * (xf @ su) @ sd
        xn = _l2norm(xf)
        group_scores = xn @ _l2norm(group_centroids).T
        n_top_groups = max(1, G // 2)
        _, top_group_idx = jax.lax.top_k(group_scores, n_top_groups)
        expert_scores = xn @ _l2norm(expert_centroids).T + bias
        expert_to_group = jnp.arange(E) // (E // G)
        sel = jnp.zeros((N, G), xf.dtype).at[jnp.arange(N)[:, None], top_group_idx].set(1.0)
        group_mask = sel[:, expert_to_group]
        masked = expert_scores * group_mask + (1.0 - group_mask) * -1000000000.0
        top_scores, top_idx = jax.lax.top_k(masked, K)
        gates = jax.nn.softmax(top_scores, axis=-1)
        capacity = max(1, int(N / E * K * CAP_FACTOR))
        flat_e = top_idx.reshape(-1)
        flat_g = gates.reshape(-1)
        tok = jnp.repeat(jnp.arange(N), K)
        onehot = jax.nn.one_hot(flat_e, E, dtype=jnp.int32)
        pos = jnp.cumsum(onehot, axis=0)[jnp.arange(N * K), flat_e] - 1
        keep = pos < capacity
        e_s = jnp.where(keep, flat_e, E)
        p_s = jnp.where(keep, pos, 0)
        buf = jnp.zeros((E + 1, capacity, d), xf.dtype).at[e_s, p_s].set(xf[tok])[:E]
        h = jax.nn.silu(jnp.einsum('ecd,edh->ech', buf, wg)) * jnp.einsum('ecd,edh->ech', buf, wu)
        out_e = jnp.einsum('ech,ehd->ecd', h, wd)
        gathered = out_e[flat_e, jnp.minimum(pos, capacity - 1)]
        contrib = gathered * (flat_g * keep.astype(xf.dtype))[:, None]
        routed = jnp.zeros_like(xf).at[tok].add(contrib)
        return (shared + routed).reshape(b, s, d)
    x = L0_attn_x
    x = x + 0.5 * _L0_ffn_ref(_layernorm(x, axis=-1), L0_ffn_gate_W, L0_ffn_expert_W, L0_ffn_out_W)
    x = x + _L0_attn_ref(_layernorm(x, axis=-1), L0_attn_Wq, L0_attn_bq, L0_attn_Wk, L0_attn_bk, L0_attn_Wv, L0_attn_bv, L0_attn_Wo, L0_attn_bo, L0_attn_qk_scale)
    x = x + 0.5 * _L0_ffn_ref(_layernorm(x, axis=-1), L0_ffn_gate_W, L0_ffn_expert_W, L0_ffn_out_W)
    x = x + 0.5 * _L1_ffn_ref(_layernorm(x, axis=-1), L1_ffn_group_centroids, L1_ffn_expert_centroids, L1_ffn_bias, L1_ffn_wg, L1_ffn_wu, L1_ffn_wd, L1_ffn_sg, L1_ffn_su, L1_ffn_sd)
    x = x + _L1_attn_ref(_layernorm(x, axis=-1), L1_attn_Wqkv, L1_attn_bqkv, L1_attn_Wout, L1_attn_bout)
    x = x + 0.5 * _L1_ffn_ref(_layernorm(x, axis=-1), L1_ffn_group_centroids, L1_ffn_expert_centroids, L1_ffn_bias, L1_ffn_wg, L1_ffn_wu, L1_ffn_wd, L1_ffn_sg, L1_ffn_su, L1_ffn_sd)
    return x

_drawn_inputs = setup_inputs


def setup_inputs(seed=0):
    import zlib

    import numpy as np

    out = dict(_drawn_inputs(seed))
    spreads = {'L0_attn_bq': (0.0, 0.1),
     'L0_attn_bk': (0.0, 0.1),
     'L0_attn_bv': (0.0, 0.1),
     'L0_attn_bo': (0.0, 0.1),
     'L1_ffn_bias': (0.0, 0.1)}
    factors = {}
    for name, (base, spread) in spreads.items():
        noise = np.random.default_rng([zlib.crc32(name.encode()), seed]).standard_normal(out[name].shape)
        drawn = base * np.exp(spread * noise) if base else spread * noise
        out[name] = jnp.asarray(drawn.astype(out[name].dtype))
    for name, factor in factors.items():
        out[name] = (out[name] * factor).astype(out[name].dtype)
    return out
```

```python
from contextlib import ExitStack
from collections import namedtuple

import numpy as np

import concourse.bass as bass
from concourse import mybir

F32 = mybir.dt.float32
BF16 = mybir.dt.bfloat16
I32 = mybir.dt.int32
U32 = mybir.dt.uint32
ALU = mybir.AluOpType
ACT = mybir.ActivationFunctionType
AX = mybir.AxisListType

P = 128
NTOK = 2048
NT = NTOK // P
CH = 512
NCH = NTOK // CH
TPC = CH // P
LN_EPS = 1e-5

E0 = 8
TOP_P = 0.3

NH = 16
HD = P // NH
QUADS = NH // 4
ITERS = QUADS * NCH
CHUNKS = 2 * NT
VW = HD + 1
PRING = 8
NORM_EPS = 1e-6
RUNS_K = ((0, 3), (0, 2), (0, 1))
RUNS_Q = ((0, 3), (1, 3), (2, 3))
SHIFT_ROW = 6 * HD

NE = 32
NG = 8
TOPG = NG // 2
TOPK = 4
HID = 256
CAP = int(NTOK / NE * TOPK * 1.25)
RT = (CAP + P - 1) // P
BUF = RT * P
ROWS = NE * BUF
TAIL = CAP - (RT - 1) * P
RING = 4
FAR = float(2 * ROWS)

C_ID, C_PERM, C_ROT, C_G, C_U, C_ONE, C_PAD = 0, 128, 256, 384, 512, 640, 768
C_I8 = C_PAD + QUADS * P
C_I32 = C_I8 + NG
C_BASE = C_I32 + NE
C_RES = C_BASE + NE
C_END = C_RES + NT


def constants():
    c = np.zeros((P, C_END), np.float32)
    i = np.arange(P)
    c[:, C_ID:C_ID + P] = np.eye(P)
    for h in range(NH):
        for d in range(HD):
            m = NH * d + h
            c[HD * h + d, C_PERM + m] = 1.0
            half = HD // 2
            c[HD * h + (d + half) % HD, C_ROT + m] = -1.0 if d < half else 1.0
    c[:, C_G:C_G + P] = (i[:, None] % NH) == (i[None, :] % NH)
    c[:, C_U:C_U + P] = i[:, None] < i[None, :]
    c[:, C_ONE:C_ONE + P] = 1.0
    for h in range(NH):
        for d in range(HD):
            c[h * HD + d, C_PAD + (h // 4) * P + 32 * (h % 4) + d] = 1.0
    c[:, C_I8:C_I8 + NG] = np.arange(NG)
    c[:, C_I32:C_I32 + NE] = np.arange(NE)
    c[:, C_BASE:C_BASE + NE] = np.arange(NE) * BUF
    c[:, C_RES:C_RES + NT] = 1.0
    c[:, C_RES] = 0.0
    inv = (np.float32(1.0) / np.float32(10000.0) ** (np.arange(0, HD, 2, dtype=np.float32) / np.float32(HD)))
    ang = np.outer(np.arange(NTOK, dtype=np.float32), inv.astype(np.float32)).astype(np.float32)
    ang = ang[:, (i // NH) % (HD // 2)].T
    return c, np.ascontiguousarray(np.cos(ang), np.float32), np.ascontiguousarray(np.sin(ang), np.float32)


def build(nc, a, consts_d, cos_d, sin_d, out, stages=6):
    ctx = ExitStack()
    with ctx:
        def sb(name, shape, dt=F32):
            return ctx.enter_context(nc.sbuf_tensor(name, shape, dt))

        def sem(name):
            return ctx.enter_context(nc.semaphore(name))

        def sems(prefix, names):
            return namedtuple(prefix, names)(*[sem(f"{prefix}_{n}") for n in names.split()])

        X = sb("X", [P, NT, P])
        XNT = sb("XNT", [P, NTOK])
        Kt = sb("Kt", [P, NH // 2, NTOK], BF16)
        Qt = sb("Qt", [P, ITERS, 4, CH], BF16)
        RA = sb("RA", [P, 8192])
        RB = sb("RB", [P, 8192])
        V = sb("V", [P, NT, P])
        raw0 = V[:, NT - 10:NT - 8, :]
        raw = V[:, NT - 8:NT, :]
        CST = sb("CST", [P, C_END])
        U16 = sb("U16", [P, 2, P], BF16)
        wcat = sb("wcat", [P, 2 * P + E0])
        w0 = sb("w0", [P, 3, P])
        w1 = sb("w1", [P, 5, P])
        wo = sb("wo", [P, 2, QUADS, P])
        wt = sb("wt", [P, 2, P])
        cen = V[0:NG + NE, 3, :]
        cen2 = V[0:NG + NE, 4, :]
        cst1 = sb("cst1", [NG + NE, 4])
        r40 = sb("r40", [P, NG + NE])
        bcol = sb("bcol", [P, 8])
        brow = sb("brow", [P, 4, P])
        bexp = sb("bexp", [P, NE])
        st = sb("st", [P, NT, 6])
        mv = sb("mv", [P, NT, 2])
        sm = sb("sm", [P, 8, NT])
        km = sb("km", [P, 8])
        PS = ctx.enter_context(nc.psum_tensor("PS", [P, 8, CH], F32))

        RA16 = RA[:, :].bitcast(BF16)
        KP = RA16[:, 0:3 * NTOK].rearrange("p (s n) -> p s n", s=3)
        QP = RA16[:, 3 * NTOK:6 * NTOK].rearrange("p (s n) -> p s n", s=3)
        SHB = RA16[:, 6 * NTOK:7 * NTOK]
        COS, SIN = RA[:, 0:NTOK], RA[:, NTOK:2 * NTOK]
        AT = RA[:, :].rearrange("p (i n) -> p i n", i=ITERS)
        wq_, wk_, t1_, t2_ = (RB[:, i * NTOK:(i + 1) * NTOK] for i in range(4))
        PR = RB[:, :].rearrange("p (s n) -> p s n", s=PRING)
        VQ = XNT[:, 0:2 * NT * 4 * VW].rearrange("p (b t h w) -> p b t h w", b=2, t=NT, h=4)
        XNA = RB[:, 3 * NTOK:4 * NTOK].rearrange("p (t d) -> p t d", t=NT)
        RS = XNT[:, NTOK - CH:NTOK]

        XN = RA[:, 0:NTOK].rearrange("p (t d) -> p t d", t=NT)
        GB = RB[:, :].rearrange("p (j d) -> p j d", j=NT * TOPK)
        SH = RA[:, NTOK:3 * NTOK].rearrange("p (k n) -> p k n", k=2)
        WR = V[:, :, :].rearrange("p a b -> p (a b)")
        OH2 = RB[:, 3 * NTOK:4 * NTOK]
        OH = RB[:, 2 * NTOK:3 * NTOK]
        EW = HID * 3
        WRING = RB[:, 0:RING * EW].rearrange("p (r n) -> p r n", r=RING)
        o = RING * EW
        XET = RB[:, o:o + 2 * CAP].rearrange("p (b n) -> p b n", b=2)
        o += 2 * CAP
        XE = RB[:, o:o + RING * BUF].rearrange("p (r c d) -> p r c d", r=RING, c=RT)
        o += RING * BUF
        HT = RB[:, o:o + 4 * CAP].rearrange("p (b k n) -> p b k n", b=2, k=2)
        o += 4 * CAP
        SIL = RB[:, o:o + 2 * CAP].rearrange("p (k n) -> p k n", k=2)
        o += 2 * CAP
        OB = RB[:, o:o + 2 * BUF].rearrange("p (b c d) -> p b c d", b=2, c=RT)
        assert o + 2 * BUF <= 4 * NTOK
        S40 = WR[:, 0:NT * (NG + NE)].rearrange("p (t e) -> p t e", t=NT)
        MSK = WR[:, 640:1152]
        POS = WR[:, 1152:1664]
        ESC = WR[:, 1664:1664 + P].rearrange("p (t g) -> p t g", t=NT)
        rtt = sb("rtt", [P, 4, P])
        top8 = rtt[:, 0, :].rearrange("p (t k) -> p t k", t=NT)
        idx8 = rtt[:, 1, :].bitcast(U32).rearrange("p (t k) -> p t k", t=NT)
        idxf = rtt[:, 2, :].rearrange("p (t k) -> p t k", t=NT)
        gmk = rtt[:, 3, :].rearrange("p (t g) -> p t g", t=NT)
        gsl = sb("gsl", [P, 4, NT * TOPK])
        gate = gsl[:, 0, :]
        slotf = gsl[:, 1, :]
        srow = gsl[:, 2, :].bitcast(U32)
        grow = gsl[:, 3, :].bitcast(U32)
        M16 = sb("M16", [P, NE * NT], BF16)
        XD = nc.dram_tensor("expert_rows", (ROWS, P), F32, kind="Internal").ap()
        OD = nc.dram_tensor("expert_out", (ROWS, P), F32, kind="Internal").ap()
        ws = RA[:, 3 * NTOK:3 * NTOK + 2 * HID].rearrange("p (k n) -> p k n", k=2)
        wsd = RA[:, 3 * NTOK + 2 * HID:3 * NTOK + 2 * HID + 2 * P].rearrange("p (k n) -> p k n", k=2)

        ident = CST[:, C_ID:C_ID + P]
        rotT = CST[:, C_ROT:C_ROT + P]
        G = CST[:, C_G:C_G + P]

        dram_x = a["L0_attn_x"].rearrange("b (t p) d -> p (b t) d", p=P)
        dram_out = out.rearrange("b (t p) d -> p (b t) d", p=P)
        wqkv_d = a["L1_attn_Wqkv"].rearrange("(s o) d -> o s d", o=P)

        s_in = sem("s_in")
        s_x = sem("s_x")
        s_tab = sem("s_tab")
        s_out = sem("s_out")
        N_IN = [0]
        dch = sem("dch")
        ach = sem("ach")
        s_x_ready = sem("s_x_ready")
        SET = sems("setup", "mm1 cp1 mm2 cp2 cen sq cn ctr zero ones onesrow fill")
        NS = sems("n", "var std xn tr xt")
        FS = {i: sems(f"f{i}", "g d e y used") for i in (0, 2)}
        AS = {i: sems(f"a{i}", "pj pj2 used sq n2 rt hi r mid parts st v vr s exp vq pv at o l0 l1 l2 l3")
              for i in (1, 4)}

        MS = {i: sems(f"m{i}", "w lg sq sr rn mk pfx fill d e slot si sh sd sdu sc xt gu h sil dn ev "
                      "lx0 lx1 lx2 lx3 lw0 lw1 lw2 lw3 so0 so1") for i in (3, 5)}
        GA = [sem(f"ga{t}") for t in range(NCH)]

        block = ctx.enter_context(nc.Block())

        loads = [
            (CST[:, :], consts_d),
            (raw[:, 0:2, :], a["L0_ffn_expert_W"][0:2].rearrange("e h d -> h e d")),
            (raw[:, 2, :], a["L0_ffn_out_W"]),
            (raw[:, 3, :], a["L0_attn_Wo"]),
            (raw[:, 4:7, :], wqkv_d),
            (raw[:, 7, :], a["L1_attn_Wout"]),
            (raw0[:, 0, :], a["L0_attn_Wq"]),
            (raw0[:, 1, :], a["L0_attn_Wk"]),
            (w0[:, 2, :], a["L0_attn_Wv"]),
            (cen[0:NG, :], a["L1_ffn_group_centroids"]),
            (cen[NG:NG + NE, :], a["L1_ffn_expert_centroids"]),
            (cen2[0:E0, :], a["L0_ffn_gate_W"]),
            (bcol[:, 0:1], a["L0_attn_bq"].rearrange("(p o) -> p o", o=1)),
            (bcol[:, 1:2], a["L0_attn_bk"].rearrange("(p o) -> p o", o=1)),
            (bcol[:, 2:3], a["L1_attn_bqkv"][0:P].rearrange("(p o) -> p o", o=1)),
            (bcol[:, 3:4], a["L1_attn_bqkv"][P:2 * P].rearrange("(p o) -> p o", o=1)),
            (bcol[:, 6:7], a["L0_attn_qk_scale"].rearrange("a b c d -> (a b c) d").to_broadcast([P, 1])),
            (brow[:, 0, :], a["L0_attn_bv"].rearrange("(o d) -> o d", o=1).to_broadcast([P, P])),
            (brow[:, 1, :], a["L0_attn_bo"].rearrange("(o d) -> o d", o=1).to_broadcast([P, P])),
            (brow[:, 2, :], a["L1_attn_bqkv"][2 * P:3 * P].rearrange("(o d) -> o d", o=1).to_broadcast([P, P])),
            (brow[:, 3, :], a["L1_attn_bout"].rearrange("(o d) -> o d", o=1).to_broadcast([P, P])),
            (bexp[:, :], a["L1_ffn_bias"].rearrange("(o d) -> o d", o=1).to_broadcast([P, NE])),
        ]
        ALL_IN = 16 * len(loads)

        KD = nc.dram_tensor("k_parts", (SHIFT_ROW, NH, NTOK), BF16, kind="Internal").ap()
        QD = nc.dram_tensor("q_parts", (SHIFT_ROW + 1, NH, NTOK), BF16, kind="Internal").ap()

        def attention_loads(eng, s):
            for parts, dram, runs in ((KP, KD, RUNS_K), (QP, QD, RUNS_Q)):
                row = 0
                for lo, hi in runs:
                    n = hi - lo
                    eng.dma_start(dram[row:row + HD * n].rearrange("(s d) h n -> (d h) s n", s=n),
                                  parts[:, lo:hi, :]).then_inc(s.st, 16)
                    row += HD * n
            eng.dma_start(QD[SHIFT_ROW], SHB[0:NH, :]).then_inc(s.st, 16)
            eng.wait_ge(s.st, 16 * 7)
            for q in range(QUADS):
                done = (s.l0, s.l1, s.l2, s.l3)[q]
                for j in range(4):
                    h, r0 = 4 * q + j, 64 * (j % 2)
                    eng.dma_start(Kt[r0:r0 + SHIFT_ROW, 2 * q + j // 2, :], KD[:, h, :]).then_inc(done, 16)
                    eng.dma_start(Qt[r0:r0 + SHIFT_ROW + 1, NCH * q:NCH * q + NCH, j, :],
                                  QD[:, h, :].rearrange("r (c n) -> r c n", c=NCH)).then_inc(done, 16)

        QUAD_LOADED = 16 * 4 * 2

        @block.sync
        def _(sp):
            def routed_dmas(i):
                s = MS[i]
                lx, lw = (s.lx0, s.lx1, s.lx2, s.lx3), (s.lw0, s.lw1, s.lw2, s.lw3)
                sp.wait_ge(NS.xn, NT * i + 1)
                sp.dma_start(ws[:, 0, :], a["L1_ffn_sg"]).then_inc(s.w, 16)
                sp.dma_start(ws[:, 1, :], a["L1_ffn_su"]).then_inc(s.w, 16)
                sp.dma_start(wsd, a["L1_ffn_sd"].rearrange("(k p) d -> p k d", p=P)).then_inc(s.w, 16)

                def load_weights(e, r):
                    one = bass.ds(e, 1)
                    sp.dma_start(WRING[:, r, 0:HID], a["L1_ffn_wg"][one].rearrange("e d h -> d (e h)")).then_inc(lw[r], 16)
                    sp.dma_start(WRING[:, r, HID:2 * HID], a["L1_ffn_wu"][one].rearrange("e d h -> d (e h)")).then_inc(lw[r], 16)
                    sp.dma_start(WRING[:, r, 2 * HID:3 * HID].rearrange("p (k d) -> p k d", k=2),
                                 a["L1_ffn_wd"][one].rearrange("e (k p) d -> p (e k) d", p=P)).then_inc(lw[r], 16)

                def load_rows(e, r):
                    sp.dma_start(XE[:, r, :, :], XD[bass.ds(e * BUF, BUF)].rearrange("(c p) d -> p c d", p=P)
                                 ).then_inc(lx[r], 16)

                for r in range(RING):
                    load_weights(r, r)
                sp.wait_ge(s.sc, 16 * NT * TOPK)
                for r in range(RING):
                    load_rows(r, r)
                with sp.Fori(0, NE // RING - 1) as u:
                    for r in range(RING):
                        e = u * RING + r
                        sp.wait_ge(s.dn, e + 1)
                        load_weights(e + RING, r)
                        load_rows(e + RING, r)

            for c in range(NCH):
                sp.dma_start(X[:, TPC * c:TPC * c + TPC, :], dram_x[:, TPC * c:TPC * c + TPC, :]).then_inc(s_x, 16)
            for dst, src in loads:
                sp.dma_start(dst, src).then_inc(s_in, 16)
            sp.wait_ge(SET.zero, 2)
            sp.wait_ge(SET.ones, 1)
            for r in (SHIFT_ROW, 64 + SHIFT_ROW):
                for pair in range(NH // 2):
                    sp.dma_start(Kt[r:r + 1, pair, :], SHB[0:1, :]).then_inc(SET.onesrow, 16)
            sp.dma_start(XD.rearrange("(p r) d -> p (r d)", p=P),
                         Qt[:, :, :, :].rearrange("p i h n -> p (i h n)").bitcast(F32)[:, 0:ROWS]).then_inc(SET.fill, 16)
            sp.wait_ge(SET.onesrow, 16 * NH)
            sp.wait_ge(SET.fill, 16)
            for i in range(stages):
                if i in AS:
                    sp.wait_ge(AS[i].parts, 3)
                    attention_loads(sp, AS[i])
                if i in MS:
                    routed_dmas(i)
            sp.wait_ge(s_x_ready, stages)
            for c in range(NCH):
                sp.dma_start(dram_out[:, TPC * c:TPC * c + TPC, :], X[:, TPC * c:TPC * c + TPC, :]).then_inc(s_out, 16)
            sp.wait_ge(s_out, 16 * NCH)

        @block.gpsimd
        def _(pool):
            nc.gpsimd.memset(SHB, 1.0).then_inc(SET.ones, 1)
            nc.gpsimd.memset(Kt[:, :, :], 0.0).then_inc(SET.zero, 1)
            nc.gpsimd.memset(Qt[:, :, :, :], 0.0).then_inc(SET.zero, 1)
            for i in range(stages):
                if i not in MS:
                    continue
                s = MS[i]
                pool.wait_ge(s.slot, 1)
                if i == 3:
                    pool.wait_ge(SET.fill, 16)
                for j in range(NT * TOPK):
                    nc.gpsimd.indirect_dma_start(XD, bass.IndirectOffsetOnAxis(srow[:, j:j + 1], 0), XN[:, j // TOPK, :],
                                                 None, bounds_check=ROWS - 1, oob_is_err=False).then_inc(s.sc, 16)
                pool.wait_ge(s.so0, 16 * NE // 2)
                pool.wait_ge(s.so1, 16 * NE // 2)
                pool.wait_ge(s.h, 2 * NE)
                pool.wait_ge(s.dn, NE)
                for j in range(NT * TOPK):
                    nc.gpsimd.indirect_dma_start(GB[:, j, :], None, OD, bass.IndirectOffsetOnAxis(grow[:, j:j + 1], 0)
                                                 ).then_inc(GA[j // (TOPK * TPC)], 16)

        @block.vector
        def _(dve):
            count = [0]

            def link(ins):
                count[0] += 1
                ins.then_inc(dch, 1)
                dve.wait_ge(dch, count[0])

            def setup():
                dve.wait_ge(s_in, ALL_IN)
                nc.vector.tensor_copy(U16[:, 0, :], CST[:, C_U:C_U + P])
                nc.vector.tensor_copy(U16[:, 1, :], CST[:, C_ONE:C_ONE + P])
                link(nc.vector.tensor_scalar(bcol[:, 7:8], bcol[:, 6:7], -1.0, None, ALU.mult))
                link(nc.vector.tensor_tensor(bcol[:, 7:8], bcol[:, 7:8], bcol[:, 6:7], ALU.min))
                link(nc.vector.tensor_tensor(cen2x, cen, cen, ALU.mult))
                nc.vector.tensor_reduce(cst1[:, 0:1], cen2x, AX.X, ALU.add).then_inc(SET.sq, 1)
                dve.wait_ge(SET.cen, 1)
                link(nc.vector.tensor_scalar(cst1[:, 2:3], cst1[:, 1:2], 1e-12, None, ALU.max))
                link(nc.vector.reciprocal(cst1[:, 3:4], cst1[:, 2:3]))
                nc.vector.tensor_scalar(cen, cen, cst1[:, 3:4], None, ALU.mult).then_inc(SET.cn, 1)

            def norm(i, XNi):
                s = NS
                if i == 0:
                    dve.wait_ge(s_x, 16 * NCH)
                for t in range(NT):
                    last = nc.vector.bn_stats(st[:, t, :], X[:, t, :])
                link(last)
                for t in range(NT):
                    last = nc.vector.bn_aggr(mv[:, t, :], st[:, t, :])
                link(last)
                nc.vector.tensor_scalar(sm[:, 0, :], mv[:, :, 1], LN_EPS, None, ALU.add).then_inc(s.var, 1)
                dve.wait_ge(s.std, i + 1)
                link(nc.vector.reciprocal(sm[:, 2, :], sm[:, 1, :]))
                for t in range(NT):
                    nc.vector.tensor_scalar(XNi[:, t, :], X[:, t, :], mv[:, t, 0:1], sm[:, 2, t:t + 1],
                                            ALU.subtract, ALU.mult).then_inc(s.xn, 1)

            def ffn0(i):
                s = FS[i]
                lg = PS[:, 4, 0:NT * E0].rearrange("p (t e) -> p t e", e=E0)
                ge = V[:, 0, :].rearrange("p (t e) -> p t e", e=E0)
                pp = V[:, 1, :].rearrange("p (t e) -> p t e", e=E0)
                ov = V[:, 2, :].rearrange("p (t e) -> p t e", e=E0)
                dve.wait_ge(s.g, 1)
                link(nc.vector.tensor_reduce(sm[:, 3, :], lg, AX.X, ALU.max))
                nc.vector.tensor_tensor(ge, lg, sm[:, 3, :].unsqueeze(2).to_broadcast([P, NT, E0]),
                                        ALU.subtract).then_inc(s.d, 1)
                dve.wait_ge(s.e, 1)
                link(nc.vector.tensor_reduce(sm[:, 4, :], pp, AX.X, ALU.add))
                link(nc.vector.reciprocal(sm[:, 5, :], sm[:, 4, :]))
                link(nc.vector.tensor_tensor(ge, pp, sm[:, 5, :].unsqueeze(2).to_broadcast([P, NT, E0]), ALU.mult))
                link(nc.vector.tensor_scalar(ov, ge, TOP_P, None, ALU.is_gt))
                link(nc.vector.tensor_reduce(sm[:, 6, :], ov, AX.X, ALU.add))
                nc.vector.tensor_scalar(sm[:, 7, :], sm[:, 6, :], -0.5, 0.5 * E0, ALU.mult, ALU.add)
                link(nc.vector.scalar_tensor_tensor(out=sm[:, 4, :], in0=sm[:, 6, :], scalar=0.5,
                                                    in1=ge[:, :, 1], op0=ALU.mult, op1=ALU.mult))
                link(nc.vector.tensor_tensor(sm[:, 3, :], sm[:, 7, :], ge[:, :, 0], ALU.mult))
                for pr in range(NT // 2):
                    dve.wait_ge(s.y, pr + 1)
                    b = 5 + pr % 3
                    for e in range(2):
                        for k in range(2):
                            t = 2 * pr + k
                            last = nc.vector.scalar_tensor_tensor(
                                out=X[:, t, :], in0=PS[:, b, 2 * P * k + P * e:2 * P * k + P * e + P],
                                scalar=sm[:, 3 + e, t:t + 1], in1=X[:, t, :], op0=ALU.mult, op1=ALU.add)
                        if e == 0:
                            link(last)
                    last.then_inc(s.used, 1)
                dve.wait_ge(s.used, NT // 2)
                nc.vector.tensor_copy(sm[:, 5, 0:1], sm[:, 3, 0:1]).then_inc(s_x_ready, 1)

            def attention(i):
                s = AS[i]
                rope = i == 4
                if rope:
                    dve.wait_ge(s_tab, 32)
                else:
                    dve.wait_ge(SET.onesrow, 16 * NH)
                for c in range(NCH):
                    cs = slice(c * CH, c * CH + CH)
                    dve.wait_ge(s.pj, c + 1)
                    b = 4 if c % 2 == 0 else 0
                    if rope:
                        for w, z, zb, n in ((wk_, t1_, 3, 2), (wq_, t2_, 2, 0)):
                            nc.vector.scalar_tensor_tensor(out=w[:, cs], in0=PS[:, b + n, :], scalar=bcol[:, zb:zb + 1],
                                                           in1=COS[:, cs], op0=ALU.add, op1=ALU.mult)
                            last = nc.vector.scalar_tensor_tensor(out=z[:, cs], in0=PS[:, b + n + 1, :],
                                                                  scalar=bcol[:, zb + 2:zb + 3], in1=SIN[:, cs],
                                                                  op0=ALU.add, op1=ALU.mult)
                        last.then_inc(s.used, 1)
                        dve.wait_ge(s.used, c + 1)
                        nc.vector.tensor_tensor(wk_[:, cs], wk_[:, cs], t1_[:, cs], ALU.add).then_inc(s.sq, 1)
                        nc.vector.tensor_tensor(wq_[:, cs], wq_[:, cs], t2_[:, cs], ALU.add).then_inc(s.sq, 1)
                    else:
                        nc.vector.tensor_scalar(wk_[:, cs], PS[:, b + 2, :], bcol[:, 1:2], None, ALU.add).then_inc(s.sq, 1)
                        nc.vector.tensor_scalar(wq_[:, cs], PS[:, b, :], bcol[:, 0:1], None, ALU.add).then_inc(s.sq, 1)
                        dve.wait_ge(s.sq, 2 * c + 2)
                        nc.vector.tensor_copy(km[:, 6:7], wq_[:, 0:1]).then_inc(s.used, 1)
                if rope:
                    dve.wait_ge(s.n2, 2 * NCH)
                    for c in range(NCH):
                        last = nc.vector.tensor_reduce(km[:, c:c + 1], PS[:, c, :], AX.X, ALU.max)
                    link(last)
                    link(nc.vector.tensor_reduce(km[:, 4:5], km[:, 0:NCH], AX.X, ALU.max))
                    for c in range(NCH):
                        cs = slice(c * CH, c * CH + CH)
                        nc.vector.tensor_scalar(t1_[:, cs], PS[:, NCH + c, :], km[:, 4:5], None, ALU.mult).then_inc(s.r, 1)
                    for c in range(NCH):
                        cs = slice(c * CH, c * CH + CH)
                        dve.wait_ge(s.rt, c + 1)
                        last = nc.vector.tensor_scalar(SHB[:, cs], t1_[:, cs], -1.0, None, ALU.mult)
                    last.then_inc(s.parts, 1)
                    dve.wait_ge(s.parts, 1)
                    rn = 0
                else:
                    for c in range(NCH):
                        cs = slice(c * CH, c * CH + CH)
                        for n, (w, z) in enumerate(((wk_, t1_), (wq_, t2_))):
                            dve.wait_ge(s.rt, 2 * c + n + 1)
                            link(nc.vector.tensor_scalar(z[:, cs], z[:, cs], NORM_EPS, None, ALU.add))
                            link(nc.vector.reciprocal(z[:, cs], z[:, cs]))
                            if n == 0:
                                nc.vector.tensor_tensor(w[:, cs], w[:, cs], z[:, cs], ALU.mult).then_inc(s.r, 1)
                            else:
                                nc.vector.scalar_tensor_tensor(out=w[:, cs], in0=w[:, cs], scalar=bcol[:, 6:7],
                                                               in1=z[:, cs], op0=ALU.mult, op1=ALU.mult).then_inc(s.r, 1)
                    dve.wait_ge(s.r, 2 * NCH)
                    nc.vector.tensor_scalar(SHB[:, :], wq_[:, :], 0.0, bcol[:, 7:8], ALU.mult, ALU.add).then_inc(s.parts, 1)
                for n, (w, z, hi) in enumerate(((wk_, t1_, KP[:, 0, :]), (wq_, t2_, QP[:, 2, :]))):
                    for c in range(NCH):
                        cs = slice(c * CH, c * CH + CH)
                        dve.wait_ge(s.hi, NCH * n + c + 1)
                        nc.vector.tensor_tensor(z[:, cs], w[:, cs], hi[:, cs], ALU.subtract).then_inc(s.mid, 1)
                for n, (z, parts, low) in enumerate(((t1_, KP, 2), (t2_, QP, 0))):
                    for c in range(NCH):
                        cs = slice(c * CH, c * CH + CH)
                        dve.wait_ge(s.o, NCH * n + c + 1)
                        last = nc.vector.tensor_tensor(parts[:, low, cs], z[:, cs], parts[:, 1, cs], ALU.subtract)
                    last.then_inc(s.parts, 1)
                for c in range(NCH):
                    dve.wait_ge(s.v, c + 1)
                    last = nc.vector.tensor_tensor(
                        V[:, TPC * c:TPC * c + TPC, :], PS[:, c, :].rearrange("p (t d) -> p t d", t=TPC),
                        brow[:, 2 * (i == 4), :].unsqueeze(1).to_broadcast([P, TPC, P]), ALU.add)
                link(last)
                nc.vector.tensor_tensor(X[:, :, :], X[:, :, :],
                                        brow[:, 1 + 2 * (i == 4), :].unsqueeze(1).to_broadcast([P, NT, P]), ALU.add)
                nc.vector.memset(PS[:, 4:8, :].rearrange("p a b -> p (a b)"), 0.0)
                dve.wait_ge(s.v, NCH)
                nc.vector.memset(VQ[:, :, :, :, HD:VW].rearrange("p b t h w -> p (b t h) w"), 1.0)
                V4 = V[:, :, :].rearrange("p t (q h w) -> p t q h w", q=QUADS, h=4)
                for b in range(2):
                    nc.vector.tensor_copy(VQ[:, b, :, :, 0:HD], V4[:, :, 0, :, :]).then_inc(s.vq, 1)
                dve.wait_ge(s.st, 16 * 7)
                oc = sem(f"oc{i}")
                ocn = 0
                Vf = V[:, :, :]

                def step(it, b, more):
                    dve.wait_ge(s.pv, it + 1)
                    at = AT[:, bass.ds(it, 1), :].rearrange("p o n -> p (o n)")
                    got = PS[:, 4 + 2 * b:6 + 2 * b, 0:CH // 2]
                    nc.vector.tensor_copy(at.rearrange("p (a n) -> p a n", a=2), got).then_inc(oc, 1)
                    for half in range(2):
                        last = nc.vector.stream_shuffle(RS[:, half * CH // 2:(half + 1) * CH // 2], got[:, half, :], [HD] * 32)
                    last.then_inc(oc, 1)
                    if more:
                        nc.vector.tensor_copy(VQ[:, b, :, :, 0:HD], Vf[:, :, bass.ds(vcol(it), 4 * HD)].rearrange(
                            "p t (h w) -> p t h w", h=4)).then_inc(s.vq, 1)
                    dve.wait_ge(oc, it * 4 + 2)
                    nc.vector.reciprocal(RS, RS).then_inc(oc, 1)
                    dve.wait_ge(oc, it * 4 + 3)
                    nc.vector.tensor_tensor(at, at, RS, ALU.mult).then_inc(oc, 1)
                    dve.wait_ge(oc, it * 4 + 4)

                def vcol(it):
                    return ((it + 2) // NCH) * (4 * HD)

                with dve.Fori(0, ITERS // 2 - 1) as u:
                    for b in range(2):
                        step(2 * u + b, b, True)
                for b in range(2):
                    step(ITERS - 2 + b, b, False)
                nc.vector.tensor_copy(km[:, 7:8], AT[:, ITERS - 1, 0:1]).then_inc(s.at, 1)
                for c in range(NCH):
                    dve.wait_ge(s.vr, c + 1)
                    last = nc.vector.tensor_tensor(X[:, TPC * c:TPC * c + TPC, :], X[:, TPC * c:TPC * c + TPC, :],
                                                   PS[:, c, :].rearrange("p (t d) -> p t d", t=TPC), ALU.add)
                link(last)
                nc.vector.tensor_copy(km[:, 6:7], X[:, 0, 0:1]).then_inc(s_x_ready, 1)

            def routed(i):
                s = MS[i]
                dve.wait_ge(NS.xn, NT * i + NT)
                link(nc.vector.tensor_tensor(OH.rearrange("p (t d) -> p t d", t=NT), XN, XN, ALU.mult))
                nc.vector.tensor_reduce(sm[:, 3, :], OH.rearrange("p (t d) -> p t d", t=NT), AX.X, ALU.add).then_inc(s.sq, 1)
                dve.wait_ge(s.sr, 1)
                link(nc.vector.tensor_scalar(sm[:, 5, :], sm[:, 4, :], 1e-12, None, ALU.max))
                link(nc.vector.reciprocal(sm[:, 6, :], sm[:, 5, :]))
                dve.wait_ge(s.lg, 1)
                W = NG + NE
                for k in range(2):
                    ts_ = slice(8 * k, 8 * k + 8)
                    last = nc.vector.tensor_tensor(S40[:, ts_, :], PS[:, 4 + k, 0:8 * W].rearrange("p (t e) -> p t e", t=8),
                                                   sm[:, 6, ts_].unsqueeze(2).to_broadcast([P, 8, W]), ALU.mult)
                link(last)

                def top(values):
                    for t in range(NT):
                        last = nc.vector.max(top8[:, t, :], values(t))
                    link(last)
                    for t in range(NT):
                        last = nc.vector.max_index(idx8[:, t, :], top8[:, t, :], values(t))
                    link(last)
                    link(nc.vector.tensor_copy(idxf, idx8))

                def one_hot(dst, width, col):
                    link(nc.vector.tensor_tensor(
                        dst, CST[:, col:col + width].unsqueeze(1).unsqueeze(1).to_broadcast([P, NT, TOPK, width]),
                        idxf[:, :, 0:TOPK].unsqueeze(3).to_broadcast([P, NT, TOPK, width]), ALU.is_equal))

                top(lambda t: S40[:, t, 0:NG])
                ohg = OH[:, 0:NT * TOPG * NG].rearrange("p (t k g) -> p t k g", t=NT, k=TOPG)
                one_hot(ohg, NG, C_I8)
                link(nc.vector.tensor_reduce(gmk, ohg.rearrange("p t k g -> p t g k"), AX.X, ALU.add))
                es = MSK.rearrange("p (t e) -> p t e", t=NT)
                link(nc.vector.tensor_tensor(es, S40[:, :, NG:W], bexp[:, :].unsqueeze(1).to_broadcast([P, NT, NE]), ALU.add))
                esg = MSK.rearrange("p (t g e) -> p t g e", t=NT, g=NG)
                gb = [P, NT, NG, NE // NG]
                nc.vector.tensor_scalar(ESC, gmk, -1.0, 1e9, ALU.add, ALU.mult)
                link(nc.vector.tensor_tensor(esg, esg, gmk.unsqueeze(3).to_broadcast(gb), ALU.mult))
                link(nc.vector.tensor_tensor(esg, esg, ESC.unsqueeze(3).to_broadcast(gb), ALU.add))
                top(lambda t: es[:, t, :])
                oh = OH.rearrange("p (t k e) -> p t k e", t=NT, k=TOPK)
                one_hot(oh, NE, C_I32)
                m3 = M16[:, :].rearrange("p (e t) -> p e t", e=NE)
                with nc.allow_low_precision("zeros and ones"):
                    nc.vector.tensor_reduce(m3, oh.rearrange("p t k e -> p e t k"), AX.X, ALU.add).then_inc(s.mk, 1)
                g3 = gate.rearrange("p (t k) -> p t k", t=NT)
                nc.vector.tensor_tensor(g3, top8[:, :, 0:TOPK], top8[:, :, 0:1].to_broadcast([P, NT, TOPK]),
                                        ALU.subtract).then_inc(s.d, 1)
                nc.vector.tensor_copy(OH2[:, 0:NE * NT].rearrange("p (e t) -> p e t", e=NE),
                                      CST[:, C_RES:C_RES + NT].unsqueeze(1).to_broadcast([P, NE, NT])).then_inc(s.rn, 1)
                dve.wait_ge(s.rn, 1)
                dve.wait_ge(s.pfx, 1)
                link(nc.vector.tensor_tensor_scan(POS, OH2[:, 0:NE * NT], PS[:, 7, :], 0.0, ALU.mult, ALU.add))
                link(nc.vector.tensor_tensor(POS, POS, PS[:, 7, :], ALU.subtract))
                link(nc.vector.tensor_tensor(POS, POS, PS[:, 6, :], ALU.add))
                link(nc.vector.tensor_scalar(MSK, POS, float(CAP), FAR, ALU.is_ge, ALU.mult))
                p3 = POS.rearrange("p (e t) -> p e t", e=NE)
                link(nc.vector.tensor_tensor(p3, p3, CST[:, C_BASE:C_BASE + NE].unsqueeze(2).to_broadcast([P, NE, NT]), ALU.add))
                link(nc.vector.tensor_tensor(POS, POS, MSK, ALU.add))
                oh2 = OH2.rearrange("p (t k e) -> p t k e", t=NT, k=TOPK)
                link(nc.vector.tensor_tensor(oh2, oh, p3.rearrange("p e t -> p t e").unsqueeze(2).to_broadcast([P, NT, TOPK, NE]),
                                             ALU.mult))
                link(nc.vector.tensor_reduce(slotf.rearrange("p (t k) -> p t k", t=NT), oh2, AX.X, ALU.add))
                nc.vector.tensor_copy(srow, slotf).then_inc(s.slot, 1)
                nc.vector.tensor_scalar(grow, slotf, float(ROWS - 1), None, ALU.min)
                dve.wait_ge(s.e, 1)
                e3 = rtt[:, 3, 0:NT * TOPK]
                link(nc.vector.tensor_reduce(sm[:, 3, :], e3.rearrange("p (t k) -> p t k", t=NT), AX.X, ALU.add))
                link(nc.vector.reciprocal(sm[:, 4, :], sm[:, 3, :]))
                link(nc.vector.scalar_tensor_tensor(out=g3, in0=e3.rearrange("p (t k) -> p t k", t=NT), scalar=0.5,
                                                    in1=sm[:, 4, :].unsqueeze(2).to_broadcast([P, NT, TOPK]),
                                                    op0=ALU.mult, op1=ALU.mult))
                link(nc.vector.scalar_tensor_tensor(out=gate, in0=slotf, scalar=float(ROWS), in1=gate,
                                                    op0=ALU.is_lt, op1=ALU.mult))
                link(nc.vector.memset(OB.rearrange("p b c d -> p (b c d)"), 0.0))
                for st_ in range(2 * NCH):
                    c, m = st_ // 2, st_ % 2
                    dve.wait_ge(s.sh, st_ + 1)
                    hs = SH[:, m, c * CH:c * CH + CH]
                    nc.vector.tensor_tensor(hs, hs, PS[:, 2 * m + 1, :], ALU.mult).then_inc(s.si, 1)
                for c in range(NCH):
                    dve.wait_ge(s.sd, c + 1)
                    nc.vector.scalar_tensor_tensor(out=X[:, TPC * c:TPC * c + TPC, :].rearrange("p t d -> p (t d)"),
                                                   in0=PS[:, 6 + c % 2, :], scalar=0.5,
                                                   in1=X[:, TPC * c:TPC * c + TPC, :].rearrange("p t d -> p (t d)"),
                                                   op0=ALU.mult, op1=ALU.add).then_inc(s.sdu, 1)

                def take_rows(e, b):
                    dve.wait_ge(s.xt, e + 1)
                    nc.vector.tensor_copy(XET[:, b, :], PS[:, b, 0:CAP]).then_inc(s.rn, 1)

                def hidden(e, b, first=False):
                    for m in range(2):
                        dve.wait_ge(s.sil, e * 2 + (m + 1))
                        if not first and m == 0:
                            dve.wait_ge(s.dn, e - 1)
                        nc.vector.tensor_tensor(HT[:, b, m, :], SIL[:, m, :], PS[:, 3 + 2 * m, 0:CAP],
                                                ALU.mult).then_inc(s.h, 1)

                for e in range(4):
                    take_rows(e, e % 2)
                    if e:
                        hidden(e - 1, (e - 1) % 2, first=e <= 2)
                with dve.Fori(1, NE // RING) as u:
                    for r in range(RING):
                        take_rows(u * RING + r, r % 2)
                        hidden(u * RING + (r - 1), (r - 1) % 2)
                hidden(NE - 1, (NE - 1) % 2)
                for t0 in range(0, NT, 4):
                    dve.wait_ge(GA[t0 // 4], 16 * TOPK * TPC * (1 if i == 3 else 2))
                    for k in range(TOPK):
                        for t in range(t0, t0 + 4):
                            j = TOPK * t + k
                            last = nc.vector.scalar_tensor_tensor(out=X[:, t, :], in0=GB[:, j, :], scalar=gate[:, j:j + 1],
                                                                  in1=X[:, t, :], op0=ALU.mult, op1=ALU.add)
                        link(last)
                nc.vector.tensor_copy(km[:, 7:8], X[:, 0, 0:1]).then_inc(s_x_ready, 1)

            cen2x = XNT[0:NG + NE, 0:P]
            setup()
            for i in range(stages):
                norm(i, XNA if i in (1, 4) else XN)
                if i in FS:
                    ffn0(i)
                elif i in AS:
                    attention(i)
                else:
                    routed(i)

        @block.scalar
        def _(act):
            def setup():
                act.wait_ge(SET.mm1, 1)
                nc.scalar.copy(wt[:, 0, :], PS[:, 0, 0:P])
                nc.scalar.copy(wcat[:, 2 * P:2 * P + E0], PS[:, 0, P:P + E0])
                nc.scalar.copy(wt[:, 1, :], PS[:, 0, 2 * P:3 * P])
                nc.scalar.mul(w1[:, 0:2, :].rearrange("p a b -> p (a b)"), PS[:, 1, 0:2 * P], float(HD) ** -0.5)
                nc.scalar.copy(w1[:, 2:4, :].rearrange("p a b -> p (a b)"), PS[:, 1, 2 * P:4 * P])
                nc.scalar.copy(w1[:, 4, :], PS[:, 2, 0:P]).then_inc(SET.cp1, 1)
                act.wait_ge(SET.mm2, 1)
                nc.scalar.copy(wcat[:, 0:2 * P], PS[:, 4, 0:2 * P])
                nc.scalar.copy(wo[:, 0, :, :].rearrange("p a b -> p (a b)"), PS[:, 5, :])
                nc.scalar.copy(wo[:, 1, :, :].rearrange("p a b -> p (a b)"), PS[:, 6, :])
                nc.scalar.copy(bcol[:, 0:4], PS[:, 7, 0:4])
                nc.scalar.mul(bcol[:, 4:5], PS[:, 7, 4:5], float(HD) ** -0.5)
                nc.scalar.copy(bcol[:, 5:6], PS[:, 7, 5:6]).then_inc(ach, 1)
                act.wait_ge(ach, 1)
                nc.scalar.mul(bcol[:, 2:3], bcol[:, 2:3], float(HD) ** -0.5).then_inc(SET.cp2, 1)
                for n in range(2):
                    nc.scalar.copy(w0[:, n, :].rearrange("p (d h) -> p h d", d=HD),
                                   raw0[:, n, :].rearrange("p (h d) -> p h d", d=HD))
                act.wait_ge(SET.sq, 1)
                nc.scalar.activation(cst1[:, 1:2], cst1[:, 0:1], ACT.Sqrt).then_inc(SET.cen, 1)
                act.wait_ge(SET.ctr, 1)
                nc.scalar.copy(r40[:, :], PS[:, 3, 0:NG + NE]).then_inc(ach, 1)
                act.wait_ge(ach, 2)

            def norm(i):
                s = NS
                act.wait_ge(s.var, i + 1)
                nc.scalar.activation(sm[:, 1, :], sm[:, 0, :], ACT.Sqrt).then_inc(s.std, 1)
                for c in range(NCH):
                    act.wait_ge(s.tr, NCH * i + c + 1)
                    nc.scalar.copy(XNT[:, c * CH:c * CH + CH], PS[:, c, :]).then_inc(s.xt, 1)

            def ffn0(i):
                s = FS[i]
                act.wait_ge(s.d, 1)
                nc.scalar.activation(V[:, 1, :], V[:, 0, :], ACT.Exp).then_inc(s.e, 1)

            def attention(i):
                s = AS[i]
                rope = i == 4
                if rope:
                    act.dma_start(COS, cos_d).then_inc(s_tab, 16)
                    act.dma_start(SIN, sin_d).then_inc(s_tab, 16)
                for c in range(NCH):
                    cs = slice(c * CH, c * CH + CH)
                    for n, (w, z) in enumerate(((wk_, t1_), (wq_, t2_))):
                        act.wait_ge(s.sq, 2 * c + n + 1)
                        nc.scalar.activation(z[:, cs], w[:, cs], ACT.Square).then_inc(s.pj2, 1)
                for c in range(NCH):
                    cs = slice(c * CH, c * CH + CH)
                    if rope:
                        act.wait_ge(s.r, c + 1)
                        nc.scalar.activation(t1_[:, cs], t1_[:, cs], ACT.Sqrt).then_inc(s.rt, 1)
                    else:
                        for n, z in enumerate((t1_, t2_)):
                            act.wait_ge(s.n2, 2 * c + n + 1)
                            nc.scalar.activation(z[:, cs], PS[:, NCH * n + c, :], ACT.Sqrt).then_inc(s.rt, 1)
                for n, (w, parts, high) in enumerate(((wk_, KP, 0), (wq_, QP, 2))):
                    for c in range(NCH):
                        cs = slice(c * CH, c * CH + CH)
                        if not rope:
                            act.wait_ge(s.r, 2 * c + n + 1)
                        nc.scalar.copy(parts[:, high, cs], w[:, cs]).then_inc(s.hi, 1)
                for n, (z, parts) in enumerate(((t1_, KP), (t2_, QP))):
                    for c in range(NCH):
                        cs = slice(c * CH, c * CH + CH)
                        act.wait_ge(s.mid, NCH * n + c + 1)
                        nc.scalar.copy(parts[:, 1, cs], z[:, cs]).then_inc(s.o, 1)
                nc.scalar.activation(km[:, 5:6], bcol[:, 7:8], ACT.Exp)
                act.wait_ge(s.parts, 3)
                with act.Fori(0, ITERS // 2) as u:
                    for g in range(2 * CHUNKS):
                        act.wait_ge(s.s, u * (2 * CHUNKS) + (g + 1))
                        nc.scalar.activation(PR[:, g % PRING, :], PS[:, 2 * (g % 2):2 * (g % 2) + 2, :].rearrange("p a b -> p (a b)"),
                                             ACT.Exp).then_inc(s.exp, 1)

            def routed(i):
                s = MS[i]
                act.wait_ge(s.sq, 1)
                nc.scalar.activation(sm[:, 4, :], sm[:, 3, :], ACT.Sqrt).then_inc(s.sr, 1)
                act.wait_ge(s.d, 1)
                nc.scalar.activation(rtt[:, 3, 0:NT * TOPK], gate, ACT.Exp).then_inc(s.e, 1)
                for st_ in range(2 * NCH):
                    c, m = st_ // 2, st_ % 2
                    act.wait_ge(s.gu, st_ + 1)
                    nc.scalar.activation(SH[:, m, c * CH:c * CH + CH], PS[:, 2 * m, :], ACT.Silu).then_inc(s.sh, 1)

                def gates(e):
                    for m in range(2):
                        act.wait_ge(s.gu, e * 2 + (2 * NCH + m + 1))
                        nc.scalar.activation(SIL[:, m, :], PS[:, 2 + 2 * m, 0:CAP], ACT.Silu).then_inc(s.sil, 1)

                def take_out(e, b, again):
                    act.wait_ge(s.dn, e + 1)
                    if again is not None:
                        act.wait_ge((s.so0, s.so1)[b], again * 16)
                    nc.scalar.copy(OB[:, b, 0:RT - 1, :].rearrange("p c d -> p (c d)"), PS[:, 6 + b, 0:(RT - 1) * P])
                    nc.scalar.copy(OB[0:TAIL, b, RT - 1, :], PS[0:TAIL, 6 + b, (RT - 1) * P:RT * P]).then_inc(s.ev, 1)
                    act.wait_ge(s.ev, e + 1)
                    act.dma_start(OD[bass.ds(e * BUF, BUF)].rearrange("(c p) d -> p c d", p=P),
                                  OB[:, b, :, :]).then_inc((s.so0, s.so1)[b], 16)

                gates(0)
                gates(1)
                take_out(0, 0, None)
                gates(2)
                take_out(1, 1, None)
                with act.Fori(1, NE // RING) as u:
                    for r in range(RING):
                        gates(u * RING + (r - 1))
                        take_out(u * RING + (r - 2), r % 2, u * 2 + (r // 2 - 1))
                gates(NE - 1)
                for e in (NE - 2, NE - 1):
                    take_out(e, e % 2, e // 2)

            setup()
            for i in range(stages):
                norm(i)
                if i in FS:
                    ffn0(i)
                elif i in AS:
                    attention(i)
                else:
                    routed(i)

        @block.tensor
        def _(pe):
            def setup():
                pe.wait_ge(s_in, ALL_IN)
                nc.tensor.transpose(PS[:, 0, 0:P], raw[:, 2, :], ident)
                nc.tensor.transpose(PS[:, 0, P:P + E0], cen2[0:E0, :], ident[0:E0, 0:E0])
                nc.tensor.transpose(PS[:, 0, 2 * P:3 * P], raw[:, 7, :], ident)
                nc.tensor.matmul(PS[:, 1, 0:2 * P], raw[:, 4, :], CST[:, C_PERM:C_PERM + 2 * P], start=True, stop=True)
                nc.tensor.matmul(PS[:, 1, 2 * P:4 * P], raw[:, 5, :], CST[:, C_PERM:C_PERM + 2 * P], start=True, stop=True)
                nc.tensor.matmul(PS[:, 2, 0:P], raw[:, 6, :], ident, start=True, stop=True).then_inc(SET.mm1, 1)
                pe.wait_ge(SET.cp1, 1)
                for e in range(2):
                    nc.tensor.matmul(PS[:, 4, P * e:P * e + P], raw[:, e, :], wt[:, 0, :], start=True, stop=True)
                for q in range(QUADS):
                    pad = CST[:, C_PAD + q * P:C_PAD + q * P + P]
                    nc.tensor.matmul(PS[:, 5, P * q:P * q + P], pad, raw[:, 3, :], start=True, stop=True)
                    nc.tensor.matmul(PS[:, 6, P * q:P * q + P], pad, wt[:, 1, :], start=True, stop=True)
                nc.tensor.matmul(PS[:, 7, 0:4], CST[:, C_PERM:C_PERM + P], bcol[:, 0:4], start=True, stop=True)
                last = nc.tensor.matmul(PS[:, 7, 4:6], rotT, bcol[:, 2:4], start=True, stop=True)
                last.then_inc(SET.mm2, 1)
                pe.wait_ge(SET.cn, 1)
                nc.tensor.transpose(PS[:, 3, 0:NG + NE], cen, ident[0:NG + NE, 0:NG + NE]).then_inc(SET.ctr, 1)
                pe.wait_ge(SET.cp2, 1)
                pe.wait_ge(ach, 2)

            def norm(i, XNi):
                s = NS
                for t in range(NT):
                    pe.wait_ge(s.xn, NT * i + t + 1)
                    last = nc.tensor.transpose(PS[:, t // TPC, P * (t % TPC):P * (t % TPC) + P], XNi[:, t, :], ident)
                    if t % TPC == TPC - 1:
                        last.then_inc(s.tr, 1)

            def ffn0(i):
                s, n = FS[i], NS
                for t in range(NT):
                    if t % TPC == 0:
                        pe.wait_ge(n.xt, NCH * i + t // TPC + 1)
                    last = nc.tensor.matmul(PS[:, 4, E0 * t:E0 * t + E0], XNT[:, P * t:P * t + P], wcat[:, 2 * P:],
                                            start=True, stop=True)
                last.then_inc(s.g, 1)
                for t in range(NT):
                    pr = t // 2
                    if t % 2 == 0 and pr >= 3:
                        pe.wait_ge(s.used, pr - 2)
                    last = nc.tensor.matmul(PS[:, 5 + pr % 3, 2 * P * (t % 2):2 * P * (t % 2) + 2 * P],
                                            XNT[:, P * t:P * t + P], wcat[:, 0:2 * P], start=True, stop=True)
                    if t % 2:
                        last.then_inc(s.y, 1)

            def attention(i):
                s, n = AS[i], NS
                rope = i == 4
                w = w1 if rope else w0
                pe.wait_ge(n.xt, NCH * i + NCH)
                for c in range(NCH):
                    cs = slice(c * CH, c * CH + CH)
                    b = 4 if c % 2 == 0 else 0
                    if c >= 2:
                        pe.wait_ge(s.used, c - 1)
                    for k in range(4):
                        if rope:
                            last = nc.tensor.matmul(PS[:, b + k, :], w1[:, k, :], XNT[:, cs], start=True, stop=True)
                        elif k % 2 == 0:
                            last = nc.tensor.matmul(PS[:, b + k, :], w0[:, k // 2, :], XNT[:, cs], start=True, stop=True)
                    last.then_inc(s.pj, 1)
                pe.wait_ge(s.used, NCH)
                for c in range(NCH):
                    cs = slice(c * CH, c * CH + CH)
                    for k, z in enumerate((t1_, t2_)):
                        pe.wait_ge(s.pj2, 2 * c + k + 1)
                        nc.tensor.matmul(PS[:, NCH * k + c, :], G, z[:, cs], start=True, stop=True).then_inc(s.n2, 1)
                if rope:
                    pe.wait_ge(s.r, NCH)
                else:
                    pe.wait_ge(s.rt, 2 * NCH)
                for t in range(NT):
                    last = nc.tensor.matmul(PS[:, t // TPC, P * (t % TPC):P * (t % TPC) + P], XNT[:, P * t:P * t + P],
                                            w[:, 4 if rope else 2, :], start=True, stop=True)
                    if t % TPC == TPC - 1:
                        last.then_inc(s.v, 1)

                def scores(it, g):
                    kt, half = g // 2, g % 2
                    pair = (it // NCH) * 2 + half
                    for k in range(2):
                        j = 2 * half + k
                        last = nc.tensor.matmul(
                            PS[:, 2 * half + k, :],
                            Kt[:, bass.ds(pair, 1), P * kt:P * kt + P].rearrange("p o n -> p (o n)"),
                            Qt[:, bass.ds(it, 1), j, :].rearrange("p o n -> p (o n)"), start=True, stop=True)
                    last.then_inc(s.s, 1)

                def weigh(b, kt, half):
                    for j in range(4):
                        p0 = CH * (j % 2) + half * (CH // 2)
                        last = nc.tensor.matmul(PS[32 * j:32 * j + VW, 4 + 2 * b + half, 0:CH // 2], VQ[:, b, kt, j, :],
                                                PR[:, (b * CHUNKS + 2 * kt + j // 2) % PRING, p0:p0 + CH // 2],
                                                start=(kt == 0), stop=(kt == NT - 1), tile_position=(0, 32 * j))
                    if kt == NT - 1 and half:
                        last.then_inc(s.pv, 1)

                def iteration(it, b, first=False, final=False):
                    for kt in range(NT):
                        for half in range(2):
                            g = 2 * kt + half
                            pe.wait_ge(s.exp, it * CHUNKS + (g + 1))
                            if kt < NT - 1:
                                scores(it, g + 2)
                            elif not final:
                                scores(it + 1, half)
                            if kt == 1 and half == 0:
                                pe.wait_ge(s.vq, it + 1)
                            if kt:
                                weigh(b, kt - 1, half)
                            elif not first:
                                weigh(1 - b, NT - 1, half)
                    if final:
                        for half in range(2):
                            weigh(b, NT - 1, half)

                pe.wait_ge(s.l0, QUAD_LOADED)
                pe.wait_ge(s.vq, 2)
                scores(0, 0)
                scores(0, 1)
                iteration(0, 0, first=True)
                iteration(1, 1)
                for l in (s.l1, s.l2, s.l3):
                    pe.wait_ge(l, QUAD_LOADED)
                with pe.Fori(1, ITERS // 2 - 1) as u:
                    for b in range(2):
                        iteration(2 * u + b, b)
                iteration(ITERS - 2, 0)
                iteration(ITERS - 1, 1, final=True)
                pe.wait_ge(s.at, 1)
                for t in range(NT):
                    for q in range(QUADS):
                        last = nc.tensor.matmul(PS[:, t // TPC, P * (t % TPC):P * (t % TPC) + P],
                                                AT[:, NCH * q + t // TPC, P * (t % TPC):P * (t % TPC) + P],
                                                wo[:, 1 if rope else 0, q, :], start=(q == 0), stop=(q == QUADS - 1))
                    if t % TPC == TPC - 1:
                        last.then_inc(s.vr, 1)

            def routed(i):
                s, n = MS[i], NS
                lx, lw = (s.lx0, s.lx1, s.lx2, s.lx3), (s.lw0, s.lw1, s.lw2, s.lw3)
                W = NG + NE
                for t in range(NT):
                    if t % TPC == 0:
                        pe.wait_ge(n.xt, NCH * i + t // TPC + 1)
                    last = nc.tensor.matmul(PS[:, 4 + t // 8, W * (t % 8):W * (t % 8) + W], XNT[:, P * t:P * t + P], r40[:, :],
                                            start=True, stop=True)
                last.then_inc(s.lg, 1)
                pe.wait_ge(s.mk, 1)
                nc.tensor.matmul(PS[:, 6, :], U16[:, 0, :], M16[:, :], start=True, stop=True)
                nc.tensor.matmul(PS[:, 7, :], U16[:, 1, :], M16[:, :], start=True, stop=True).then_inc(s.pfx, 1)
                pe.wait_ge(s.w, 48)
                for st_ in range(2 * NCH):
                    c, m = st_ // 2, st_ % 2
                    if c:
                        pe.wait_ge(s.si, st_ - 1)
                    for k in range(2):
                        last = nc.tensor.matmul(PS[:, 2 * m + k, :], ws[:, k, P * m:P * m + P], XNT[:, c * CH:c * CH + CH],
                                                start=True, stop=True)
                    last.then_inc(s.gu, 1)
                pe.wait_ge(s.slot, 1)
                for t in range(NT):
                    c = t // TPC
                    if t % TPC == 0:
                        pe.wait_ge(s.si, 2 * c + 2)
                        if c >= 2:
                            pe.wait_ge(s.sdu, c - 1)
                    for m in range(2):
                        last = nc.tensor.matmul(PS[:, 6 + c % 2, P * (t % TPC):P * (t % TPC) + P], SH[:, m, P * t:P * t + P],
                                                wsd[:, m, :], start=(m == 0), stop=(m == 1))
                    if t % TPC == TPC - 1:
                        last.then_inc(s.sd, 1)
                pe.wait_ge(s.si, 2 * NCH)
                pe.wait_ge(s.sdu, NCH)

                def turn(u, r, first):
                    b = r % 2
                    pe.wait_ge(lx[r], u * 16 + 16)
                    if not first:
                        pe.wait_ge(s.rn, u * RING + r)
                    for c in range(RT):
                        n_ = P if c < RT - 1 else TAIL
                        last = nc.tensor.transpose(PS[:, b, P * c:P * c + n_], XE[0:n_, r, c, :], ident[0:n_, 0:n_])
                    last.then_inc(s.xt, 1)

                def up(e, u, r, first=False):
                    b = r % 2
                    pe.wait_ge(s.rn, e + 2)
                    pe.wait_ge(lw[r], u * 48 + 48)
                    for m in range(2):
                        if not first:
                            pe.wait_ge(s.h, e * 2 + (m - 1))
                        for k in range(2):
                            last = nc.tensor.matmul(PS[:, 2 + 2 * m + k, 0:CAP], WRING[:, r, HID * k + P * m:HID * k + P * m + P],
                                                    XET[:, b, :], start=True, stop=True)
                        last.then_inc(s.gu, 1)

                def down(e, r, first=False):
                    b = r % 2
                    pe.wait_ge(s.h, e * 2 + 2)
                    if not first:
                        pe.wait_ge(s.ev, e - 1)
                    for c in range(RT):
                        n_ = P if c < RT - 1 else TAIL
                        for m in range(2):
                            last = nc.tensor.matmul(PS[0:n_, 6 + b, P * c:P * c + P], HT[:, b, m, P * c:P * c + n_],
                                                    WRING[:, r, 2 * HID + P * m:2 * HID + P * m + P],
                                                    start=(m == 0), stop=(m == 1))
                    last.then_inc(s.dn, 1)

                for r in range(RING):
                    turn(0, r, r < 2)
                    if r >= 1:
                        up(r - 1, 0, r - 1, first=(r == 1))
                    if r >= 2:
                        down(r - 2, r - 2, first=True)
                with pe.Fori(1, NE // RING) as u:
                    for r in range(RING):
                        turn(u, r, False)
                        up(u * RING + (r - 1), u if r else u - 1, (r - 1) % RING)
                        down(u * RING + (r - 2), (r - 2) % RING)
                up(NE - 1, NE // RING - 1, RING - 1)
                down(NE - 2, RING - 2)
                down(NE - 1, RING - 1)

            setup()
            for i in range(stages):
                norm(i, XNA if i in (1, 4) else XN)
                if i in FS:
                    ffn0(i)
                elif i in AS:
                    attention(i)
                else:
                    routed(i)


_INS = ['L0_attn_x', 'L0_attn_Wq', 'L0_attn_bq', 'L0_attn_Wk', 'L0_attn_bk', 'L0_attn_Wv', 'L0_attn_bv', 'L0_attn_Wo',
        'L0_attn_bo', 'L0_attn_qk_scale', 'L0_ffn_gate_W', 'L0_ffn_expert_W', 'L0_ffn_out_W', 'L1_attn_Wqkv',
        'L1_attn_bqkv', 'L1_attn_Wout', 'L1_attn_bout', 'L1_ffn_group_centroids', 'L1_ffn_expert_centroids',
        'L1_ffn_bias', 'L1_ffn_wg', 'L1_ffn_wu', 'L1_ffn_wd', 'L1_ffn_sg', 'L1_ffn_su', 'L1_ffn_sd']


def kernel(**inputs):
    import concourse.bacc as bacc
    from concourse.bass_utils import run_bass_kernel_spmd

    nc = bacc.Bacc("TRN2", target_bir_lowering=False, num_devices=1)
    arrays = {f"in_{n}_dram": np.ascontiguousarray(inputs[n]) for n in _INS}
    arrays.update(zip(("consts_dram", "cos_dram", "sin_dram"), constants()))
    aps = {n: nc.dram_tensor(n, v.shape, mybir.dt.from_np(v.dtype), kind="ExternalInput").ap()
           for n, v in arrays.items()}
    out = nc.dram_tensor("out_dram", (1, NTOK, P), F32, kind="ExternalOutput").ap()
    build(nc, {n: aps[f"in_{n}_dram"] for n in _INS}, aps["consts_dram"], aps["cos_dram"], aps["sin_dram"], out)
    r = run_bass_kernel_spmd(nc, [arrays], core_ids=[0])
    return r.results[0]["out_dram"]
```

```python
from contextlib import ExitStack
from collections import namedtuple

import numpy as np

import concourse.bass as bass
from concourse import mybir

F32 = mybir.dt.float32
BF16 = mybir.dt.bfloat16
I32 = mybir.dt.int32
U32 = mybir.dt.uint32
ALU = mybir.AluOpType
ACT = mybir.ActivationFunctionType
AX = mybir.AxisListType

P = 128
NTOK = 2048
NT = NTOK // P
CH = 512
NCH = NTOK // CH
TPC = CH // P
LN_EPS = 1e-5

E0 = 8
TOP_P = 0.3

NH = 16
HD = P // NH
QUADS = NH // 4
ITERS = QUADS * NCH
CHUNKS = 2 * NT
VW = HD + 1
PRING = 8
NORM_EPS = 1e-6
RUNS_K = ((0, 3), (0, 2), (0, 1))
RUNS_Q = ((0, 3), (1, 3), (2, 3))
SHIFT_ROW = 6 * HD
Q_ROWS = SHIFT_ROW + 2
BOUND_MAX = 40.0
MAX_STEPS = ITERS * 4 * TPC

NE = 32
NG = 8
TOPG = NG // 2
TOPK = 4
HID = 256
CAP = int(NTOK / NE * TOPK * 1.25)
RT = (CAP + P - 1) // P
BUF = RT * P
ROWS = NE * BUF
TAIL = CAP - (RT - 1) * P
RING = 4
FAR = float(2 * ROWS)
PW = P + 2 * TOPK

C_ID, C_PERM, C_ROT, C_G, C_U, C_ONE, C_PAD = 0, 128, 256, 384, 512, 640, 768
C_I8 = C_PAD + QUADS * P
C_I32 = C_I8 + NG
C_BASE = C_I32 + NE
C_RES = C_BASE + NE
C_DEST = C_RES + NT
C_ROW = C_DEST + NT * TOPK
C_END = C_ROW + RT


def constants():
    c = np.zeros((P, C_END), np.float32)
    i = np.arange(P)
    c[:, C_ID:C_ID + P] = np.eye(P)
    for h in range(NH):
        for d in range(HD):
            m = NH * d + h
            c[HD * h + d, C_PERM + m] = 1.0
            half = HD // 2
            c[HD * h + (d + half) % HD, C_ROT + m] = -1.0 if d < half else 1.0
    c[:, C_G:C_G + P] = (i[:, None] % NH) == (i[None, :] % NH)
    c[:, C_U:C_U + P] = i[:, None] < i[None, :]
    c[:, C_ONE:C_ONE + P] = 1.0
    for h in range(NH):
        for d in range(HD):
            c[h * HD + d, C_PAD + (h // 4) * P + 32 * (h % 4) + d] = 1.0
    c[:, C_I8:C_I8 + NG] = np.arange(NG)
    c[:, C_I32:C_I32 + NE] = np.arange(NE)
    c[:, C_BASE:C_BASE + NE] = np.arange(NE) * BUF
    c[:, C_RES:C_RES + NT] = 1.0
    c[:, C_RES] = 0.0
    token = P * np.arange(NT)[None, :, None] + i[:, None, None]
    c[:, C_DEST:C_DEST + NT * TOPK] = (TOPK * token + np.arange(TOPK)).reshape(P, -1)
    c[:, C_ROW:C_ROW + RT] = P * np.arange(RT) + i[:, None]
    inv = (np.float32(1.0) / np.float32(10000.0) ** (np.arange(0, HD, 2, dtype=np.float32) / np.float32(HD)))
    ang = np.outer(np.arange(NTOK, dtype=np.float32), inv.astype(np.float32)).astype(np.float32)
    ang = ang[:, (i // NH) % (HD // 2)].T
    return c, np.ascontiguousarray(np.cos(ang), np.float32), np.ascontiguousarray(np.sin(ang), np.float32)


def build(nc, a, consts_d, cos_d, sin_d, out, stages=6):
    ctx = ExitStack()
    with ctx:
        def sb(name, shape, dt=F32):
            return ctx.enter_context(nc.sbuf_tensor(name, shape, dt))

        def sem(name):
            return ctx.enter_context(nc.semaphore(name))

        def sems(prefix, names):
            return namedtuple(prefix, names)(*[sem(f"{prefix}_{n}") for n in names.split()])

        X = sb("X", [P, NT, P])
        XNT = sb("XNT", [P, NTOK])
        Kt = sb("Kt", [P, NH // 2, NTOK], BF16)
        Qt = sb("Qt", [P, ITERS, 4, CH], BF16)
        RA = sb("RA", [P, 8192])
        RB = sb("RB", [P, 8192])
        V = sb("V", [P, NT, P])
        raw0 = V[:, NT - 10:NT - 8, :]
        raw = V[:, NT - 8:NT, :]
        CST = sb("CST", [P, C_END])
        U16 = sb("U16", [P, 2, P], BF16)
        wcat = sb("wcat", [P, 2 * P + E0])
        w0 = sb("w0", [P, 3, P])
        w1 = sb("w1", [P, 5, P])
        wo = sb("wo", [P, 2, QUADS, P])
        wt = sb("wt", [P, 2, P])
        cen = V[0:NG + NE, 3, :]
        cen2 = V[0:NG + NE, 4, :]
        cst1 = sb("cst1", [NG + NE, 4])
        r40 = sb("r40", [P, NG + NE])
        bcol = sb("bcol", [P, 8])
        brow = sb("brow", [P, 4, P])
        bexp = sb("bexp", [P, NE])
        st = sb("st", [P, NT, 6])
        mv = sb("mv", [P, NT, 2])
        sm = sb("sm", [P, 8, NT])
        km = sb("km", [P, 12])
        flag = sb("flag", [1, 1], I32)
        PS = ctx.enter_context(nc.psum_tensor("PS", [P, 8, CH], F32))

        RA16 = RA[:, :].bitcast(BF16)
        KP = RA16[:, 0:3 * NTOK].rearrange("p (s n) -> p s n", s=3)
        QP = RA16[:, 3 * NTOK:6 * NTOK].rearrange("p (s n) -> p s n", s=3)
        SHB = RA16[:, 6 * NTOK:7 * NTOK]
        MX = RA[:, 0:MAX_STEPS]
        MXT = RA16[:, 2 * MAX_STEPS:3 * MAX_STEPS].rearrange("p (a n) -> p a n", a=2)
        COS, SIN = RA[:, 0:NTOK], RA[:, NTOK:2 * NTOK]
        AT = RA[:, :].rearrange("p (i n) -> p i n", i=ITERS)
        wq_, wk_, t1_, t2_ = (RB[:, i * NTOK:(i + 1) * NTOK] for i in range(4))
        PR = RB[:, :].rearrange("p (s n) -> p s n", s=PRING)
        VQ = XNT[:, 0:2 * NT * 4 * VW].rearrange("p (b t h w) -> p b t h w", b=2, t=NT, h=4)
        XNA = RB[:, 3 * NTOK:4 * NTOK].rearrange("p (t d) -> p t d", t=NT)
        RS = XNT[:, NTOK - CH:NTOK]

        XNW = RA[:, 0:NT * PW].rearrange("p (t d) -> p t d", t=NT)
        XN = XNW[:, :, 0:P]
        GB = RB[:, :].rearrange("p (j d) -> p j d", j=NT * TOPK)
        o = NT * PW
        SH = RA[:, o:o + 2 * NTOK].rearrange("p (k n) -> p k n", k=2)
        o += 2 * NTOK
        ws = RA[:, o:o + 2 * HID].rearrange("p (k n) -> p k n", k=2)
        o += 2 * HID
        wsd = RA[:, o:o + 2 * P].rearrange("p (k n) -> p k n", k=2)
        WR = V[:, :, :].rearrange("p a b -> p (a b)")
        OH2 = RB[:, 3 * NTOK:4 * NTOK]
        OH = RB[:, 2 * NTOK:3 * NTOK]
        EW = HID * 3
        WRING = RB[:, 0:RING * EW].rearrange("p (r n) -> p r n", r=RING)
        o = RING * EW
        XET = RB[:, o:o + 2 * CAP].rearrange("p (b n) -> p b n", b=2)
        o += 2 * CAP
        XE = RB[:, o:o + RING * RT * PW].rearrange("p (r c d) -> p r c d", r=RING, c=RT)
        o += RING * RT * PW
        HT = RB[:, o:o + 4 * CAP].rearrange("p (b k n) -> p b k n", b=2, k=2)
        o += 4 * CAP
        SIL = RB[:, o:o + 2 * CAP].rearrange("p (k n) -> p k n", k=2)
        o += 2 * CAP
        OB = RB[:, o:o + 2 * BUF].rearrange("p (b c d) -> p b c d", b=2, c=RT)
        assert o + 2 * BUF <= 4 * NTOK
        S40 = WR[:, 0:NT * (NG + NE)].rearrange("p (t e) -> p t e", t=NT)
        MSK = WR[:, 640:1152]
        POS = WR[:, 1152:1664]
        ESC = WR[:, 1664:1664 + P].rearrange("p (t g) -> p t g", t=NT)
        rtt = sb("rtt", [P, 4, P])
        top8 = rtt[:, 0, :].rearrange("p (t k) -> p t k", t=NT)
        idx8 = rtt[:, 1, :].bitcast(U32).rearrange("p (t k) -> p t k", t=NT)
        idxf = rtt[:, 2, :].rearrange("p (t k) -> p t k", t=NT)
        gmk = rtt[:, 3, :].rearrange("p (t g) -> p t g", t=NT)
        gsl = sb("gsl", [P, 3, NT * TOPK])
        gate = gsl[:, 0, :]
        slotf = gsl[:, 1, :]
        srow = gsl[:, 2, :].bitcast(U32)
        M16 = sb("M16", [P, NE * NT], BF16)
        UNUSED = WR[:, 1792:1792 + NE * RT]
        HIT = sb("HIT", [P, RT, TOPK])
        DST = sb("DST", [P, 2, RT])
        DI = sb("DI", [P, 2, RT], U32)
        XD = nc.dram_tensor("expert_rows", (ROWS, PW), F32, kind="Internal").ap()
        YD = nc.dram_tensor("weighted_terms", (NTOK * TOPK, P), F32, kind="Internal").ap()

        ident = CST[:, C_ID:C_ID + P]
        rotT = CST[:, C_ROT:C_ROT + P]
        G = CST[:, C_G:C_G + P]

        dram_x = a["L0_attn_x"].rearrange("b (t p) d -> p (b t) d", p=P)
        dram_out = out.rearrange("b (t p) d -> p (b t) d", p=P)
        wqkv_d = a["L1_attn_Wqkv"].rearrange("(s o) d -> o s d", o=P)

        s_in = sem("s_in")
        s_x = sem("s_x")
        s_tab = sem("s_tab")
        s_out = sem("s_out")
        N_IN = [0]
        dch = sem("dch")
        ach = sem("ach")
        s_x_ready = sem("s_x_ready")
        SET = sems("setup", "mm1 cp1 mm2 cp2 cen sq cn ctr zero ones onesrow fill")
        NS = sems("n", "var std xn tr xt")
        FS = {i: sems(f"f{i}", "g d e y used") for i in (0, 2)}
        AS = {i: sems(f"a{i}", "pj pj2 used sq n2 rt hi r mid parts st v vr s exp vq pv at o fl fm gs gm gd o2")
              for i in (1, 4)}

        MS = {i: sems(f"m{i}", "w lg sq sr rn mk pfx fill d e slot si sh sd sdu sc xt gu h sil dn ev di dl go") for i in (3, 5)}
        LQ = [sem(f"lq{q}") for q in range(QUADS)]
        LX = [sem(f"lx{r}") for r in range(RING)]
        LW = [sem(f"lw{r}") for r in range(RING)]
        SO = [sem(f"so{b}") for b in range(2)]
        GA = [sem(f"ga{t}") for t in range(NCH)]

        block = ctx.enter_context(nc.Block())

        loads = [
            (CST[:, :], consts_d),
            (raw[:, 0:2, :], a["L0_ffn_expert_W"][0:2].rearrange("e h d -> h e d")),
            (raw[:, 2, :], a["L0_ffn_out_W"]),
            (raw[:, 3, :], a["L0_attn_Wo"]),
            (raw[:, 4:7, :], wqkv_d),
            (raw[:, 7, :], a["L1_attn_Wout"]),
            (raw0[:, 0, :], a["L0_attn_Wq"]),
            (raw0[:, 1, :], a["L0_attn_Wk"]),
            (w0[:, 2, :], a["L0_attn_Wv"]),
            (cen[0:NG, :], a["L1_ffn_group_centroids"]),
            (cen[NG:NG + NE, :], a["L1_ffn_expert_centroids"]),
            (cen2[0:E0, :], a["L0_ffn_gate_W"]),
            (bcol[:, 0:1], a["L0_attn_bq"].rearrange("(p o) -> p o", o=1)),
            (bcol[:, 1:2], a["L0_attn_bk"].rearrange("(p o) -> p o", o=1)),
            (bcol[:, 2:3], a["L1_attn_bqkv"][0:P].rearrange("(p o) -> p o", o=1)),
            (bcol[:, 3:4], a["L1_attn_bqkv"][P:2 * P].rearrange("(p o) -> p o", o=1)),
            (bcol[:, 6:7], a["L0_attn_qk_scale"].rearrange("a b c d -> (a b c) d").to_broadcast([P, 1])),
            (brow[:, 0, :], a["L0_attn_bv"].rearrange("(o d) -> o d", o=1).to_broadcast([P, P])),
            (brow[:, 1, :], a["L0_attn_bo"].rearrange("(o d) -> o d", o=1).to_broadcast([P, P])),
            (brow[:, 2, :], a["L1_attn_bqkv"][2 * P:3 * P].rearrange("(o d) -> o d", o=1).to_broadcast([P, P])),
            (brow[:, 3, :], a["L1_attn_bout"].rearrange("(o d) -> o d", o=1).to_broadcast([P, P])),
            (bexp[:, :], a["L1_ffn_bias"].rearrange("(o d) -> o d", o=1).to_broadcast([P, NE])),
        ]
        ALL_IN = 16 * len(loads)

        KD = nc.dram_tensor("k_parts", (SHIFT_ROW, NH, NTOK), BF16, kind="Internal").ap()
        QD = nc.dram_tensor("q_parts", (Q_ROWS, NH, NTOK), BF16, kind="Internal").ap()
        MD = nc.dram_tensor("maxima", (MAX_STEPS, P), BF16, kind="Internal").ap()

        def attention_loads(eng, s):
            for parts, dram, runs in ((KP, KD, RUNS_K), (QP, QD, RUNS_Q)):
                row = 0
                for lo, hi in runs:
                    n = hi - lo
                    eng.dma_start(dram[row:row + HD * n].rearrange("(s d) h n -> (d h) s n", s=n),
                                  parts[:, lo:hi, :]).then_inc(s.st, 16)
                    row += HD * n
            eng.dma_start(QD[SHIFT_ROW], SHB[0:NH, :]).then_inc(s.st, 16)
            eng.wait_ge(s.st, 16 * 7)
            for q in range(QUADS):
                done = LQ[q]
                for j in range(4):
                    h, r0 = 4 * q + j, 64 * (j % 2)
                    eng.dma_start(Kt[r0:r0 + SHIFT_ROW, 2 * q + j // 2, :], KD[:, h, :]).then_inc(done, 16)
                    eng.dma_start(Qt[r0:r0 + Q_ROWS, NCH * q:NCH * q + NCH, j, :],
                                  QD[:, h, :].rearrange("r (c n) -> r c n", c=NCH)).then_inc(done, 16)

        QUAD_LOADED = 16 * 4 * 2

        def bound_is_large(eng, s):
            eng.wait_ge(s.fl, 2)
            return eng.value_load(flag[0:1, 0:1], min_val=0, max_val=1) > 0

        def maximum_loads(eng, s):
            with eng.If(bound_is_large(eng, s)):
                eng.wait_ge(s.gm, MAX_STEPS + 3)
                eng.dma_start(MD.rearrange("(a r) p -> r a p", a=2), MXT).then_inc(s.gd, 16)
                eng.wait_ge(s.gd, 16)
                rows = MD.rearrange("(q c j t) p -> q j c (t p)", q=QUADS, c=NCH, j=4)
                for q in range(QUADS):
                    for j in range(4):
                        r = 64 * (j % 2) + SHIFT_ROW + 1
                        eng.dma_start(Qt[r:r + 1, NCH * q:NCH * q + NCH, j, :], rows[q, j].unsqueeze(0)).then_inc(s.gd, 16)
                eng.wait_ge(s.gd, 16 * (1 + NH))

        @block.sync
        def _(sp):
            def routed_dmas(i):
                s = MS[i]
                sp.wait_ge(NS.xn, NT * i + 1)
                sp.dma_start(ws[:, 0, :], a["L1_ffn_sg"]).then_inc(s.w, 16)
                sp.dma_start(ws[:, 1, :], a["L1_ffn_su"]).then_inc(s.w, 16)
                sp.dma_start(wsd, a["L1_ffn_sd"].rearrange("(k p) d -> p k d", p=P)).then_inc(s.w, 16)

                def load_weights(e, r):
                    one = bass.ds(e, 1)
                    sp.dma_start(WRING[:, r, 0:HID], a["L1_ffn_wg"][one].rearrange("e d h -> d (e h)")).then_inc(LW[r], 16)
                    sp.dma_start(WRING[:, r, HID:2 * HID], a["L1_ffn_wu"][one].rearrange("e d h -> d (e h)")).then_inc(LW[r], 16)
                    sp.dma_start(WRING[:, r, 2 * HID:3 * HID].rearrange("p (k d) -> p k d", k=2),
                                 a["L1_ffn_wd"][one].rearrange("e (k p) d -> p (e k) d", p=P)).then_inc(LW[r], 16)

                def load_rows(e, r):
                    sp.dma_start(XE[:, r, :, :], XD[bass.ds(e * BUF, BUF)].rearrange("(c p) d -> p c d", p=P)
                                 ).then_inc(LX[r], 16)

                for r in range(RING):
                    load_weights(r, r)
                turns = 1 if i == 3 else 2
                sp.wait_ge(s.sc, 16 * NT * TOPK)
                for r in range(RING):
                    load_rows(r, r)
                with sp.Fori(0, NE // RING - 1) as u:
                    for r in range(RING):
                        e = u * RING + r
                        sp.wait_ge(s.dn, e + 1)
                        sp.wait_ge(s.di, e + 1)
                        load_weights(e + RING, r)
                        load_rows(e + RING, r)
                for b in range(2):
                    sp.wait_ge(SO[b], 16 * RT * NE // 2 * turns)
                sp.wait_ge(s.h, 2 * NE)
                sp.wait_ge(s.dn, NE)
                sp.wait_ge(s.di, NE)
                for c in range(NCH):
                    sp.dma_start(GB[:, TOPK * TPC * c:TOPK * TPC * (c + 1), :].rearrange("p (t k) d -> p t (k d)", t=TPC),
                                 YD[TOPK * CH * c:TOPK * CH * (c + 1)].rearrange("(t p k) d -> p t (k d)", t=TPC, k=TOPK)
                                 ).then_inc(GA[c], 16)

            for c in range(NCH):
                sp.dma_start(X[:, TPC * c:TPC * c + TPC, :], dram_x[:, TPC * c:TPC * c + TPC, :]).then_inc(s_x, 16)
            for dst, src in loads:
                sp.dma_start(dst, src).then_inc(s_in, 16)
            sp.wait_ge(SET.zero, 2)
            sp.wait_ge(SET.ones, 1)
            for r in (SHIFT_ROW, 64 + SHIFT_ROW):
                for pair in range(NH // 2):
                    sp.dma_start(Kt[r:r + 2, pair, :], SHB[0:2, :]).then_inc(SET.onesrow, 16)
            sp.dma_start(QD[SHIFT_ROW + 1:Q_ROWS], Qt[0:1, :, :, :]).then_inc(SET.onesrow, 16)
            zeros = Qt[:, :, :, :].rearrange("p i h n -> p (i h n)").bitcast(F32)
            sp.dma_start(XD.rearrange("(p r) d -> p (r d)", p=P),
                         zeros[:, 0:ROWS // P * PW]).then_inc(SET.fill, 16)
            sp.dma_start(YD.rearrange("(p r) d -> p (r d)", p=P), zeros[:, 0:NTOK * TOPK]).then_inc(SET.fill, 16)
            sp.wait_ge(SET.onesrow, 16 * (NH + 1))
            sp.wait_ge(SET.fill, 32)
            for i in range(stages):
                if i in AS:
                    sp.wait_ge(AS[i].parts, 3)
                    attention_loads(sp, AS[i])
                    maximum_loads(sp, AS[i])
                if i in MS:
                    routed_dmas(i)
            sp.wait_ge(s_x_ready, stages)
            for c in range(NCH):
                sp.dma_start(dram_out[:, TPC * c:TPC * c + TPC, :], X[:, TPC * c:TPC * c + TPC, :]).then_inc(s_out, 16)
            sp.wait_ge(s_out, 16 * NCH)

        @block.gpsimd
        def _(pool):
            nc.gpsimd.memset(SHB, 1.0).then_inc(SET.ones, 1)
            nc.gpsimd.memset(Kt[:, :, :], 0.0).then_inc(SET.zero, 1)
            nc.gpsimd.memset(Qt[:, :, :, :], 0.0).then_inc(SET.zero, 1)
            for i in range(stages):
                if i not in MS:
                    continue
                s = MS[i]
                pool.wait_ge(s.slot, 1)
                if i == 3:
                    pool.wait_ge(SET.fill, 32)
                for j in range(NT * TOPK):
                    nc.gpsimd.indirect_dma_start(XD, bass.IndirectOffsetOnAxis(srow[:, j:j + 1], 0), XNW[:, j // TOPK, :],
                                                 None, bounds_check=ROWS - 1, oob_is_err=False).then_inc(s.sc, 16)
                with pool.Fori(0, NE // 2) as u:
                    for b in range(2):
                        pool.wait_ge(s.di, 2 * u + (b + 1))
                        pool.wait_ge(s.ev, 2 * u + (b + 1))
                        pool.sem_inc(s.go, 1)
                        for c in range(RT):
                            n_ = P if c < RT - 1 else TAIL
                            nc.gpsimd.indirect_dma_start(
                                YD, bass.IndirectOffsetOnAxis(DI[0:n_, b, c:c + 1], 0), OB[0:n_, b, c, :], None,
                                bounds_check=NTOK * TOPK - 1, oob_is_err=False).then_inc(SO[b], 16)

        @block.vector
        def _(dve):
            count = [0]

            def link(ins):
                count[0] += 1
                ins.then_inc(dch, 1)
                dve.wait_ge(dch, count[0])

            def setup():
                dve.wait_ge(s_in, ALL_IN)
                nc.vector.tensor_copy(U16[:, 0, :], CST[:, C_U:C_U + P])
                nc.vector.tensor_copy(U16[:, 1, :], CST[:, C_ONE:C_ONE + P])
                link(nc.vector.tensor_scalar(bcol[:, 7:8], bcol[:, 6:7], -1.0, None, ALU.mult))
                link(nc.vector.tensor_tensor(bcol[:, 7:8], bcol[:, 7:8], bcol[:, 6:7], ALU.min))
                link(nc.vector.tensor_tensor(cen2x, cen, cen, ALU.mult))
                nc.vector.tensor_reduce(cst1[:, 0:1], cen2x, AX.X, ALU.add).then_inc(SET.sq, 1)
                dve.wait_ge(SET.cen, 1)
                link(nc.vector.tensor_scalar(cst1[:, 2:3], cst1[:, 1:2], 1e-12, None, ALU.max))
                link(nc.vector.reciprocal(cst1[:, 3:4], cst1[:, 2:3]))
                nc.vector.tensor_scalar(cen, cen, cst1[:, 3:4], None, ALU.mult).then_inc(SET.cn, 1)

            def norm(i, XNi):
                s = NS
                if i == 0:
                    dve.wait_ge(s_x, 16 * NCH)
                for t in range(NT):
                    last = nc.vector.bn_stats(st[:, t, :], X[:, t, :])
                link(last)
                for t in range(NT):
                    last = nc.vector.bn_aggr(mv[:, t, :], st[:, t, :])
                link(last)
                nc.vector.tensor_scalar(sm[:, 0, :], mv[:, :, 1], LN_EPS, None, ALU.add).then_inc(s.var, 1)
                dve.wait_ge(s.std, i + 1)
                link(nc.vector.reciprocal(sm[:, 2, :], sm[:, 1, :]))
                for t in range(NT):
                    nc.vector.tensor_scalar(XNi[:, t, :], X[:, t, :], mv[:, t, 0:1], sm[:, 2, t:t + 1],
                                            ALU.subtract, ALU.mult).then_inc(s.xn, 1)

            def ffn0(i):
                s = FS[i]
                lg = PS[:, 4, 0:NT * E0].rearrange("p (t e) -> p t e", e=E0)
                ge = V[:, 0, :].rearrange("p (t e) -> p t e", e=E0)
                pp = V[:, 1, :].rearrange("p (t e) -> p t e", e=E0)
                ov = V[:, 2, :].rearrange("p (t e) -> p t e", e=E0)
                dve.wait_ge(s.g, 1)
                link(nc.vector.tensor_reduce(sm[:, 3, :], lg, AX.X, ALU.max))
                nc.vector.tensor_tensor(ge, lg, sm[:, 3, :].unsqueeze(2).to_broadcast([P, NT, E0]),
                                        ALU.subtract).then_inc(s.d, 1)
                dve.wait_ge(s.e, 1)
                link(nc.vector.tensor_reduce(sm[:, 4, :], pp, AX.X, ALU.add))
                link(nc.vector.reciprocal(sm[:, 5, :], sm[:, 4, :]))
                link(nc.vector.tensor_tensor(ge, pp, sm[:, 5, :].unsqueeze(2).to_broadcast([P, NT, E0]), ALU.mult))
                link(nc.vector.tensor_scalar(ov, ge, TOP_P, None, ALU.is_gt))
                link(nc.vector.tensor_reduce(sm[:, 6, :], ov, AX.X, ALU.add))
                nc.vector.tensor_scalar(sm[:, 7, :], sm[:, 6, :], -0.5, 0.5 * E0, ALU.mult, ALU.add)
                link(nc.vector.scalar_tensor_tensor(out=sm[:, 4, :], in0=sm[:, 6, :], scalar=0.5,
                                                    in1=ge[:, :, 1], op0=ALU.mult, op1=ALU.mult))
                link(nc.vector.tensor_tensor(sm[:, 3, :], sm[:, 7, :], ge[:, :, 0], ALU.mult))
                for pr in range(NT // 2):
                    dve.wait_ge(s.y, pr + 1)
                    b = 5 + pr % 3
                    for e in range(2):
                        for k in range(2):
                            t = 2 * pr + k
                            last = nc.vector.scalar_tensor_tensor(
                                out=X[:, t, :], in0=PS[:, b, 2 * P * k + P * e:2 * P * k + P * e + P],
                                scalar=sm[:, 3 + e, t:t + 1], in1=X[:, t, :], op0=ALU.mult, op1=ALU.add)
                        if e == 0:
                            link(last)
                    last.then_inc(s.used, 1)
                dve.wait_ge(s.used, NT // 2)
                nc.vector.tensor_copy(sm[:, 5, 0:1], sm[:, 3, 0:1]).then_inc(s_x_ready, 1)

            def set_flag(s, a, b):
                nc.vector.tensor_tensor(km[:, 7:8], a, b, ALU.mult).then_inc(s.fl, 1)
                dve.wait_ge(s.fm, 1)
                link(nc.vector.tensor_reduce(km[0:1, 6:7], PS[0:1, 0, 0:P], AX.X, ALU.max))
                nc.vector.tensor_scalar(flag[:, :], km[0:1, 6:7], BOUND_MAX ** 2, None, ALU.is_gt).then_inc(s.fl, 1)

            def exact_maximum(s):
                with dve.If(bound_is_large(dve, s)):
                    nc.vector.tensor_copy(km[:, 6:7], km[:, 7:8]).then_inc(s.gm, 2)
                    with dve.Fori(0, ITERS) as u:
                        for k in range(4 * TPC):
                            b = 4 * (k % 2)
                            dve.wait_ge(s.gs, u * (4 * TPC) + (k + 1))
                            nc.vector.tensor_reduce(MX[:, bass.ds(u * (4 * TPC) + k, 1)], PS[:, b:b + 4, :],
                                                    AX.XY, ALU.max).then_inc(s.gm, 1)
                    dve.wait_ge(s.gs, MAX_STEPS + 1)
                    nc.vector.tensor_scalar(MXT, PS[:, 0, 0:MAX_STEPS].rearrange("p (a n) -> p a n", a=2), -1.0, None,
                                            ALU.mult).then_inc(s.gm, 1)
                    nc.vector.memset(PS[:, 4:8, :].rearrange("p a b -> p (a b)"), 0.0).then_inc(s.gm, 1)

            def attention(i):
                s = AS[i]
                rope = i == 4
                if rope:
                    dve.wait_ge(s_tab, 32)
                else:
                    dve.wait_ge(SET.onesrow, 16 * (NH + 1))
                for c in range(NCH):
                    cs = slice(c * CH, c * CH + CH)
                    dve.wait_ge(s.pj, c + 1)
                    b = 4 if c % 2 == 0 else 0
                    if rope:
                        for w, z, zb, n in ((wk_, t1_, 3, 2), (wq_, t2_, 2, 0)):
                            nc.vector.scalar_tensor_tensor(out=w[:, cs], in0=PS[:, b + n, :], scalar=bcol[:, zb:zb + 1],
                                                           in1=COS[:, cs], op0=ALU.add, op1=ALU.mult)
                            last = nc.vector.scalar_tensor_tensor(out=z[:, cs], in0=PS[:, b + n + 1, :],
                                                                  scalar=bcol[:, zb + 2:zb + 3], in1=SIN[:, cs],
                                                                  op0=ALU.add, op1=ALU.mult)
                        last.then_inc(s.used, 1)
                        dve.wait_ge(s.used, c + 1)
                        nc.vector.tensor_tensor(wk_[:, cs], wk_[:, cs], t1_[:, cs], ALU.add).then_inc(s.sq, 1)
                        nc.vector.tensor_tensor(wq_[:, cs], wq_[:, cs], t2_[:, cs], ALU.add).then_inc(s.sq, 1)
                    else:
                        nc.vector.tensor_scalar(wk_[:, cs], PS[:, b + 2, :], bcol[:, 1:2], None, ALU.add).then_inc(s.sq, 1)
                        nc.vector.tensor_scalar(wq_[:, cs], PS[:, b, :], bcol[:, 0:1], None, ALU.add).then_inc(s.sq, 1)
                        dve.wait_ge(s.sq, 2 * c + 2)
                        nc.vector.tensor_copy(km[:, 6:7], wq_[:, 0:1]).then_inc(s.used, 1)
                if rope:
                    dve.wait_ge(s.n2, 2 * NCH)
                    for c in range(NCH):
                        last = nc.vector.tensor_reduce(km[:, c:c + 1], PS[:, c, :], AX.X, ALU.max)
                    link(last)
                    for c in range(NCH):
                        last = nc.vector.tensor_reduce(km[:, 8 + c:9 + c], PS[:, NCH + c, :], AX.X, ALU.max)
                    link(nc.vector.tensor_reduce(km[:, 4:5], km[:, 0:NCH], AX.X, ALU.max))
                    link(nc.vector.tensor_reduce(km[:, 6:7], km[:, 8:8 + NCH], AX.X, ALU.max))
                    set_flag(s, km[:, 4:5], km[:, 6:7])
                    for c in range(NCH):
                        cs = slice(c * CH, c * CH + CH)
                        nc.vector.tensor_scalar(t1_[:, cs], PS[:, NCH + c, :], km[:, 4:5], None, ALU.mult).then_inc(s.r, 1)
                    for c in range(NCH):
                        cs = slice(c * CH, c * CH + CH)
                        dve.wait_ge(s.rt, c + 1)
                        last = nc.vector.tensor_scalar(SHB[:, cs], t1_[:, cs], -1.0, None, ALU.mult)
                    last.then_inc(s.parts, 1)
                    dve.wait_ge(s.parts, 1)
                    rn = 0
                else:
                    for c in range(NCH):
                        cs = slice(c * CH, c * CH + CH)
                        for n, (w, z) in enumerate(((wk_, t1_), (wq_, t2_))):
                            dve.wait_ge(s.rt, 2 * c + n + 1)
                            link(nc.vector.tensor_scalar(z[:, cs], z[:, cs], NORM_EPS, None, ALU.add))
                            link(nc.vector.reciprocal(z[:, cs], z[:, cs]))
                            if n == 0:
                                nc.vector.tensor_tensor(w[:, cs], w[:, cs], z[:, cs], ALU.mult).then_inc(s.r, 1)
                            else:
                                nc.vector.scalar_tensor_tensor(out=w[:, cs], in0=w[:, cs], scalar=bcol[:, 6:7],
                                                               in1=z[:, cs], op0=ALU.mult, op1=ALU.mult).then_inc(s.r, 1)
                    set_flag(s, bcol[:, 7:8], bcol[:, 7:8])
                    dve.wait_ge(s.r, 2 * NCH)
                    nc.vector.tensor_scalar(SHB[:, :], wq_[:, :], 0.0, bcol[:, 7:8], ALU.mult, ALU.add).then_inc(s.parts, 1)
                for n, (w, z, hi) in enumerate(((wk_, t1_, KP[:, 0, :]), (wq_, t2_, QP[:, 2, :]))):
                    for c in range(NCH):
                        cs = slice(c * CH, c * CH + CH)
                        dve.wait_ge(s.hi, NCH * n + c + 1)
                        nc.vector.tensor_tensor(z[:, cs], w[:, cs], hi[:, cs], ALU.subtract).then_inc(s.mid, 1)
                for n, (z, parts, low) in enumerate(((t1_, KP, 2), (t2_, QP, 0))):
                    for c in range(NCH):
                        cs = slice(c * CH, c * CH + CH)
                        dve.wait_ge(s.o, NCH * n + c + 1)
                        last = nc.vector.tensor_tensor(parts[:, low, cs], z[:, cs], parts[:, 1, cs], ALU.subtract)
                    last.then_inc(s.parts, 1)
                for c in range(NCH):
                    dve.wait_ge(s.v, c + 1)
                    last = nc.vector.tensor_tensor(
                        V[:, TPC * c:TPC * c + TPC, :], PS[:, c, :].rearrange("p (t d) -> p t d", t=TPC),
                        brow[:, 2 * (i == 4), :].unsqueeze(1).to_broadcast([P, TPC, P]), ALU.add)
                link(last)
                nc.vector.tensor_tensor(X[:, :, :], X[:, :, :],
                                        brow[:, 1 + 2 * (i == 4), :].unsqueeze(1).to_broadcast([P, NT, P]), ALU.add)
                nc.vector.memset(PS[:, 4:8, :].rearrange("p a b -> p (a b)"), 0.0)
                dve.wait_ge(s.v, NCH)
                nc.vector.memset(VQ[:, :, :, :, HD:VW].rearrange("p b t h w -> p (b t h) w"), 1.0)
                V4 = V[:, :, :].rearrange("p t (q h w) -> p t q h w", q=QUADS, h=4)
                for b in range(2):
                    nc.vector.tensor_copy(VQ[:, b, :, :, 0:HD], V4[:, :, 0, :, :]).then_inc(s.vq, 1)
                dve.wait_ge(s.st, 16 * 7)
                exact_maximum(s)
                oc = s.o2
                ocn = 0
                Vf = V[:, :, :]

                def step(it, b, more):
                    dve.wait_ge(s.pv, it + 1)
                    at = AT[:, bass.ds(it, 1), :].rearrange("p o n -> p (o n)")
                    got = PS[:, 4 + 2 * b:6 + 2 * b, 0:CH // 2]
                    nc.vector.tensor_copy(at.rearrange("p (a n) -> p a n", a=2), got).then_inc(oc, 1)
                    for half in range(2):
                        last = nc.vector.stream_shuffle(RS[:, half * CH // 2:(half + 1) * CH // 2], got[:, half, :], [HD] * 32)
                    last.then_inc(oc, 1)
                    if more:
                        nc.vector.tensor_copy(VQ[:, b, :, :, 0:HD], Vf[:, :, bass.ds(vcol(it), 4 * HD)].rearrange(
                            "p t (h w) -> p t h w", h=4)).then_inc(s.vq, 1)
                    dve.wait_ge(oc, it * 4 + 2)
                    nc.vector.reciprocal(RS, RS).then_inc(oc, 1)
                    dve.wait_ge(oc, it * 4 + 3)
                    nc.vector.tensor_tensor(at, at, RS, ALU.mult).then_inc(oc, 1)
                    dve.wait_ge(oc, it * 4 + 4)

                def vcol(it):
                    return ((it + 2) // NCH) * (4 * HD)

                with dve.Fori(0, ITERS // 2 - 1) as u:
                    for b in range(2):
                        step(2 * u + b, b, True)
                for b in range(2):
                    step(ITERS - 2 + b, b, False)
                nc.vector.tensor_copy(km[:, 7:8], AT[:, ITERS - 1, 0:1]).then_inc(s.at, 1)
                for c in range(NCH):
                    dve.wait_ge(s.vr, c + 1)
                    last = nc.vector.tensor_tensor(X[:, TPC * c:TPC * c + TPC, :], X[:, TPC * c:TPC * c + TPC, :],
                                                   PS[:, c, :].rearrange("p (t d) -> p t d", t=TPC), ALU.add)
                link(last)
                nc.vector.tensor_copy(km[:, 6:7], X[:, 0, 0:1]).then_inc(s_x_ready, 1)

            def routed(i):
                s = MS[i]
                dve.wait_ge(NS.xn, NT * i + NT)
                nc.vector.tensor_copy(XNW[:, :, P + TOPK:PW], CST[:, C_DEST:C_DEST + NT * TOPK].rearrange("p (t k) -> p t k", t=NT))
                link(nc.vector.tensor_tensor(OH.rearrange("p (t d) -> p t d", t=NT), XN, XN, ALU.mult))
                nc.vector.tensor_reduce(sm[:, 3, :], OH.rearrange("p (t d) -> p t d", t=NT), AX.X, ALU.add).then_inc(s.sq, 1)
                dve.wait_ge(s.sr, 1)
                link(nc.vector.tensor_scalar(sm[:, 5, :], sm[:, 4, :], 1e-12, None, ALU.max))
                link(nc.vector.reciprocal(sm[:, 6, :], sm[:, 5, :]))
                dve.wait_ge(s.lg, 1)
                W = NG + NE
                for k in range(2):
                    ts_ = slice(8 * k, 8 * k + 8)
                    last = nc.vector.tensor_tensor(S40[:, ts_, :], PS[:, 4 + k, 0:8 * W].rearrange("p (t e) -> p t e", t=8),
                                                   sm[:, 6, ts_].unsqueeze(2).to_broadcast([P, 8, W]), ALU.mult)
                link(last)

                def top(values):
                    for t in range(NT):
                        last = nc.vector.max(top8[:, t, :], values(t))
                    link(last)
                    for t in range(NT):
                        last = nc.vector.max_index(idx8[:, t, :], top8[:, t, :], values(t))
                    link(last)
                    link(nc.vector.tensor_copy(idxf, idx8))

                def one_hot(dst, width, col):
                    link(nc.vector.tensor_tensor(
                        dst, CST[:, col:col + width].unsqueeze(1).unsqueeze(1).to_broadcast([P, NT, TOPK, width]),
                        idxf[:, :, 0:TOPK].unsqueeze(3).to_broadcast([P, NT, TOPK, width]), ALU.is_equal))

                top(lambda t: S40[:, t, 0:NG])
                ohg = OH[:, 0:NT * TOPG * NG].rearrange("p (t k g) -> p t k g", t=NT, k=TOPG)
                one_hot(ohg, NG, C_I8)
                link(nc.vector.tensor_reduce(gmk, ohg.rearrange("p t k g -> p t g k"), AX.X, ALU.add))
                es = MSK.rearrange("p (t e) -> p t e", t=NT)
                link(nc.vector.tensor_tensor(es, S40[:, :, NG:W], bexp[:, :].unsqueeze(1).to_broadcast([P, NT, NE]), ALU.add))
                esg = MSK.rearrange("p (t g e) -> p t g e", t=NT, g=NG)
                gb = [P, NT, NG, NE // NG]
                nc.vector.tensor_scalar(ESC, gmk, -1.0, 1e9, ALU.add, ALU.mult)
                link(nc.vector.tensor_tensor(esg, esg, gmk.unsqueeze(3).to_broadcast(gb), ALU.mult))
                link(nc.vector.tensor_tensor(esg, esg, ESC.unsqueeze(3).to_broadcast(gb), ALU.add))
                top(lambda t: es[:, t, :])
                nc.vector.tensor_copy(XNW[:, :, P:P + TOPK], idxf[:, :, 0:TOPK])
                oh = OH.rearrange("p (t k e) -> p t k e", t=NT, k=TOPK)
                one_hot(oh, NE, C_I32)
                m3 = M16[:, :].rearrange("p (e t) -> p e t", e=NE)
                with nc.allow_low_precision("zeros and ones"):
                    nc.vector.tensor_reduce(m3, oh.rearrange("p t k e -> p e t k"), AX.X, ALU.add).then_inc(s.mk, 1)
                g3 = gate.rearrange("p (t k) -> p t k", t=NT)
                nc.vector.tensor_tensor(g3, top8[:, :, 0:TOPK], top8[:, :, 0:1].to_broadcast([P, NT, TOPK]),
                                        ALU.subtract).then_inc(s.d, 1)
                nc.vector.tensor_copy(OH2[:, 0:NE * NT].rearrange("p (e t) -> p e t", e=NE),
                                      CST[:, C_RES:C_RES + NT].unsqueeze(1).to_broadcast([P, NE, NT])).then_inc(s.rn, 1)
                dve.wait_ge(s.rn, 1)
                dve.wait_ge(s.pfx, 1)
                link(nc.vector.tensor_tensor_scan(POS, OH2[:, 0:NE * NT], PS[:, 7, :], 0.0, ALU.mult, ALU.add))
                link(nc.vector.tensor_tensor(
                    UNUSED.rearrange("p (e c) -> p e c", e=NE),
                    CST[:, C_ROW:C_ROW + RT].unsqueeze(1).to_broadcast([P, NE, RT]),
                    POS.rearrange("p (e t) -> p e t", e=NE)[:, :, NT - 1:NT].to_broadcast([P, NE, RT]), ALU.is_ge))
                nc.vector.tensor_scalar(UNUSED, UNUSED, FAR, None, ALU.mult)
                link(nc.vector.tensor_tensor(POS, POS, PS[:, 7, :], ALU.subtract))
                link(nc.vector.tensor_tensor(POS, POS, PS[:, 6, :], ALU.add))
                link(nc.vector.tensor_scalar(MSK, POS, float(CAP), FAR, ALU.is_ge, ALU.mult))
                p3 = POS.rearrange("p (e t) -> p e t", e=NE)
                link(nc.vector.tensor_tensor(p3, p3, CST[:, C_BASE:C_BASE + NE].unsqueeze(2).to_broadcast([P, NE, NT]), ALU.add))
                link(nc.vector.tensor_tensor(POS, POS, MSK, ALU.add))
                oh2 = OH2.rearrange("p (t k e) -> p t k e", t=NT, k=TOPK)
                link(nc.vector.tensor_tensor(oh2, oh, p3.rearrange("p e t -> p t e").unsqueeze(2).to_broadcast([P, NT, TOPK, NE]),
                                             ALU.mult))
                link(nc.vector.tensor_reduce(slotf.rearrange("p (t k) -> p t k", t=NT), oh2, AX.X, ALU.add))
                nc.vector.tensor_copy(srow, slotf).then_inc(s.slot, 1)
                dve.wait_ge(s.e, 1)
                e3 = rtt[:, 3, 0:NT * TOPK]
                link(nc.vector.tensor_reduce(sm[:, 3, :], e3.rearrange("p (t k) -> p t k", t=NT), AX.X, ALU.add))
                link(nc.vector.reciprocal(sm[:, 4, :], sm[:, 3, :]))
                link(nc.vector.scalar_tensor_tensor(out=g3, in0=e3.rearrange("p (t k) -> p t k", t=NT), scalar=0.5,
                                                    in1=sm[:, 4, :].unsqueeze(2).to_broadcast([P, NT, TOPK]),
                                                    op0=ALU.mult, op1=ALU.mult))
                link(nc.vector.scalar_tensor_tensor(out=gate, in0=slotf, scalar=float(ROWS), in1=gate,
                                                    op0=ALU.is_lt, op1=ALU.mult))
                for st_ in range(2 * NCH):
                    c, m = st_ // 2, st_ % 2
                    dve.wait_ge(s.sh, st_ + 1)
                    hs = SH[:, m, c * CH:c * CH + CH]
                    nc.vector.tensor_tensor(hs, hs, PS[:, 2 * m + 1, :], ALU.mult).then_inc(s.si, 1)
                for c in range(NCH):
                    dve.wait_ge(s.sd, c + 1)
                    nc.vector.scalar_tensor_tensor(out=X[:, TPC * c:TPC * c + TPC, :].rearrange("p t d -> p (t d)"),
                                                   in0=PS[:, 6 + c % 2, :], scalar=0.5,
                                                   in1=X[:, TPC * c:TPC * c + TPC, :].rearrange("p t d -> p (t d)"),
                                                   op0=ALU.mult, op1=ALU.add).then_inc(s.sdu, 1)

                def take_rows(e, b):
                    dve.wait_ge(s.xt, e + 1)
                    nc.vector.tensor_copy(XET[:, b, :], PS[:, b, 0:CAP]).then_inc(s.rn, 1)

                def destinations(e, r, first=False):
                    b = r % 2
                    link_in_loop = s.dl
                    if not first:
                        dve.wait_ge(SO[b], 16 * RT * (e // 2 + sent))
                    nc.vector.scalar_tensor_tensor(
                        out=HIT[:, :, :], in0=XE[:, r, :, P:P + TOPK], scalar=CST[:, bass.ds(C_I32 + e, 1)],
                        in1=XE[:, r, :, P + TOPK:PW], op0=ALU.is_equal, op1=ALU.mult).then_inc(link_in_loop, 1)
                    dve.wait_ge(link_in_loop, 2 * e + 1)
                    nc.vector.tensor_reduce(DST[:, b, :], HIT[:, :, :], AX.X, ALU.add).then_inc(link_in_loop, 1)
                    dve.wait_ge(link_in_loop, 2 * e + 2)
                    nc.vector.tensor_tensor(DI[:, b, :], DST[:, b, :], UNUSED[:, bass.ds(RT * e, RT)], ALU.add).then_inc(s.di, 1)

                sent = 0 if i == 3 else NE // 2

                def hidden(e, b, first=False):
                    for m in range(2):
                        dve.wait_ge(s.sil, e * 2 + (m + 1))
                        if not first and m == 0:
                            dve.wait_ge(s.dn, e - 1)
                        nc.vector.tensor_tensor(HT[:, b, m, :], SIL[:, m, :], PS[:, 3 + 2 * m, 0:CAP],
                                                ALU.mult).then_inc(s.h, 1)

                for e in range(RING):
                    take_rows(e, e % 2)
                    if e:
                        hidden(e - 1, (e - 1) % 2, first=e <= 2)
                        destinations(e - 1, e - 1, first=e <= 2)
                with dve.Fori(1, NE // RING) as u:
                    for r in range(RING):
                        take_rows(u * RING + r, r % 2)
                        hidden(u * RING + (r - 1), (r - 1) % 2)
                        destinations(u * RING + (r - 1), (r - 1) % RING)
                hidden(NE - 1, (NE - 1) % 2)
                destinations(NE - 1, RING - 1)
                for t0 in range(0, NT, 4):
                    dve.wait_ge(GA[t0 // 4], 16 * (1 if i == 3 else 2))
                    for k in range(TOPK):
                        for t in range(t0, t0 + 4):
                            j = TOPK * t + k
                            last = nc.vector.scalar_tensor_tensor(out=X[:, t, :], in0=GB[:, j, :], scalar=gate[:, j:j + 1],
                                                                  in1=X[:, t, :], op0=ALU.mult, op1=ALU.add)
                        link(last)
                nc.vector.tensor_copy(km[:, 7:8], X[:, 0, 0:1]).then_inc(s_x_ready, 1)

            cen2x = XNT[0:NG + NE, 0:P]
            setup()
            for i in range(stages):
                norm(i, XNA if i in (1, 4) else XN)
                if i in FS:
                    ffn0(i)
                elif i in AS:
                    attention(i)
                else:
                    routed(i)

        @block.scalar
        def _(act):
            def setup():
                act.wait_ge(SET.mm1, 1)
                nc.scalar.copy(wt[:, 0, :], PS[:, 0, 0:P])
                nc.scalar.copy(wcat[:, 2 * P:2 * P + E0], PS[:, 0, P:P + E0])
                nc.scalar.copy(wt[:, 1, :], PS[:, 0, 2 * P:3 * P])
                nc.scalar.mul(w1[:, 0:2, :].rearrange("p a b -> p (a b)"), PS[:, 1, 0:2 * P], float(HD) ** -0.5)
                nc.scalar.copy(w1[:, 2:4, :].rearrange("p a b -> p (a b)"), PS[:, 1, 2 * P:4 * P])
                nc.scalar.copy(w1[:, 4, :], PS[:, 2, 0:P]).then_inc(SET.cp1, 1)
                act.wait_ge(SET.mm2, 1)
                nc.scalar.copy(wcat[:, 0:2 * P], PS[:, 4, 0:2 * P])
                nc.scalar.copy(wo[:, 0, :, :].rearrange("p a b -> p (a b)"), PS[:, 5, :])
                nc.scalar.copy(wo[:, 1, :, :].rearrange("p a b -> p (a b)"), PS[:, 6, :])
                nc.scalar.copy(bcol[:, 0:4], PS[:, 7, 0:4])
                nc.scalar.mul(bcol[:, 4:5], PS[:, 7, 4:5], float(HD) ** -0.5)
                nc.scalar.copy(bcol[:, 5:6], PS[:, 7, 5:6]).then_inc(ach, 1)
                act.wait_ge(ach, 1)
                nc.scalar.mul(bcol[:, 2:3], bcol[:, 2:3], float(HD) ** -0.5).then_inc(SET.cp2, 1)
                for n in range(2):
                    nc.scalar.copy(w0[:, n, :].rearrange("p (d h) -> p h d", d=HD),
                                   raw0[:, n, :].rearrange("p (h d) -> p h d", d=HD))
                act.wait_ge(SET.sq, 1)
                nc.scalar.activation(cst1[:, 1:2], cst1[:, 0:1], ACT.Sqrt).then_inc(SET.cen, 1)
                act.wait_ge(SET.ctr, 1)
                nc.scalar.copy(r40[:, :], PS[:, 3, 0:NG + NE]).then_inc(ach, 1)
                act.wait_ge(ach, 2)

            def norm(i):
                s = NS
                act.wait_ge(s.var, i + 1)
                nc.scalar.activation(sm[:, 1, :], sm[:, 0, :], ACT.Sqrt).then_inc(s.std, 1)
                for c in range(NCH):
                    act.wait_ge(s.tr, NCH * i + c + 1)
                    nc.scalar.copy(XNT[:, c * CH:c * CH + CH], PS[:, c, :]).then_inc(s.xt, 1)

            def ffn0(i):
                s = FS[i]
                act.wait_ge(s.d, 1)
                nc.scalar.activation(V[:, 1, :], V[:, 0, :], ACT.Exp).then_inc(s.e, 1)

            def attention(i):
                s = AS[i]
                rope = i == 4
                if rope:
                    act.dma_start(COS, cos_d).then_inc(s_tab, 16)
                    act.dma_start(SIN, sin_d).then_inc(s_tab, 16)
                for c in range(NCH):
                    cs = slice(c * CH, c * CH + CH)
                    for n, (w, z) in enumerate(((wk_, t1_), (wq_, t2_))):
                        act.wait_ge(s.sq, 2 * c + n + 1)
                        nc.scalar.activation(z[:, cs], w[:, cs], ACT.Square).then_inc(s.pj2, 1)
                for c in range(NCH):
                    cs = slice(c * CH, c * CH + CH)
                    if rope:
                        act.wait_ge(s.r, c + 1)
                        nc.scalar.activation(t1_[:, cs], t1_[:, cs], ACT.Sqrt).then_inc(s.rt, 1)
                    else:
                        for n, z in enumerate((t1_, t2_)):
                            act.wait_ge(s.n2, 2 * c + n + 1)
                            nc.scalar.activation(z[:, cs], PS[:, NCH * n + c, :], ACT.Sqrt).then_inc(s.rt, 1)
                for n, (w, parts, high) in enumerate(((wk_, KP, 0), (wq_, QP, 2))):
                    for c in range(NCH):
                        cs = slice(c * CH, c * CH + CH)
                        if not rope:
                            act.wait_ge(s.r, 2 * c + n + 1)
                        nc.scalar.copy(parts[:, high, cs], w[:, cs]).then_inc(s.hi, 1)
                for n, (z, parts) in enumerate(((t1_, KP), (t2_, QP))):
                    for c in range(NCH):
                        cs = slice(c * CH, c * CH + CH)
                        act.wait_ge(s.mid, NCH * n + c + 1)
                        nc.scalar.copy(parts[:, 1, cs], z[:, cs]).then_inc(s.o, 1)
                nc.scalar.activation(km[:, 5:6], bcol[:, 7:8], ACT.Exp)
                act.wait_ge(s.parts, 3)
                with act.Fori(0, ITERS // 2) as u:
                    for g in range(2 * CHUNKS):
                        act.wait_ge(s.s, u * (2 * CHUNKS) + (g + 1))
                        nc.scalar.activation(PR[:, g % PRING, :], PS[:, 2 * (g % 2):2 * (g % 2) + 2, :].rearrange("p a b -> p (a b)"),
                                             ACT.Exp).then_inc(s.exp, 1)

            def routed(i):
                s = MS[i]
                act.wait_ge(s.sq, 1)
                nc.scalar.activation(sm[:, 4, :], sm[:, 3, :], ACT.Sqrt).then_inc(s.sr, 1)
                act.wait_ge(s.d, 1)
                nc.scalar.activation(rtt[:, 3, 0:NT * TOPK], gate, ACT.Exp).then_inc(s.e, 1)
                for st_ in range(2 * NCH):
                    c, m = st_ // 2, st_ % 2
                    act.wait_ge(s.gu, st_ + 1)
                    nc.scalar.activation(SH[:, m, c * CH:c * CH + CH], PS[:, 2 * m, :], ACT.Silu).then_inc(s.sh, 1)

                def gates(e):
                    for m in range(2):
                        act.wait_ge(s.gu, e * 2 + (2 * NCH + m + 1))
                        nc.scalar.activation(SIL[:, m, :], PS[:, 2 + 2 * m, 0:CAP], ACT.Silu).then_inc(s.sil, 1)

                stored = 0 if i == 3 else NE // 2

                def take_out(e, b, again):
                    act.wait_ge(s.dn, e + 1)
                    if again is not None:
                        act.wait_ge(SO[b], (again + stored) * (16 * RT))
                    nc.scalar.copy(OB[:, b, 0:RT - 1, :].rearrange("p c d -> p (c d)"), PS[:, 6 + b, 0:(RT - 1) * P])
                    nc.scalar.copy(OB[0:TAIL, b, RT - 1, :], PS[0:TAIL, 6 + b, (RT - 1) * P:RT * P]).then_inc(s.ev, 1)

                gates(0)
                gates(1)
                take_out(0, 0, None)
                gates(2)
                take_out(1, 1, None)
                with act.Fori(1, NE // RING) as u:
                    for r in range(RING):
                        gates(u * RING + (r - 1))
                        take_out(u * RING + (r - 2), r % 2, u * 2 + (r // 2 - 1))
                gates(NE - 1)
                for e in (NE - 2, NE - 1):
                    take_out(e, e % 2, e // 2)

            setup()
            for i in range(stages):
                norm(i)
                if i in FS:
                    ffn0(i)
                elif i in AS:
                    attention(i)
                else:
                    routed(i)

        @block.tensor
        def _(pe):
            def setup():
                pe.wait_ge(s_in, ALL_IN)
                nc.tensor.transpose(PS[:, 0, 0:P], raw[:, 2, :], ident)
                nc.tensor.transpose(PS[:, 0, P:P + E0], cen2[0:E0, :], ident[0:E0, 0:E0])
                nc.tensor.transpose(PS[:, 0, 2 * P:3 * P], raw[:, 7, :], ident)
                nc.tensor.matmul(PS[:, 1, 0:2 * P], raw[:, 4, :], CST[:, C_PERM:C_PERM + 2 * P], start=True, stop=True)
                nc.tensor.matmul(PS[:, 1, 2 * P:4 * P], raw[:, 5, :], CST[:, C_PERM:C_PERM + 2 * P], start=True, stop=True)
                nc.tensor.matmul(PS[:, 2, 0:P], raw[:, 6, :], ident, start=True, stop=True).then_inc(SET.mm1, 1)
                pe.wait_ge(SET.cp1, 1)
                for e in range(2):
                    nc.tensor.matmul(PS[:, 4, P * e:P * e + P], raw[:, e, :], wt[:, 0, :], start=True, stop=True)
                for q in range(QUADS):
                    pad = CST[:, C_PAD + q * P:C_PAD + q * P + P]
                    nc.tensor.matmul(PS[:, 5, P * q:P * q + P], pad, raw[:, 3, :], start=True, stop=True)
                    nc.tensor.matmul(PS[:, 6, P * q:P * q + P], pad, wt[:, 1, :], start=True, stop=True)
                nc.tensor.matmul(PS[:, 7, 0:4], CST[:, C_PERM:C_PERM + P], bcol[:, 0:4], start=True, stop=True)
                last = nc.tensor.matmul(PS[:, 7, 4:6], rotT, bcol[:, 2:4], start=True, stop=True)
                last.then_inc(SET.mm2, 1)
                pe.wait_ge(SET.cn, 1)
                nc.tensor.transpose(PS[:, 3, 0:NG + NE], cen, ident[0:NG + NE, 0:NG + NE]).then_inc(SET.ctr, 1)
                pe.wait_ge(SET.cp2, 1)
                pe.wait_ge(ach, 2)

            def norm(i, XNi):
                s = NS
                for t in range(NT):
                    pe.wait_ge(s.xn, NT * i + t + 1)
                    last = nc.tensor.transpose(PS[:, t // TPC, P * (t % TPC):P * (t % TPC) + P], XNi[:, t, :], ident)
                    if t % TPC == TPC - 1:
                        last.then_inc(s.tr, 1)

            def ffn0(i):
                s, n = FS[i], NS
                for t in range(NT):
                    if t % TPC == 0:
                        pe.wait_ge(n.xt, NCH * i + t // TPC + 1)
                    last = nc.tensor.matmul(PS[:, 4, E0 * t:E0 * t + E0], XNT[:, P * t:P * t + P], wcat[:, 2 * P:],
                                            start=True, stop=True)
                last.then_inc(s.g, 1)
                for t in range(NT):
                    pr = t // 2
                    if t % 2 == 0 and pr >= 3:
                        pe.wait_ge(s.used, pr - 2)
                    last = nc.tensor.matmul(PS[:, 5 + pr % 3, 2 * P * (t % 2):2 * P * (t % 2) + 2 * P],
                                            XNT[:, P * t:P * t + P], wcat[:, 0:2 * P], start=True, stop=True)
                    if t % 2:
                        last.then_inc(s.y, 1)

            def attention(i):
                s, n = AS[i], NS
                rope = i == 4
                w = w1 if rope else w0
                loaded = QUAD_LOADED * (2 if rope else 1)
                pe.wait_ge(n.xt, NCH * i + NCH)
                for c in range(NCH):
                    cs = slice(c * CH, c * CH + CH)
                    b = 4 if c % 2 == 0 else 0
                    if c >= 2:
                        pe.wait_ge(s.used, c - 1)
                    for k in range(4):
                        if rope:
                            last = nc.tensor.matmul(PS[:, b + k, :], w1[:, k, :], XNT[:, cs], start=True, stop=True)
                        elif k % 2 == 0:
                            last = nc.tensor.matmul(PS[:, b + k, :], w0[:, k // 2, :], XNT[:, cs], start=True, stop=True)
                    last.then_inc(s.pj, 1)
                pe.wait_ge(s.used, NCH)
                for c in range(NCH):
                    cs = slice(c * CH, c * CH + CH)
                    for k, z in enumerate((t1_, t2_)):
                        pe.wait_ge(s.pj2, 2 * c + k + 1)
                        nc.tensor.matmul(PS[:, NCH * k + c, :], G, z[:, cs], start=True, stop=True).then_inc(s.n2, 1)
                pe.wait_ge(s.fl, 1)
                if not rope:
                    pe.wait_ge(s.rt, 2 * NCH)
                nc.tensor.transpose(PS[0:1, 0, 0:P], km[:, 7:8], ident).then_inc(s.fm, 1)
                if rope:
                    pe.wait_ge(s.r, NCH)
                pe.wait_ge(s.fl, 2)
                for t in range(NT):
                    last = nc.tensor.matmul(PS[:, t // TPC, P * (t % TPC):P * (t % TPC) + P], XNT[:, P * t:P * t + P],
                                            w[:, 4 if rope else 2, :], start=True, stop=True)
                    if t % TPC == TPC - 1:
                        last.then_inc(s.v, 1)

                def scores(it, g):
                    kt, half = g // 2, g % 2
                    pair = (it // NCH) * 2 + half
                    for k in range(2):
                        j = 2 * half + k
                        last = nc.tensor.matmul(
                            PS[:, 2 * half + k, :],
                            Kt[:, bass.ds(pair, 1), P * kt:P * kt + P].rearrange("p o n -> p (o n)"),
                            Qt[:, bass.ds(it, 1), j, :].rearrange("p o n -> p (o n)"), start=True, stop=True)
                    last.then_inc(s.s, 1)

                def weigh(b, kt, half):
                    for j in range(4):
                        p0 = CH * (j % 2) + half * (CH // 2)
                        last = nc.tensor.matmul(PS[32 * j:32 * j + VW, 4 + 2 * b + half, 0:CH // 2], VQ[:, b, kt, j, :],
                                                PR[:, (b * CHUNKS + 2 * kt + j // 2) % PRING, p0:p0 + CH // 2],
                                                start=(kt == 0), stop=(kt == NT - 1), tile_position=(0, 32 * j))
                    if kt == NT - 1 and half:
                        last.then_inc(s.pv, 1)

                def iteration(it, b, first=False, final=False):
                    for kt in range(NT):
                        for half in range(2):
                            g = 2 * kt + half
                            pe.wait_ge(s.exp, it * CHUNKS + (g + 1))
                            if kt < NT - 1:
                                scores(it, g + 2)
                            elif not final:
                                scores(it + 1, half)
                            if kt == 1 and half == 0:
                                pe.wait_ge(s.vq, it + 1)
                            if kt:
                                weigh(b, kt - 1, half)
                            elif not first:
                                weigh(1 - b, NT - 1, half)
                    if final:
                        for half in range(2):
                            weigh(b, NT - 1, half)

                pe.wait_ge(LQ[0], loaded)
                pe.wait_ge(s.vq, 2)
                with pe.If(bound_is_large(pe, s)):
                    for l in LQ[1:]:
                        pe.wait_ge(l, loaded)
                    with pe.Fori(0, ITERS) as u:
                        for k in range(4 * TPC):
                            j, t = k // TPC, k % TPC
                            pe.wait_ge(s.gm, u * (4 * TPC) + (k + 1))
                            for c in range(NCH):
                                last = nc.tensor.matmul(
                                    PS[:, 4 * (k % 2) + c, :],
                                    Qt[:, bass.ds(u, 1), j, P * t:P * t + P].rearrange("p o n -> p (o n)"),
                                    Kt[:, bass.ds((u // NCH) * 2 + j // 2, 1), CH * c:CH * c + CH].rearrange("p o n -> p (o n)"),
                                    start=True, stop=True)
                            last.then_inc(s.gs, 1)
                    pe.wait_ge(s.gm, MAX_STEPS + 2)
                    for k in range(2):
                        last = nc.tensor.transpose(PS[:, 0, P * k:P * k + P], MX[:, P * k:P * k + P], ident)
                    last.then_inc(s.gs, 1)
                    pe.wait_ge(s.gm, MAX_STEPS + 4)
                    pe.wait_ge(s.gd, 16 * (1 + NH))
                scores(0, 0)
                scores(0, 1)
                iteration(0, 0, first=True)
                iteration(1, 1)
                for l in LQ[1:]:
                    pe.wait_ge(l, loaded)
                with pe.Fori(1, ITERS // 2 - 1) as u:
                    for b in range(2):
                        iteration(2 * u + b, b)
                iteration(ITERS - 2, 0)
                iteration(ITERS - 1, 1, final=True)
                pe.wait_ge(s.at, 1)
                for t in range(NT):
                    for q in range(QUADS):
                        last = nc.tensor.matmul(PS[:, t // TPC, P * (t % TPC):P * (t % TPC) + P],
                                                AT[:, NCH * q + t // TPC, P * (t % TPC):P * (t % TPC) + P],
                                                wo[:, 1 if rope else 0, q, :], start=(q == 0), stop=(q == QUADS - 1))
                    if t % TPC == TPC - 1:
                        last.then_inc(s.vr, 1)

            def routed(i):
                s, n = MS[i], NS
                W = NG + NE
                for t in range(NT):
                    if t % TPC == 0:
                        pe.wait_ge(n.xt, NCH * i + t // TPC + 1)
                    last = nc.tensor.matmul(PS[:, 4 + t // 8, W * (t % 8):W * (t % 8) + W], XNT[:, P * t:P * t + P], r40[:, :],
                                            start=True, stop=True)
                last.then_inc(s.lg, 1)
                pe.wait_ge(s.mk, 1)
                nc.tensor.matmul(PS[:, 6, :], U16[:, 0, :], M16[:, :], start=True, stop=True)
                nc.tensor.matmul(PS[:, 7, :], U16[:, 1, :], M16[:, :], start=True, stop=True).then_inc(s.pfx, 1)
                pe.wait_ge(s.w, 48)
                for st_ in range(2 * NCH):
                    c, m = st_ // 2, st_ % 2
                    if c:
                        pe.wait_ge(s.si, st_ - 1)
                    for k in range(2):
                        last = nc.tensor.matmul(PS[:, 2 * m + k, :], ws[:, k, P * m:P * m + P], XNT[:, c * CH:c * CH + CH],
                                                start=True, stop=True)
                    last.then_inc(s.gu, 1)
                pe.wait_ge(s.slot, 1)
                for t in range(NT):
                    c = t // TPC
                    if t % TPC == 0:
                        pe.wait_ge(s.si, 2 * c + 2)
                        if c >= 2:
                            pe.wait_ge(s.sdu, c - 1)
                    for m in range(2):
                        last = nc.tensor.matmul(PS[:, 6 + c % 2, P * (t % TPC):P * (t % TPC) + P], SH[:, m, P * t:P * t + P],
                                                wsd[:, m, :], start=(m == 0), stop=(m == 1))
                    if t % TPC == TPC - 1:
                        last.then_inc(s.sd, 1)
                pe.wait_ge(s.si, 2 * NCH)
                pe.wait_ge(s.sdu, NCH)

                before = 0 if i == 3 else NE // RING

                def turn(u, r, first):
                    b = r % 2
                    pe.wait_ge(LX[r], (u + before) * 16 + 16)
                    if not first:
                        pe.wait_ge(s.rn, u * RING + r)
                    for c in range(RT):
                        n_ = P if c < RT - 1 else TAIL
                        last = nc.tensor.transpose(PS[:, b, P * c:P * c + n_], XE[0:n_, r, c, 0:P], ident[0:n_, 0:n_])
                    last.then_inc(s.xt, 1)

                def up(e, u, r, first=False):
                    b = r % 2
                    pe.wait_ge(s.rn, e + 2)
                    pe.wait_ge(LW[r], (u + before) * 48 + 48)
                    for m in range(2):
                        if not first:
                            pe.wait_ge(s.h, e * 2 + (m - 1))
                        for k in range(2):
                            last = nc.tensor.matmul(PS[:, 2 + 2 * m + k, 0:CAP], WRING[:, r, HID * k + P * m:HID * k + P * m + P],
                                                    XET[:, b, :], start=True, stop=True)
                        last.then_inc(s.gu, 1)

                def down(e, r, first=False):
                    b = r % 2
                    pe.wait_ge(s.h, e * 2 + 2)
                    if not first:
                        pe.wait_ge(s.ev, e - 1)
                    for c in range(RT):
                        n_ = P if c < RT - 1 else TAIL
                        for m in range(2):
                            last = nc.tensor.matmul(PS[0:n_, 6 + b, P * c:P * c + P], HT[:, b, m, P * c:P * c + n_],
                                                    WRING[:, r, 2 * HID + P * m:2 * HID + P * m + P],
                                                    start=(m == 0), stop=(m == 1))
                    last.then_inc(s.dn, 1)

                for r in range(RING):
                    turn(0, r, r < 2)
                    if r >= 1:
                        up(r - 1, 0, r - 1, first=(r == 1))
                    if r >= 2:
                        down(r - 2, r - 2, first=True)
                with pe.Fori(1, NE // RING) as u:
                    for r in range(RING):
                        turn(u, r, False)
                        up(u * RING + (r - 1), u if r else u - 1, (r - 1) % RING)
                        down(u * RING + (r - 2), (r - 2) % RING)
                up(NE - 1, NE // RING - 1, RING - 1)
                down(NE - 2, RING - 2)
                down(NE - 1, RING - 1)

            setup()
            for i in range(stages):
                norm(i, XNA if i in (1, 4) else XN)
                if i in FS:
                    ffn0(i)
                elif i in AS:
                    attention(i)
                else:
                    routed(i)


_INS = ['L0_attn_x', 'L0_attn_Wq', 'L0_attn_bq', 'L0_attn_Wk', 'L0_attn_bk', 'L0_attn_Wv', 'L0_attn_bv', 'L0_attn_Wo',
        'L0_attn_bo', 'L0_attn_qk_scale', 'L0_ffn_gate_W', 'L0_ffn_expert_W', 'L0_ffn_out_W', 'L1_attn_Wqkv',
        'L1_attn_bqkv', 'L1_attn_Wout', 'L1_attn_bout', 'L1_ffn_group_centroids', 'L1_ffn_expert_centroids',
        'L1_ffn_bias', 'L1_ffn_wg', 'L1_ffn_wu', 'L1_ffn_wd', 'L1_ffn_sg', 'L1_ffn_su', 'L1_ffn_sd']


def kernel(**inputs):
    import concourse.bacc as bacc
    from concourse.bass_utils import run_bass_kernel_spmd

    nc = bacc.Bacc("TRN2", target_bir_lowering=False, num_devices=1)
    arrays = {f"in_{n}_dram": np.ascontiguousarray(inputs[n]) for n in _INS}
    arrays.update(zip(("consts_dram", "cos_dram", "sin_dram"), constants()))
    aps = {n: nc.dram_tensor(n, v.shape, mybir.dt.from_np(v.dtype), kind="ExternalInput").ap()
           for n, v in arrays.items()}
    out = nc.dram_tensor("out_dram", (1, NTOK, P), F32, kind="ExternalOutput").ap()
    build(nc, {n: aps[f"in_{n}_dram"] for n in _INS}, aps["consts_dram"], aps["cos_dram"], aps["sin_dram"], out)
    r = run_bass_kernel_spmd(nc, [arrays], core_ids=[0])
    return r.results[0]["out_dram"]
```

```python
from contextlib import ExitStack
from collections import namedtuple

import numpy as np

import concourse.bass as bass
from concourse import mybir

F32 = mybir.dt.float32
BF16 = mybir.dt.bfloat16
I32 = mybir.dt.int32
U32 = mybir.dt.uint32
ALU = mybir.AluOpType
ACT = mybir.ActivationFunctionType
AX = mybir.AxisListType

P = 128
NTOK = 2048
NT = NTOK // P
CH = 512
NCH = NTOK // CH
TPC = CH // P
LN_EPS = 1e-5

E0 = 8
TOP_P = 0.3

NH = 16
HD = P // NH
QUADS = NH // 4
ITERS = QUADS * NCH
CHUNKS = 2 * NT
VW = HD + 1
PRING = 8
NORM_EPS = 1e-6
RUNS_K = ((0, 3), (0, 2), (0, 1))
RUNS_Q = ((0, 3), (1, 3), (2, 3))
SHIFT_ROW = 6 * HD
Q_ROWS = SHIFT_ROW + 2
BOUND_MAX = 40.0
MAX_STEPS = ITERS * 4 * TPC

NE = 32
NG = 8
TOPG = NG // 2
TOPK = 4
HID = 256
CAP = int(NTOK / NE * TOPK * 1.25)
RT = (CAP + P - 1) // P
BUF = RT * P
ROWS = NE * BUF
TAIL = CAP - (RT - 1) * P
RING = 4
GT = 2
FAR = float(2 * ROWS)
PW = P + 2 * TOPK

C_ID, C_G, C_U, C_ONE, C_SUM, C_SPREAD = 0, 128, 256, 384, 512, 544
C_I8 = C_SPREAD + NCH * P
C_I32 = C_I8 + NG
C_BASE = C_I32 + NE
C_RES = C_BASE + NE
C_DEST = C_RES + NT
C_ROW = C_DEST + NT * TOPK
C_END = C_ROW + RT
S_PERM, S_ROT, S_PAD = 0, 128, 256
S_END = S_PAD + QUADS * P


def row_of(h, d):
    return 4 * HD * (h // 4) + 4 * d + h % 4


def constants():
    c = np.zeros((P, C_END), np.float32)
    s = np.zeros((P, S_END), np.float32)
    i = np.arange(P)
    c[:, C_ID:C_ID + P] = np.eye(P)
    half = HD // 2
    for h in range(NH):
        for d in range(HD):
            m = row_of(h, d)
            s[HD * h + d, S_PERM + m] = 1.0
            s[HD * h + (d + half) % HD, S_ROT + m] = -1.0 if d < half else 1.0
            s[HD * h + d, S_PAD + (h // 4) * P + 32 * (h % 4) + d] = 1.0
    head = 4 * (i // 32) + i % 4
    c[:, C_G:C_G + P] = head[:, None] == head[None, :]
    c[:, C_SUM:C_SUM + 32] = head[:, None] == np.arange(32)[None, :] % NH
    for k in range(NCH):
        c[:, C_SPREAD + k * P:C_SPREAD + k * P + P] = i[:, None] - 32 * k == head[None, :]
    c[:, C_U:C_U + P] = i[:, None] < i[None, :]
    c[:, C_ONE:C_ONE + P] = 1.0
    c[:, C_I8:C_I8 + NG] = np.arange(NG)
    c[:, C_I32:C_I32 + NE] = np.arange(NE)
    c[:, C_BASE:C_BASE + NE] = np.arange(NE) * BUF
    c[:, C_RES:C_RES + NT] = 1.0
    c[:, C_RES] = 0.0
    token = P * np.arange(NT)[None, :, None] + i[:, None, None]
    c[:, C_DEST:C_DEST + NT * TOPK] = (TOPK * token + np.arange(TOPK)).reshape(P, -1)
    c[:, C_ROW:C_ROW + RT] = P * np.arange(RT) + i[:, None]
    inv = (np.float32(1.0) / np.float32(10000.0) ** (np.arange(0, HD, 2, dtype=np.float32) / np.float32(HD)))
    ang = np.outer(np.arange(NTOK, dtype=np.float32), inv.astype(np.float32)).astype(np.float32)
    ang = ang[:, (i % 32) // 4 % half].T
    return c, s, np.ascontiguousarray(np.cos(ang), np.float32), np.ascontiguousarray(np.sin(ang), np.float32)


def build(nc, a, consts_d, setup_d, cos_d, sin_d, out, stages=6):
    ctx = ExitStack()
    assert stages > 0
    with ctx:
        def sb(name, shape, dt=F32):
            return ctx.enter_context(nc.sbuf_tensor(name, shape, dt))

        def sem(name):
            return ctx.enter_context(nc.semaphore(name))

        def sems(prefix, names):
            return namedtuple(prefix, names)(*[sem(f"{prefix}_{n}") for n in names.split()])

        X = sb("X", [P, NT, P])
        XNT = sb("XNT", [P, NTOK])
        Kt = sb("Kt", [P, NH // 2, NTOK], BF16)
        Qt = sb("Qt", [P, ITERS, 4, CH], BF16)
        RA = sb("RA", [P, 8192])
        RB = sb("RB", [P, 8192])
        V = sb("V", [P, NT, P])
        raw0 = V[:, NT - 10:NT - 8, :]
        raw = V[:, NT - 8:NT, :]
        CST = sb("CST", [P, C_END])
        U16 = sb("U16", [P, 2, P], BF16)
        wcat = sb("wcat", [P, 2 * P + E0])
        w0 = sb("w0", [P, 3, P])
        w1 = sb("w1", [P, 5, P])
        wo = sb("wo", [P, 2, QUADS, P])
        wt = sb("wt", [P, 2, P])
        cen = V[0:NG + NE, 3, :]
        cen2 = V[0:NG + NE, 4, :]
        cen_sq = V[0:NG + NE, 5, :]
        cst1 = sb("cst1", [NG + NE, 4])
        r40 = sb("r40", [P, NG + NE])
        bcol = sb("bcol", [P, 8])
        brow = sb("brow", [P, 4, P])
        bexp = sb("bexp", [P, NE])
        st = sb("st", [P, NT, 6])
        mv = sb("mv", [P, NT, 2])
        sm = sb("sm", [P, 8, NT])
        km = sb("km", [P, 12])
        flag = sb("flag", [1, 1], I32)
        PS = ctx.enter_context(nc.psum_tensor("PS", [P, 8, CH], F32))

        RA16 = RA[:, :].bitcast(BF16)
        KP = RA16[:, 0:3 * NTOK].rearrange("p (s n) -> p s n", s=3)
        QP = RA16[:, 3 * NTOK:6 * NTOK].rearrange("p (s n) -> p s n", s=3)
        SHB = RA16[:, 6 * NTOK:7 * NTOK]
        MX = RA[:, 0:MAX_STEPS]
        MXT = RA16[:, 2 * MAX_STEPS:3 * MAX_STEPS].rearrange("p (a n) -> p a n", a=2)
        o = 3 * NTOK // 2
        COS, SIN = RA[:, o:o + NTOK], RA[:, o + NTOK:o + 2 * NTOK]
        AT = RA[:, :].rearrange("p (i n) -> p i n", i=ITERS)
        wq_, wk_, t1_, t2_ = (RB[:, i * NTOK:(i + 1) * NTOK] for i in range(4))
        PR = RB[:, :].rearrange("p (s n) -> p s n", s=PRING)
        VQ = XNT[:, 0:2 * NT * 4 * VW].rearrange("p (b t h w) -> p b t h w", b=2, t=NT, h=4)
        XNA = RB[:, 3 * NTOK:4 * NTOK].rearrange("p (t d) -> p t d", t=NT)
        RS = XNT[:, NTOK - CH:NTOK]

        XNW = RA[:, 0:NT * PW].rearrange("p (t d) -> p t d", t=NT)
        XN = XNW[:, :, 0:P]
        GB = RB[:, :].rearrange("p (j d) -> p j d", j=NT * TOPK)
        o = NT * PW
        SH = RA[:, o:o + 2 * NTOK].rearrange("p (k n) -> p k n", k=2)
        o += 2 * NTOK
        ws = RA[:, o:o + 2 * HID].rearrange("p (k n) -> p k n", k=2)
        o += 2 * HID
        wsd = RA[:, o:o + 2 * P].rearrange("p (k n) -> p k n", k=2)
        WR = V[:, :, :].rearrange("p a b -> p (a b)")
        OH2 = RB[:, 3 * NTOK:4 * NTOK]
        OH = RB[:, 2 * NTOK:3 * NTOK]
        EW = HID * 3
        WRING = RB[:, 0:RING * EW].rearrange("p (r n) -> p r n", r=RING)
        o = RING * EW
        XET = RB[:, o:o + 2 * CAP].rearrange("p (b n) -> p b n", b=2)
        o += 2 * CAP
        XE = RB[:, o:o + RING * RT * PW].rearrange("p (r c d) -> p r c d", r=RING, c=RT)
        o += RING * RT * PW
        HT = RB[:, o:o + 4 * CAP].rearrange("p (b k n) -> p b k n", b=2, k=2)
        o += 4 * CAP
        SIL = RB[:, o:o + 2 * CAP].rearrange("p (k n) -> p k n", k=2)
        o += 2 * CAP
        OB = RB[:, o:o + 2 * BUF].rearrange("p (b c d) -> p b c d", b=2, c=RT)
        assert o + 2 * BUF <= 4 * NTOK
        S40 = WR[:, 0:NT * (NG + NE)].rearrange("p (t e) -> p t e", t=NT)
        MSK = WR[:, 640:1152]
        POS = WR[:, 1152:1664]
        ESC = WR[:, 1664:1664 + P].rearrange("p (t g) -> p t g", t=NT)
        rtt = sb("rtt", [P, 4, P])
        top8 = rtt[:, 0, :].rearrange("p (t k) -> p t k", t=NT)
        idx8 = rtt[:, 1, :].bitcast(U32).rearrange("p (t k) -> p t k", t=NT)
        idxf = rtt[:, 2, :].rearrange("p (t k) -> p t k", t=NT)
        gmk = rtt[:, 3, :].rearrange("p (t g) -> p t g", t=NT)
        gsl = sb("gsl", [P, 3, NT * TOPK])
        gate = gsl[:, 0, :]
        slotf = gsl[:, 1, :]
        srow = gsl[:, 2, :].bitcast(U32)
        M16 = sb("M16", [P, NE * NT], BF16)
        UNUSED = WR[:, 1792:1792 + NE * RT]
        HITS = WR[:, 1888:1888 + NE * RT]
        HIT = sb("HIT", [P, RT, TOPK])
        DST = sb("DST", [P, 2, RT])
        DI = sb("DI", [P, 2, RT], U32)
        XD = nc.dram_tensor("expert_rows", (ROWS, PW), F32, kind="Internal").ap()
        YD = nc.dram_tensor("weighted_terms", (NTOK * TOPK, P), F32, kind="Internal").ap()

        ident = CST[:, C_ID:C_ID + P]
        CS = RB[:, 0:S_END]
        G = CST[:, C_G:C_G + P]

        dram_x = a["L0_attn_x"].rearrange("b (t p) d -> p (b t) d", p=P)
        dram_out = out.rearrange("b (t p) d -> p (b t) d", p=P)
        wqkv_d = a["L1_attn_Wqkv"].rearrange("(s o) d -> o s d", o=P)

        s_first = sem("s_first")
        s_in = sem("s_in")
        s_x = sem("s_x")
        s_tab = sem("s_tab")
        s_out = sem("s_out")
        dch = sem("dch")
        ach = sem("ach")
        s_x_ready = sem("s_x_ready")
        SET = sems("setup", "mm1 cp1 mm2 cp2 centroid_roots squares unit_centroids centroids_turned zero ones onesrow fill")
        NS = sems("n", "var std normalised in_psum turned")
        FS = sems("f", "gates shifted exps products banks_free")
        AS = {i: sems(f"a{i}", "projected squared banks_free squares head_sums roots spread unit high "
                    "inverse rest parts values scores exps v_ready out_ready heads_done middle "
                    "flag flag_row max_scores maxima maxima_in_qt out_steps")
              for i in (1, 4)}

        MS = {i: sems(f"m{i}", "shared_weights logits squares l2_norms rows_taken members counted summed "
                    "shifted exps slots shared_hidden shared_silu shared_down shared_added "
                    "scattered turned gate_up hidden silu down results destinations dest_chain "
                    "go") for i in (3, 5)}
        SK = sem("sk")
        SQ = [sem(f"sq{b}") for b in range(2)]
        LQ = [sem(f"lq{q}") for q in range(QUADS)]
        LX = [sem(f"lx{r}") for r in range(RING)]
        LW = [sem(f"lw{r}") for r in range(RING)]
        SO = [sem(f"so{b}") for b in range(2)]
        GA = [sem(f"ga{g}") for g in range(NT // GT)]

        block = ctx.enter_context(nc.Block())

        first_loads = [
            (CST[:, :], consts_d),
            (raw[:, 2, :], a["L0_ffn_out_W"]),
            (cen2[0:E0, :], a["L0_ffn_gate_W"]),
            (raw[:, 0:2, :], a["L0_ffn_expert_W"][0:2].rearrange("e h d -> h e d")),
        ]
        loads = [
            (CS[:, :], setup_d),
            (raw[:, 3, :], a["L0_attn_Wo"]),
            (raw[:, 4:7, :], wqkv_d),
            (raw[:, 7, :], a["L1_attn_Wout"]),
            (raw0[:, 0, :], a["L0_attn_Wq"]),
            (raw0[:, 1, :], a["L0_attn_Wk"]),
            (w0[:, 2, :], a["L0_attn_Wv"]),
            (cen[0:NG, :], a["L1_ffn_group_centroids"]),
            (cen[NG:NG + NE, :], a["L1_ffn_expert_centroids"]),
            (bcol[:, 0:1], a["L0_attn_bq"].rearrange("(p o) -> p o", o=1)),
            (bcol[:, 1:2], a["L0_attn_bk"].rearrange("(p o) -> p o", o=1)),
            (bcol[:, 2:3], a["L1_attn_bqkv"][0:P].rearrange("(p o) -> p o", o=1)),
            (bcol[:, 3:4], a["L1_attn_bqkv"][P:2 * P].rearrange("(p o) -> p o", o=1)),
            (bcol[:, 6:7], a["L0_attn_qk_scale"].rearrange("a b c d -> (a b c) d").to_broadcast([P, 1])),
            (brow[:, 0, :], a["L0_attn_bv"].rearrange("(o d) -> o d", o=1).to_broadcast([P, P])),
            (brow[:, 1, :], a["L0_attn_bo"].rearrange("(o d) -> o d", o=1).to_broadcast([P, P])),
            (brow[:, 2, :], a["L1_attn_bqkv"][2 * P:3 * P].rearrange("(o d) -> o d", o=1).to_broadcast([P, P])),
            (brow[:, 3, :], a["L1_attn_bout"].rearrange("(o d) -> o d", o=1).to_broadcast([P, P])),
            (bexp[:, :], a["L1_ffn_bias"].rearrange("(o d) -> o d", o=1).to_broadcast([P, NE])),
        ]
        FIRST_IN = 16 * len(first_loads)
        ALL_IN = 16 * len(loads)

        KD = nc.dram_tensor("k_parts", (QUADS, SHIFT_ROW, 4, NTOK), BF16, kind="Internal").ap()
        QD = nc.dram_tensor("q_parts", (QUADS, Q_ROWS, 4, NTOK), BF16, kind="Internal").ap()
        MD = nc.dram_tensor("maxima", (MAX_STEPS, P), BF16, kind="Internal").ap()

        def attention_loads(eng, s, k_done, before):
            def write(q, parts, dram, runs, done):
                row = 0
                for lo, hi in runs:
                    n = hi - lo
                    eng.dma_start(dram[q, row:row + HD * n].rearrange("(s d) j n -> (d j) s n", s=n),
                                  parts[32 * q:32 * q + 32, lo:hi, :]).then_inc(done, 16)
                    row += HD * n

            def write_q(q):
                write(q, QP, QD, RUNS_Q, SQ[q % 2])
                eng.dma_start(QD[q, SHIFT_ROW], SHB[32 * q:32 * q + 4, :]).then_inc(SQ[q % 2], 16)

            def read_k(q):
                for j in range(4):
                    r0 = 64 * (j % 2)
                    eng.dma_start(Kt[r0:r0 + SHIFT_ROW, 2 * q + j // 2, :], KD[q, :, j, :]).then_inc(LQ[q], 16)

            def read_q(q):
                eng.wait_ge(SQ[q % 2], 64 * (q // 2 + 1) + 128 * before)
                for j in range(4):
                    r0 = 64 * (j % 2)
                    eng.dma_start(Qt[r0:r0 + Q_ROWS, NCH * q:NCH * q + NCH, j, :],
                                  QD[q, :, j, :].rearrange("r (c n) -> r c n", c=NCH)).then_inc(LQ[q], 16)

            eng.wait_ge(s.parts, k_done)
            for q in range(QUADS):
                write(q, KP, KD, RUNS_K, SK)
            eng.wait_ge(s.parts, 3)
            write_q(0)
            eng.wait_ge(SK, 16 * 3 * QUADS * (before + 1))
            read_k(0)
            read_q(0)
            write_q(1)
            write_q(2)
            for q in range(1, QUADS):
                read_k(q)
                read_q(q)
                if q + 2 < QUADS:
                    write_q(q + 2)

        QUAD_LOADED = 16 * 4 * 2

        def bound_is_large(eng, s):
            eng.wait_ge(s.flag, 2)
            return eng.value_load(flag[0:1, 0:1], min_val=0, max_val=1) > 0

        def maximum_loads(eng, s):
            with eng.If(bound_is_large(eng, s)):
                eng.wait_ge(s.maxima, MAX_STEPS + 3)
                eng.dma_start(MD.rearrange("(a r) p -> r a p", a=2), MXT).then_inc(s.maxima_in_qt, 16)
                eng.wait_ge(s.maxima_in_qt, 16)
                rows = MD.rearrange("(q c j t) p -> q j c (t p)", q=QUADS, c=NCH, j=4)
                for q in range(QUADS):
                    for j in range(4):
                        r = 64 * (j % 2) + SHIFT_ROW + 1
                        eng.dma_start(Qt[r:r + 1, NCH * q:NCH * q + NCH, j, :], rows[q, j].unsqueeze(0)).then_inc(s.maxima_in_qt, 16)
                eng.wait_ge(s.maxima_in_qt, 16 * (1 + NH))

        @block.sync
        def _(sp):
            def routed_dmas(i):
                s = MS[i]
                sp.wait_ge(NS.normalised, NT * i + 1)
                sp.dma_start(ws[:, 0, :], a["L1_ffn_sg"]).then_inc(s.shared_weights, 16)
                sp.dma_start(ws[:, 1, :], a["L1_ffn_su"]).then_inc(s.shared_weights, 16)
                sp.dma_start(wsd, a["L1_ffn_sd"].rearrange("(k p) d -> p k d", p=P)).then_inc(s.shared_weights, 16)

                def load_weights(e, r):
                    one = bass.ds(e, 1)
                    sp.dma_start(WRING[:, r, 0:HID], a["L1_ffn_wg"][one].rearrange("e d h -> d (e h)")).then_inc(LW[r], 16)
                    sp.dma_start(WRING[:, r, HID:2 * HID], a["L1_ffn_wu"][one].rearrange("e d h -> d (e h)")).then_inc(LW[r], 16)
                    sp.dma_start(WRING[:, r, 2 * HID:3 * HID].rearrange("p (k d) -> p k d", k=2),
                                 a["L1_ffn_wd"][one].rearrange("e (k p) d -> p (e k) d", p=P)).then_inc(LW[r], 16)

                def load_rows(e, r):
                    sp.dma_start(XE[:, r, :, :], XD[bass.ds(e * BUF, BUF)].rearrange("(c p) d -> p c d", p=P)
                                 ).then_inc(LX[r], 16)

                for r in range(RING):
                    load_weights(r, r)
                turns = 1 if i == 3 else 2
                sp.wait_ge(s.scattered, 16 * NT * TOPK)
                for r in range(RING):
                    load_rows(r, r)
                with sp.Fori(0, NE // RING - 1) as u:
                    for r in range(RING):
                        e = u * RING + r
                        sp.wait_ge(s.down, e + 1)
                        sp.wait_ge(s.destinations, e + 1)
                        load_weights(e + RING, r)
                        load_rows(e + RING, r)
                for b in range(2):
                    sp.wait_ge(SO[b], 16 * RT * NE // 2 * turns)
                sp.wait_ge(s.hidden, 2 * NE)
                sp.wait_ge(s.down, NE)
                sp.wait_ge(s.destinations, NE)
                for g in range(NT // GT):
                    n = TOPK * GT
                    sp.dma_start(GB[:, n * g:n * (g + 1), :].rearrange("p (t k) d -> p t (k d)", t=GT),
                                 YD[n * P * g:n * P * (g + 1)].rearrange("(t p k) d -> p t (k d)", t=GT, k=TOPK)
                                 ).then_inc(GA[g], 16)

            for c in range(NCH):
                sp.dma_start(X[:, TPC * c:TPC * c + TPC, :], dram_x[:, TPC * c:TPC * c + TPC, :]).then_inc(s_x, 16)
            for dst, src in first_loads:
                sp.dma_start(dst, src).then_inc(s_first, 16)
            for dst, src in loads:
                sp.dma_start(dst, src).then_inc(s_in, 16)
            sp.wait_ge(SET.zero, 2)
            sp.wait_ge(SET.ones, 1)
            for r in (SHIFT_ROW, 64 + SHIFT_ROW):
                for pair in range(NH // 2):
                    sp.dma_start(Kt[r:r + 2, pair, :], SHB[0:2, :]).then_inc(SET.onesrow, 16)
            sp.dma_start(QD[:, SHIFT_ROW + 1:Q_ROWS].rearrange("q o j n -> o q (j n)"),
                         Qt[0:1, :, :, :].rearrange("p (q c) j n -> p q (c j n)", q=QUADS)).then_inc(SET.onesrow, 16)
            zeros = Qt[:, :, :, :].rearrange("p i h n -> p (i h n)").bitcast(F32)
            sp.dma_start(XD.rearrange("(p r) d -> p (r d)", p=P),
                         zeros[:, 0:ROWS // P * PW]).then_inc(SET.fill, 16)
            sp.dma_start(YD.rearrange("(p r) d -> p (r d)", p=P), zeros[:, 0:NTOK * TOPK]).then_inc(SET.fill, 16)
            sp.wait_ge(SET.onesrow, 16 * (NH + 1))
            sp.wait_ge(SET.fill, 32)
            for i in range(stages):
                if i in AS:
                    attention_loads(sp, AS[i], *((1, 1) if i == 4 else (2, 0)))
                    maximum_loads(sp, AS[i])
                if i in MS:
                    routed_dmas(i)
            for c in range(NCH):
                if stages - 1 in MS:
                    sp.wait_ge(MS[stages - 1].summed, TPC // GT * (c + 1))
                else:
                    sp.wait_ge(s_x_ready, stages)
                sp.dma_start(dram_out[:, TPC * c:TPC * c + TPC, :], X[:, TPC * c:TPC * c + TPC, :]).then_inc(s_out, 16)
            sp.wait_ge(s_out, 16 * NCH)

        @block.gpsimd
        def _(pool):
            nc.gpsimd.memset(SHB, 1.0).then_inc(SET.ones, 1)
            nc.gpsimd.memset(Kt[:, :, :].rearrange("p h n -> p (h n)").bitcast(F32), 0.0).then_inc(SET.zero, 1)
            nc.gpsimd.memset(Qt[:, :, :, :].rearrange("p i h n -> p (i h n)").bitcast(F32), 0.0).then_inc(SET.zero, 1)
            for i in range(stages):
                if i not in MS:
                    continue
                s = MS[i]
                pool.wait_ge(s.slots, 1)
                if i == 3:
                    pool.wait_ge(SET.fill, 32)
                for j in range(NT * TOPK):
                    if j == NT * TOPK // 2:
                        pool.wait_ge(s.slots, 2)
                    nc.gpsimd.indirect_dma_start(XD, bass.IndirectOffsetOnAxis(srow[:, j:j + 1], 0), XNW[:, j // TOPK, :],
                                                 None, bounds_check=ROWS - 1, oob_is_err=False).then_inc(s.scattered, 16)
                with pool.Fori(0, NE // 2) as u:
                    for b in range(2):
                        pool.wait_ge(s.destinations, 2 * u + (b + 1))
                        pool.wait_ge(s.results, 2 * u + (b + 1))
                        pool.sem_inc(s.go, 1)
                        for c in range(RT):
                            n_ = P if c < RT - 1 else TAIL
                            nc.gpsimd.indirect_dma_start(
                                YD, bass.IndirectOffsetOnAxis(DI[0:n_, b, c:c + 1], 0), OB[0:n_, b, c, :], None,
                                bounds_check=NTOK * TOPK - 1, oob_is_err=False).then_inc(SO[b], 16)

        @block.vector
        def _(dve):
            count = [0]

            def link(ins):
                count[0] += 1
                ins.then_inc(dch, 1)
                dve.wait_ge(dch, count[0])

            def setup():
                dve.wait_ge(s_first, FIRST_IN)
                dve.wait_ge(s_in, ALL_IN)
                nc.vector.tensor_copy(U16[:, 0, :], CST[:, C_U:C_U + P])
                nc.vector.tensor_copy(U16[:, 1, :], CST[:, C_ONE:C_ONE + P])
                link(nc.vector.tensor_scalar(bcol[:, 7:8], bcol[:, 6:7], -1.0, None, ALU.mult))
                link(nc.vector.tensor_tensor(bcol[:, 7:8], bcol[:, 7:8], bcol[:, 6:7], ALU.min))
                link(nc.vector.tensor_tensor(cen_sq, cen, cen, ALU.mult))
                nc.vector.tensor_reduce(cst1[:, 0:1], cen_sq, AX.X, ALU.add).then_inc(SET.squares, 1)
                dve.wait_ge(SET.centroid_roots, 1)
                link(nc.vector.tensor_scalar(cst1[:, 2:3], cst1[:, 1:2], 1e-12, None, ALU.max))
                link(nc.vector.reciprocal(cst1[:, 3:4], cst1[:, 2:3]))
                nc.vector.tensor_scalar(cen, cen, cst1[:, 3:4], None, ALU.mult).then_inc(SET.unit_centroids, 1)

            def norm(i, XNi):
                s = NS
                if i == 0:
                    dve.wait_ge(s_x, 16 * NCH)
                for t in range(NT):
                    last = nc.vector.bn_stats(st[:, t, :], X[:, t, :])
                link(last)
                for t in range(NT):
                    last = nc.vector.bn_aggr(mv[:, t, :], st[:, t, :])
                link(last)
                nc.vector.tensor_scalar(sm[:, 0, :], mv[:, :, 1], LN_EPS, None, ALU.add).then_inc(s.var, 1)
                dve.wait_ge(s.std, i + 1)
                link(nc.vector.reciprocal(sm[:, 2, :], sm[:, 1, :]))
                if i in MS:
                    link(nc.vector.scalar_tensor_tensor(out=sm[:, 3, :], in0=mv[:, :, 1], scalar=float(P), in1=sm[:, 2, :],
                                                        op0=ALU.mult, op1=ALU.mult))
                    nc.vector.tensor_tensor(sm[:, 3, :], sm[:, 3, :], sm[:, 2, :], ALU.mult).then_inc(MS[i].squares, 1)
                for t in range(NT):
                    nc.vector.tensor_scalar(XNi[:, t, :], X[:, t, :], mv[:, t, 0:1], sm[:, 2, t:t + 1],
                                            ALU.subtract, ALU.mult).then_inc(s.normalised, 1)

            def ffn0(i):
                s, done = FS, i // 2
                lg = PS[:, 4, 0:NT * E0].rearrange("p (t e) -> p t e", e=E0)
                ge = V[:, 0, :].rearrange("p (t e) -> p t e", e=E0)
                pp = V[:, 1, :].rearrange("p (t e) -> p t e", e=E0)
                ov = V[:, 2, :].rearrange("p (t e) -> p t e", e=E0)
                dve.wait_ge(s.gates, done + 1)
                link(nc.vector.tensor_reduce(sm[:, 3, :], lg, AX.X, ALU.max))
                nc.vector.tensor_tensor(ge, lg, sm[:, 3, :].unsqueeze(2).to_broadcast([P, NT, E0]),
                                        ALU.subtract).then_inc(s.shifted, 1)
                dve.wait_ge(s.exps, done + 1)
                link(nc.vector.tensor_reduce(sm[:, 4, :], pp, AX.X, ALU.add))
                link(nc.vector.reciprocal(sm[:, 5, :], sm[:, 4, :]))
                link(nc.vector.tensor_tensor(ge, pp, sm[:, 5, :].unsqueeze(2).to_broadcast([P, NT, E0]), ALU.mult))
                link(nc.vector.tensor_scalar(ov, ge, TOP_P, None, ALU.is_gt))
                link(nc.vector.tensor_reduce(sm[:, 6, :], ov, AX.X, ALU.add))
                nc.vector.tensor_scalar(sm[:, 7, :], sm[:, 6, :], -0.5, 0.5 * E0, ALU.mult, ALU.add)
                link(nc.vector.scalar_tensor_tensor(out=sm[:, 4, :], in0=sm[:, 6, :], scalar=0.5,
                                                    in1=ge[:, :, 1], op0=ALU.mult, op1=ALU.mult))
                link(nc.vector.tensor_tensor(sm[:, 3, :], sm[:, 7, :], ge[:, :, 0], ALU.mult))
                for pr in range(NT // 2):
                    dve.wait_ge(s.products, done * (NT // 2) + pr + 1)
                    b = 5 + pr % 3
                    for e in range(2):
                        for k in range(2):
                            t = 2 * pr + k
                            last = nc.vector.scalar_tensor_tensor(
                                out=X[:, t, :], in0=PS[:, b, 2 * P * k + P * e:2 * P * k + P * e + P],
                                scalar=sm[:, 3 + e, t:t + 1], in1=X[:, t, :], op0=ALU.mult, op1=ALU.add)
                        if e == 0:
                            link(last)
                    last.then_inc(s.banks_free, 1)
                dve.wait_ge(s.banks_free, (done + 1) * (NT // 2))
                nc.vector.tensor_copy(sm[:, 5, 0:1], sm[:, 3, 0:1]).then_inc(s_x_ready, 1)

            def set_flag(s, a, b):
                nc.vector.tensor_tensor(km[:, 7:8], a, b, ALU.mult).then_inc(s.flag, 1)
                dve.wait_ge(s.flag_row, 1)
                link(nc.vector.tensor_reduce(km[0:1, 6:7], PS[0:1, 0, 0:P], AX.X, ALU.max))
                nc.vector.tensor_scalar(flag[:, :], km[0:1, 6:7], BOUND_MAX ** 2, None, ALU.is_gt).then_inc(s.flag, 1)

            def exact_maximum(s):
                with dve.If(bound_is_large(dve, s)):
                    nc.vector.tensor_copy(km[:, 6:7], km[:, 7:8]).then_inc(s.maxima, 2)
                    with dve.Fori(0, ITERS) as u:
                        for k in range(4 * TPC):
                            b = 4 * (k % 2)
                            dve.wait_ge(s.max_scores, u * (4 * TPC) + (k + 1))
                            nc.vector.tensor_reduce(MX[:, bass.ds(u * (4 * TPC) + k, 1)], PS[:, b:b + 4, :],
                                                    AX.XY, ALU.max).then_inc(s.maxima, 1)
                    dve.wait_ge(s.max_scores, MAX_STEPS + 1)
                    nc.vector.tensor_scalar(MXT, PS[:, 0, 0:MAX_STEPS].rearrange("p (a n) -> p a n", a=2), -1.0, None,
                                            ALU.mult).then_inc(s.maxima, 1)
                    nc.vector.memset(PS[:, 4:8, :].rearrange("p a b -> p (a b)"), 0.0).then_inc(s.maxima, 1)

            def attention(i):
                s = AS[i]
                rope = i == 4
                if rope:
                    dve.wait_ge(s_tab, 32)
                else:
                    dve.wait_ge(SET.onesrow, 16 * (NH + 1))
                    nc.vector.tensor_scalar(SHB[:, :], X[:, :, :].rearrange("p t d -> p (t d)"), 0.0, bcol[:, 7:8],
                                            ALU.mult, ALU.add).then_inc(s.parts, 1)

                def project(n):
                    k_side, c = n < NCH, n % NCH
                    w, z = (wk_, t1_) if k_side else (wq_, t2_)
                    cs = slice(c * CH, c * CH + CH)
                    dve.wait_ge(s.projected, n + 1)
                    if rope:
                        zb = 3 if k_side else 2
                        nc.vector.scalar_tensor_tensor(out=w[:, cs], in0=PS[:, 2 * c, :], scalar=bcol[:, zb:zb + 1],
                                                       in1=COS[:, cs], op0=ALU.add, op1=ALU.mult)
                        nc.vector.scalar_tensor_tensor(out=z[:, cs], in0=PS[:, 2 * c + 1, :], scalar=bcol[:, zb + 2:zb + 3],
                                                       in1=SIN[:, cs], op0=ALU.add, op1=ALU.mult).then_inc(s.banks_free, 1)
                        dve.wait_ge(s.banks_free, n + 1)
                        nc.vector.tensor_tensor(w[:, cs], w[:, cs], z[:, cs], ALU.add).then_inc(s.squares, 1)
                    else:
                        b = 1 if k_side else 0
                        nc.vector.tensor_scalar(w[:, cs], PS[:, n, :], bcol[:, b:b + 1], None, ALU.add).then_inc(s.squares, 1)

                def inverse(n):
                    z = (t1_, t2_)[n]
                    dve.wait_ge(s.roots, n + 1)
                    link(nc.vector.tensor_scalar(z[:, 0:CH], z[:, 0:CH], NORM_EPS, None, ALU.add))
                    nc.vector.reciprocal(z[:, 0:CH], z[:, 0:CH]).then_inc(s.inverse, 1)

                def unit(n):
                    w = wk_ if n < NCH else wq_
                    cs = slice(n % NCH * CH, n % NCH * CH + CH)
                    dve.wait_ge(s.spread, n + 1)
                    if n < NCH:
                        nc.vector.tensor_tensor(w[:, cs], w[:, cs], PS[:, NCH + n, :], ALU.mult).then_inc(s.unit, 1)
                    else:
                        nc.vector.scalar_tensor_tensor(out=w[:, cs], in0=w[:, cs], scalar=bcol[:, 6:7],
                                                       in1=PS[:, n - NCH, :], op0=ALU.mult, op1=ALU.mult).then_inc(s.unit, 1)

                def split(side):
                    w, high, mid, low = ((wk_, KP[:, 0, :], KP[:, 1, :], KP[:, 2, :]) if side[0] == 0
                                         else (wq_, QP[:, 2, :], QP[:, 1, :], QP[:, 0, :]))
                    for n in side:
                        cs = slice(n % NCH * CH, n % NCH * CH + CH)
                        dve.wait_ge(s.high, n + 1)
                        if rope:
                            dve.wait_ge(s.squared, n + 1)
                        nc.vector.tensor_tensor(w[:, cs], w[:, cs], high[:, cs], ALU.subtract).then_inc(s.rest, 1)
                    for n in side:
                        cs = slice(n % NCH * CH, n % NCH * CH + CH)
                        dve.wait_ge(s.middle, n + 1)
                        last = nc.vector.tensor_tensor(low[:, cs], w[:, cs], mid[:, cs], ALU.subtract)
                    last.then_inc(s.parts, 1)

                KC, QC = range(NCH), range(NCH, 2 * NCH)
                if rope:
                    for n in KC:
                        project(n)
                    split(KC)
                    for n in QC:
                        project(n)
                    dve.wait_ge(s.head_sums, 2 * NCH)
                    for c in range(NCH):
                        nc.vector.tensor_reduce(km[:, c:c + 1], PS[:, c, :], AX.X, ALU.max)
                        last = nc.vector.tensor_reduce(km[:, 8 + c:9 + c], PS[:, NCH + c, :], AX.X, ALU.max)
                    link(last)
                    nc.vector.tensor_reduce(km[:, 4:5], km[:, 0:NCH], AX.X, ALU.max)
                    link(nc.vector.tensor_reduce(km[:, 6:7], km[:, 8:8 + NCH], AX.X, ALU.max))
                    for c in range(NCH):
                        cs = slice(c * CH, c * CH + CH)
                        nc.vector.tensor_scalar(t1_[:, cs], PS[:, NCH + c, :], km[:, 4:5], None, ALU.mult).then_inc(s.inverse, 1)
                    set_flag(s, km[:, 4:5], km[:, 6:7])
                    for c in range(NCH):
                        cs = slice(c * CH, c * CH + CH)
                        dve.wait_ge(s.roots, c + 1)
                        last = nc.vector.tensor_scalar(SHB[:, cs], t1_[:, cs], -1.0, None, ALU.mult)
                    last.then_inc(s.parts, 1)
                    split(QC)
                else:
                    for n in (*KC, *QC):
                        project(n)
                    inverse(0)
                    for n in KC:
                        unit(n)
                    inverse(1)
                    split(KC)
                    for n in QC:
                        unit(n)
                    split(QC)
                    set_flag(s, bcol[:, 7:8], bcol[:, 7:8])
                for c in range(NCH):
                    dve.wait_ge(s.values, c + 1)
                    last = nc.vector.tensor_tensor(
                        V[:, TPC * c:TPC * c + TPC, :], PS[:, c, :].rearrange("p (t d) -> p t d", t=TPC),
                        brow[:, 2 * (i == 4), :].unsqueeze(1).to_broadcast([P, TPC, P]), ALU.add)
                link(last)
                nc.vector.memset(PS[:, 4:8, :].rearrange("p a b -> p (a b)"), 0.0)
                nc.vector.memset(VQ[:, :, :, :, HD:VW].rearrange("p b t h w -> p (b t h) w"), 1.0)
                V4 = V[:, :, :].rearrange("p t (q h w) -> p t q h w", q=QUADS, h=4)
                for b in range(2):
                    nc.vector.tensor_copy(VQ[:, b, :, :, 0:HD], V4[:, :, 0, :, :]).then_inc(s.v_ready, 1)
                nc.vector.tensor_tensor(X[:, :, :], X[:, :, :],
                                        brow[:, 1 + 2 * (i == 4), :].unsqueeze(1).to_broadcast([P, NT, P]), ALU.add)
                for written in SQ:
                    dve.wait_ge(written, 64 * QUADS // 2 * (2 if rope else 1))
                exact_maximum(s)
                oc = s.out_steps

                def step(it, b, more):
                    dve.wait_ge(s.out_ready, it + 1)
                    at = AT[:, bass.ds(it, 1), :].rearrange("p o n -> p (o n)")
                    got = PS[:, 4 + 2 * b:6 + 2 * b, 0:CH // 2]
                    nc.vector.tensor_copy(at.rearrange("p (a n) -> p a n", a=2), got).then_inc(oc, 1)
                    for half in range(2):
                        last = nc.vector.stream_shuffle(RS[:, half * CH // 2:(half + 1) * CH // 2], got[:, half, :], [HD] * 32)
                    last.then_inc(oc, 1)
                    if more:
                        nc.vector.tensor_copy(VQ[:, b, :, :, 0:HD], V[:, :, bass.ds(vcol(it), 4 * HD)].rearrange(
                            "p t (h w) -> p t h w", h=4)).then_inc(s.v_ready, 1)
                    dve.wait_ge(oc, it * 4 + 2)
                    nc.vector.reciprocal(RS, RS).then_inc(oc, 1)
                    dve.wait_ge(oc, it * 4 + 3)
                    nc.vector.tensor_tensor(at, at, RS, ALU.mult).then_inc(oc, 1)
                    dve.wait_ge(oc, it * 4 + 4)

                def vcol(it):
                    return ((it + 2) // NCH) * (4 * HD)

                with dve.Fori(0, ITERS // 2 - 1) as u:
                    for b in range(2):
                        step(2 * u + b, b, True)
                for b in range(2):
                    step(ITERS - 2 + b, b, False)
                nc.vector.tensor_copy(km[:, 7:8], AT[:, ITERS - 1, 0:1]).then_inc(s.heads_done, 1)
                for c in range(NCH):
                    dve.wait_ge(s.values, NCH + c + 1)
                    last = nc.vector.tensor_tensor(X[:, TPC * c:TPC * c + TPC, :], X[:, TPC * c:TPC * c + TPC, :],
                                                   PS[:, c, :].rearrange("p (t d) -> p t d", t=TPC), ALU.add)
                link(last)
                nc.vector.tensor_copy(km[:, 6:7], X[:, 0, 0:1]).then_inc(s_x_ready, 1)

            def routed(i):
                s = MS[i]
                nc.vector.tensor_copy(XNW[:, :, P + TOPK:PW], CST[:, C_DEST:C_DEST + NT * TOPK].rearrange("p (t k) -> p t k", t=NT))
                dve.wait_ge(s.l2_norms, 1)
                link(nc.vector.tensor_scalar(sm[:, 5, :], sm[:, 4, :], 1e-12, None, ALU.max))
                link(nc.vector.reciprocal(sm[:, 6, :], sm[:, 5, :]))
                W = NG + NE
                HN = NT // 2
                iota8 = CST[:, C_I8:C_I8 + NG]
                iota32 = CST[:, C_I32:C_I32 + NE]
                cnt = [UNUSED[:, NE * k:NE * k + NE] for k in range(2)]

                def route(h):
                    ts_ = slice(HN * h, HN * h + HN)
                    part = slice(HN * NE * h, HN * NE * (h + 1))
                    sc, tp, ix, ixf, gm = S40[:, ts_, :], top8[:, ts_, :], idx8[:, ts_, :], idxf[:, ts_, :], gmk[:, ts_, :]

                    def top(values):
                        for t in range(HN):
                            last = nc.vector.max(tp[:, t, :], values[:, t, :])
                        link(last)
                        for t in range(HN):
                            last = nc.vector.max_index(ix[:, t, :], tp[:, t, :], values[:, t, :])
                        link(last)
                        link(nc.vector.tensor_copy(ixf, ix))

                    def one_hot(dst, width, iota):
                        shape = [P, HN, TOPK, width]
                        link(nc.vector.tensor_tensor(dst, iota.unsqueeze(1).unsqueeze(1).to_broadcast(shape),
                                                     ixf[:, :, 0:TOPK].unsqueeze(3).to_broadcast(shape), ALU.is_equal))

                    link(nc.vector.tensor_tensor(sc, PS[:, 4 + h, 0:HN * W].rearrange("p (t e) -> p t e", t=HN),
                                                 sm[:, 6, ts_].unsqueeze(2).to_broadcast([P, HN, W]), ALU.mult))
                    top(sc[:, :, 0:NG])
                    ohg = OH2[:, 0:HN * TOPG * NG].rearrange("p (t k g) -> p t k g", t=HN, k=TOPG)
                    one_hot(ohg, NG, iota8)
                    link(nc.vector.tensor_reduce(gm, ohg.rearrange("p t k g -> p t g k"), AX.X, ALU.add))
                    es = MSK[:, part].rearrange("p (t e) -> p t e", t=HN)
                    link(nc.vector.tensor_tensor(es, sc[:, :, NG:W], bexp[:, :].unsqueeze(1).to_broadcast([P, HN, NE]), ALU.add))
                    esg = MSK[:, part].rearrange("p (t g e) -> p t g e", t=HN, g=NG)
                    gb = [P, HN, NG, NE // NG]
                    nc.vector.tensor_scalar(ESC[:, ts_, :], gm, -1.0, 1e9, ALU.add, ALU.mult)
                    link(nc.vector.tensor_tensor(esg, esg, gm.unsqueeze(3).to_broadcast(gb), ALU.mult))
                    link(nc.vector.tensor_tensor(esg, esg, ESC[:, ts_, :].unsqueeze(3).to_broadcast(gb), ALU.add))
                    top(es)
                    nc.vector.tensor_copy(XNW[:, ts_, P:P + TOPK], ixf[:, :, 0:TOPK])
                    oh = OH[:, TOPK * HN * NE * h:TOPK * HN * NE * (h + 1)].rearrange("p (t k e) -> p t k e", t=HN, k=TOPK)
                    one_hot(oh, NE, iota32)
                    with nc.allow_low_precision("zeros and ones"):
                        nc.vector.tensor_reduce(M16[:, part].rearrange("p (e t) -> p e t", e=NE), oh.rearrange("p t k e -> p e t k"),
                                                AX.X, ALU.add).then_inc(s.members, 1)
                    reset = OH2[:, 0:HN * NE]
                    link(nc.vector.tensor_copy(reset.rearrange("p (e t) -> p e t", e=NE),
                                               CST[:, C_RES:C_RES + HN].unsqueeze(1).to_broadcast([P, NE, HN])))
                    dve.wait_ge(s.counted, h + 1)
                    pos = POS[:, part]
                    p3 = pos.rearrange("p (e t) -> p e t", e=NE)
                    tile_sums, prefix = PS[:, 7, part], PS[:, 6, part]
                    link(nc.vector.tensor_tensor_scan(pos, reset, tile_sums, 0.0, ALU.mult, ALU.add))
                    if h == 0:
                        link(nc.vector.tensor_copy(cnt[0], p3[:, :, HN - 1]))
                    else:
                        link(nc.vector.tensor_tensor(cnt[1], cnt[0], p3[:, :, HN - 1], ALU.add))
                    link(nc.vector.tensor_tensor(pos, pos, tile_sums, ALU.subtract))
                    link(nc.vector.tensor_tensor(pos, pos, prefix, ALU.add))
                    if h:
                        link(nc.vector.tensor_tensor(p3, p3, cnt[0].unsqueeze(2).to_broadcast([P, NE, HN]), ALU.add))
                    link(nc.vector.tensor_scalar(MSK[:, part], pos, float(CAP), FAR, ALU.is_ge, ALU.mult))
                    link(nc.vector.tensor_tensor(p3, p3, CST[:, C_BASE:C_BASE + NE].unsqueeze(2).to_broadcast([P, NE, HN]), ALU.add))
                    link(nc.vector.tensor_tensor(pos, pos, MSK[:, part], ALU.add))
                    oh2 = OH2[:, TOPK * HN * NE * h:TOPK * HN * NE * (h + 1)].rearrange("p (t k e) -> p t k e", t=HN, k=TOPK)
                    link(nc.vector.tensor_tensor(oh2, oh, p3.rearrange("p e t -> p t e").unsqueeze(2).to_broadcast([P, HN, TOPK, NE]),
                                                 ALU.mult))
                    tk = slice(TOPK * HN * h, TOPK * HN * (h + 1))
                    link(nc.vector.tensor_reduce(slotf[:, tk].rearrange("p (t k) -> p t k", t=HN), oh2, AX.X, ALU.add))
                    nc.vector.tensor_copy(srow[:, tk], slotf[:, tk]).then_inc(s.slots, 1)

                dve.wait_ge(s.logits, 1)
                route(0)
                route(1)
                nc.vector.tensor_copy(cnt[0], cnt[1]).then_inc(s.rows_taken, 1)
                dve.wait_ge(s.rows_taken, 1)
                link(nc.vector.tensor_tensor(
                    HITS.rearrange("p (e c) -> p e c", e=NE),
                    CST[:, C_ROW:C_ROW + RT].unsqueeze(1).to_broadcast([P, NE, RT]),
                    cnt[0].unsqueeze(2).to_broadcast([P, NE, RT]), ALU.is_ge))
                nc.vector.tensor_scalar(UNUSED, HITS, FAR, None, ALU.mult)
                g3 = gate.rearrange("p (t k) -> p t k", t=NT)
                nc.vector.tensor_tensor(g3, top8[:, :, 0:TOPK], top8[:, :, 0:1].to_broadcast([P, NT, TOPK]),
                                        ALU.subtract).then_inc(s.shifted, 1)
                dve.wait_ge(s.exps, 1)
                e3 = rtt[:, 3, 0:NT * TOPK]
                link(nc.vector.tensor_reduce(sm[:, 3, :], e3.rearrange("p (t k) -> p t k", t=NT), AX.X, ALU.add))
                link(nc.vector.reciprocal(sm[:, 4, :], sm[:, 3, :]))
                link(nc.vector.scalar_tensor_tensor(out=g3, in0=e3.rearrange("p (t k) -> p t k", t=NT), scalar=0.5,
                                                    in1=sm[:, 4, :].unsqueeze(2).to_broadcast([P, NT, TOPK]),
                                                    op0=ALU.mult, op1=ALU.mult))
                link(nc.vector.scalar_tensor_tensor(out=gate, in0=slotf, scalar=float(ROWS), in1=gate,
                                                    op0=ALU.is_lt, op1=ALU.mult))
                for st_ in range(2 * NCH):
                    c, m = st_ // 2, st_ % 2
                    dve.wait_ge(s.shared_silu, st_ + 1)
                    hs = SH[:, m, c * CH:c * CH + CH]
                    nc.vector.tensor_tensor(hs, hs, PS[:, 2 * m + 1, :], ALU.mult).then_inc(s.shared_hidden, 1)
                for c in range(NCH):
                    dve.wait_ge(s.shared_down, c + 1)
                    nc.vector.scalar_tensor_tensor(out=X[:, TPC * c:TPC * c + TPC, :].rearrange("p t d -> p (t d)"),
                                                   in0=PS[:, 6 + c % 2, :], scalar=0.5,
                                                   in1=X[:, TPC * c:TPC * c + TPC, :].rearrange("p t d -> p (t d)"),
                                                   op0=ALU.mult, op1=ALU.add).then_inc(s.shared_added, 1)

                def take_rows(e, b):
                    dve.wait_ge(s.turned, e + 1)
                    nc.vector.tensor_copy(XET[:, b, :], PS[:, b, 0:CAP]).then_inc(s.rows_taken, 1)

                def destinations(e, r, first=False):
                    b = r % 2
                    if not first:
                        dve.wait_ge(SO[b], 16 * RT * (e // 2 + sent))
                    nc.vector.scalar_tensor_tensor(
                        out=HIT[:, :, :], in0=XE[:, r, :, P:P + TOPK], scalar=CST[:, bass.ds(C_I32 + e, 1)],
                        in1=XE[:, r, :, P + TOPK:PW], op0=ALU.is_equal, op1=ALU.mult).then_inc(s.dest_chain, 1)
                    dve.wait_ge(s.dest_chain, 2 * e + 1)
                    nc.vector.tensor_reduce(DST[:, b, :], HIT[:, :, :], AX.X, ALU.add).then_inc(s.dest_chain, 1)
                    dve.wait_ge(s.dest_chain, 2 * e + 2)
                    nc.vector.tensor_tensor(DI[:, b, :], DST[:, b, :], UNUSED[:, bass.ds(RT * e, RT)], ALU.add).then_inc(s.destinations, 1)

                sent = 0 if i == 3 else NE // 2

                def hidden(e, b, first=False):
                    for m in range(2):
                        dve.wait_ge(s.silu, e * 2 + (m + 1))
                        if not first and m == 0:
                            dve.wait_ge(s.down, e - 1)
                        nc.vector.tensor_tensor(HT[:, b, m, :], SIL[:, m, :], PS[:, 3 + 2 * m, 0:CAP],
                                                ALU.mult).then_inc(s.hidden, 1)

                for e in range(RING):
                    take_rows(e, e % 2)
                    if e:
                        hidden(e - 1, (e - 1) % 2, first=e <= 2)
                        destinations(e - 1, e - 1, first=e <= 2)
                with dve.Fori(1, NE // RING) as u:
                    for r in range(RING):
                        take_rows(u * RING + r, r % 2)
                        hidden(u * RING + (r - 1), (r - 1) % 2)
                        destinations(u * RING + (r - 1), (r - 1) % RING)
                hidden(NE - 1, (NE - 1) % 2)
                destinations(NE - 1, RING - 1)
                for t0 in range(0, NT, GT):
                    dve.wait_ge(GA[t0 // GT], 16 * (1 if i == 3 else 2))
                    for k in range(TOPK):
                        for t in range(t0, t0 + GT):
                            j = TOPK * t + k
                            last = nc.vector.scalar_tensor_tensor(out=X[:, t, :], in0=GB[:, j, :], scalar=gate[:, j:j + 1],
                                                                  in1=X[:, t, :], op0=ALU.mult, op1=ALU.add)
                        if k < TOPK - 1:
                            link(last)
                    last.then_inc(s.summed, 1)
                dve.wait_ge(s.summed, NT // GT)
                nc.vector.tensor_copy(km[:, 7:8], X[:, 0, 0:1]).then_inc(s_x_ready, 1)

            for i in range(stages):
                norm(i, XNA if i in (1, 4) else XN)
                if i == 0:
                    setup()
                if i in (0, 2):
                    ffn0(i)
                elif i in AS:
                    attention(i)
                else:
                    routed(i)

        @block.scalar
        def _(act):
            def setup_ffn0():
                act.wait_ge(SET.mm1, 1)
                nc.scalar.copy(wt[:, 0, :], PS[:, 0, 0:P])
                nc.scalar.copy(wcat[:, 2 * P:2 * P + E0], PS[:, 0, P:P + E0]).then_inc(SET.cp1, 1)
                act.wait_ge(SET.mm2, 1)
                nc.scalar.copy(wcat[:, 0:2 * P], PS[:, 4, 0:2 * P]).then_inc(SET.cp2, 1)

            def setup_centroids():
                act.wait_ge(SET.squares, 1)
                nc.scalar.activation(cst1[:, 1:2], cst1[:, 0:1], ACT.Sqrt).then_inc(SET.centroid_roots, 1)

            def setup():
                act.wait_ge(SET.mm1, 2)
                nc.scalar.copy(wt[:, 1, :], PS[:, 0, 2 * P:3 * P])
                nc.scalar.mul(w1[:, 0:2, :].rearrange("p a b -> p (a b)"), PS[:, 1, 0:2 * P], float(HD) ** -0.5)
                nc.scalar.copy(w1[:, 2:4, :].rearrange("p a b -> p (a b)"), PS[:, 1, 2 * P:4 * P])
                nc.scalar.copy(w1[:, 4, :], PS[:, 2, 0:P]).then_inc(SET.cp1, 1)
                for n in range(2):
                    nc.scalar.copy(w0[:, n, :].rearrange("p (q d j) -> p q j d", q=QUADS, j=4),
                                   raw0[:, n, :].rearrange("p (q j d) -> p q j d", q=QUADS, j=4))
                act.wait_ge(SET.mm2, 2)
                nc.scalar.copy(wo[:, 0, :, :].rearrange("p a b -> p (a b)"), PS[:, 5, :])
                nc.scalar.copy(wo[:, 1, :, :].rearrange("p a b -> p (a b)"), PS[:, 6, :])
                nc.scalar.copy(bcol[:, 0:4], PS[:, 7, 0:4])
                nc.scalar.mul(bcol[:, 4:5], PS[:, 7, 4:5], float(HD) ** -0.5)
                nc.scalar.copy(bcol[:, 5:6], PS[:, 7, 5:6]).then_inc(ach, 1)
                act.wait_ge(ach, 1)
                nc.scalar.mul(bcol[:, 2:3], bcol[:, 2:3], float(HD) ** -0.5)
                act.wait_ge(SET.centroids_turned, 1)
                nc.scalar.copy(r40[:, :], PS[:, 3, 0:NG + NE]).then_inc(SET.cp2, 1)

            def deviations(i):
                if i:
                    nc.scalar.activation(km[:, 5:6], CST[:, C_ONE:C_ONE + 1], ACT.Sqrt)
                act.wait_ge(NS.var, i + 1)
                nc.scalar.activation(sm[:, 1, :], sm[:, 0, :], ACT.Sqrt).then_inc(NS.std, 1)
                if i in MS:
                    act.wait_ge(MS[i].squares, 1)
                    nc.scalar.activation(sm[:, 4, :], sm[:, 3, :], ACT.Sqrt).then_inc(MS[i].l2_norms, 1)

            def norm(i):
                s = NS
                if i:
                    deviations(i)
                for c in range(NCH):
                    act.wait_ge(s.in_psum, NCH * i + c + 1)
                    nc.scalar.copy(XNT[:, c * CH:c * CH + CH], PS[:, c, :]).then_inc(s.turned, 1)

            def ffn0(i):
                s, done = FS, i // 2
                act.wait_ge(s.shifted, done + 1)
                nc.scalar.activation(V[:, 1, :], V[:, 0, :], ACT.Exp).then_inc(s.exps, 1)

            def attention(i):
                s = AS[i]
                rope = i == 4
                def square(n):
                    z, w = (t1_, wk_) if n < NCH else (t2_, wq_)
                    cs = slice(n % NCH * CH, n % NCH * CH + CH)
                    act.wait_ge(s.squares, n + 1)
                    nc.scalar.activation(z[:, cs], w[:, cs], ACT.Square).then_inc(s.squared, 1)

                def high(n):
                    w, part = (wk_, KP[:, 0, :]) if n < NCH else (wq_, QP[:, 2, :])
                    cs = slice(n % NCH * CH, n % NCH * CH + CH)
                    if not rope:
                        act.wait_ge(s.unit, n + 1)
                    nc.scalar.copy(part[:, cs], w[:, cs]).then_inc(s.high, 1)

                def middle(n):
                    w, part = (wk_, KP[:, 1, :]) if n < NCH else (wq_, QP[:, 1, :])
                    cs = slice(n % NCH * CH, n % NCH * CH + CH)
                    act.wait_ge(s.rest, n + 1)
                    nc.scalar.copy(part[:, cs], w[:, cs]).then_inc(s.middle, 1)

                KC, QC = range(NCH), range(NCH, 2 * NCH)
                if rope:
                    for n in KC:
                        square(n)
                        high(n)
                    for n in KC:
                        middle(n)
                    for n in QC:
                        square(n)
                    act.wait_ge(s.banks_free, 2 * NCH)
                    for n in QC:
                        high(n)
                    for c in range(NCH):
                        cs = slice(c * CH, c * CH + CH)
                        act.wait_ge(s.inverse, c + 1)
                        nc.scalar.activation(t1_[:, cs], t1_[:, cs], ACT.Sqrt).then_inc(s.roots, 1)
                    for n in QC:
                        middle(n)
                else:
                    for n in (*KC, *QC):
                        square(n)
                    for n, z in enumerate((t1_, t2_)):
                        act.wait_ge(s.head_sums, n + 1)
                        nc.scalar.activation(z[:, 0:CH], PS[:, n, :], ACT.Sqrt).then_inc(s.roots, 1)
                    for side in (KC, QC):
                        for n in side:
                            high(n)
                        for n in side:
                            middle(n)
                nc.scalar.activation(km[:, 5:6], bcol[:, 7:8], ACT.Exp)
                act.wait_ge(s.parts, 3)
                with act.Fori(0, ITERS // 2) as u:
                    for g in range(2 * CHUNKS):
                        act.wait_ge(s.scores, u * (2 * CHUNKS) + (g + 1))
                        nc.scalar.activation(PR[:, g % PRING, :], PS[:, 2 * (g % 2):2 * (g % 2) + 2, :].rearrange("p a b -> p (a b)"),
                                             ACT.Exp).then_inc(s.exps, 1)

            def routed(i):
                s = MS[i]
                act.wait_ge(s.shifted, 1)
                nc.scalar.activation(rtt[:, 3, 0:NT * TOPK], gate, ACT.Exp).then_inc(s.exps, 1)
                for st_ in range(2 * NCH):
                    c, m = st_ // 2, st_ % 2
                    act.wait_ge(s.gate_up, st_ + 1)
                    nc.scalar.activation(SH[:, m, c * CH:c * CH + CH], PS[:, 2 * m, :], ACT.Silu).then_inc(s.shared_silu, 1)

                def gates(e):
                    for m in range(2):
                        act.wait_ge(s.gate_up, e * 2 + (2 * NCH + m + 1))
                        nc.scalar.activation(SIL[:, m, :], PS[:, 2 + 2 * m, 0:CAP], ACT.Silu).then_inc(s.silu, 1)

                stored = 0 if i == 3 else NE // 2

                def take_out(e, b, again):
                    act.wait_ge(s.down, e + 1)
                    if again is not None:
                        act.wait_ge(SO[b], (again + stored) * (16 * RT))
                    nc.scalar.copy(OB[:, b, 0:RT - 1, :].rearrange("p c d -> p (c d)"), PS[:, 6 + b, 0:(RT - 1) * P])
                    nc.scalar.copy(OB[0:TAIL, b, RT - 1, :], PS[0:TAIL, 6 + b, (RT - 1) * P:RT * P]).then_inc(s.results, 1)

                gates(0)
                gates(1)
                take_out(0, 0, None)
                gates(2)
                take_out(1, 1, None)
                with act.Fori(1, NE // RING) as u:
                    for r in range(RING):
                        gates(u * RING + (r - 1))
                        take_out(u * RING + (r - 2), r % 2, u * 2 + (r // 2 - 1))
                gates(NE - 1)
                for e in (NE - 2, NE - 1):
                    take_out(e, e % 2, e // 2)
                if i == 3:
                    act.wait_ge(s.shared_added, NCH)
                    act.dma_start(COS, cos_d).then_inc(s_tab, 16)
                    act.dma_start(SIN, sin_d).then_inc(s_tab, 16)

            deviations(0)
            setup_ffn0()
            for i in range(stages):
                norm(i)
                if i == 0:
                    setup_centroids()
                if i in (0, 2):
                    ffn0(i)
                    if i == 0:
                        setup()
                elif i in AS:
                    attention(i)
                else:
                    routed(i)

        @block.tensor
        def _(pe):
            def setup_ffn0():
                pe.wait_ge(s_first, FIRST_IN)
                nc.tensor.transpose(PS[:, 0, 0:P], raw[:, 2, :], ident)
                nc.tensor.transpose(PS[:, 0, P:P + E0], cen2[0:E0, :], ident[0:E0, 0:E0]).then_inc(SET.mm1, 1)
                pe.wait_ge(SET.cp1, 1)
                for e in range(2):
                    last = nc.tensor.matmul(PS[:, 4, P * e:P * e + P], raw[:, e, :], wt[:, 0, :], start=True, stop=True)
                last.then_inc(SET.mm2, 1)
                pe.wait_ge(SET.cp2, 1)

            def setup():
                pe.wait_ge(s_in, ALL_IN)
                pe.wait_ge(FS.banks_free, NT // 2)
                nc.tensor.transpose(PS[:, 0, 2 * P:3 * P], raw[:, 7, :], ident)
                nc.tensor.matmul(PS[:, 1, 0:2 * P], raw[:, 4, :], CS[:, S_PERM:S_PERM + 2 * P], start=True, stop=True)
                nc.tensor.matmul(PS[:, 1, 2 * P:4 * P], raw[:, 5, :], CS[:, S_PERM:S_PERM + 2 * P], start=True, stop=True)
                nc.tensor.matmul(PS[:, 2, 0:P], raw[:, 6, :], ident, start=True, stop=True).then_inc(SET.mm1, 1)
                pe.wait_ge(SET.cp1, 2)
                for q in range(QUADS):
                    pad = CS[:, S_PAD + q * P:S_PAD + q * P + P]
                    nc.tensor.matmul(PS[:, 5, P * q:P * q + P], pad, raw[:, 3, :], start=True, stop=True)
                    nc.tensor.matmul(PS[:, 6, P * q:P * q + P], pad, wt[:, 1, :], start=True, stop=True)
                nc.tensor.matmul(PS[:, 7, 0:4], CS[:, S_PERM:S_PERM + P], bcol[:, 0:4], start=True, stop=True)
                last = nc.tensor.matmul(PS[:, 7, 4:6], CS[:, S_ROT:S_ROT + P], bcol[:, 2:4], start=True, stop=True)
                last.then_inc(SET.mm2, 1)
                pe.wait_ge(SET.unit_centroids, 1)
                nc.tensor.transpose(PS[:, 3, 0:NG + NE], cen, ident[0:NG + NE, 0:NG + NE]).then_inc(SET.centroids_turned, 1)
                pe.wait_ge(SET.cp2, 2)

            def norm(i, XNi):
                s = NS
                for t in range(NT):
                    pe.wait_ge(s.normalised, NT * i + t + 1)
                    last = nc.tensor.transpose(PS[:, t // TPC, P * (t % TPC):P * (t % TPC) + P], XNi[:, t, :], ident)
                    if t % TPC == TPC - 1:
                        last.then_inc(s.in_psum, 1)

            def ffn0(i):
                s, n, done = FS, NS, i // 2
                for t in range(NT):
                    if t % TPC == 0:
                        pe.wait_ge(n.turned, NCH * i + t // TPC + 1)
                    last = nc.tensor.matmul(PS[:, 4, E0 * t:E0 * t + E0], XNT[:, P * t:P * t + P], wcat[:, 2 * P:],
                                            start=True, stop=True)
                last.then_inc(s.gates, 1)
                for t in range(NT):
                    pr = t // 2
                    if t % 2 == 0 and pr >= 3:
                        pe.wait_ge(s.banks_free, done * (NT // 2) + pr - 2)
                    last = nc.tensor.matmul(PS[:, 5 + pr % 3, 2 * P * (t % 2):2 * P * (t % 2) + 2 * P],
                                            XNT[:, P * t:P * t + P], wcat[:, 0:2 * P], start=True, stop=True)
                    if t % 2:
                        last.then_inc(s.products, 1)

            def attention(i):
                s, n = AS[i], NS
                rope = i == 4
                w = w1 if rope else w0
                loaded = QUAD_LOADED * (2 if rope else 1)
                pe.wait_ge(n.turned, NCH * i + NCH)
                for m in range(2 * NCH):
                    c = m % NCH
                    cs = slice(c * CH, c * CH + CH)
                    if rope:
                        if m >= NCH:
                            pe.wait_ge(s.banks_free, c + 1)
                        for k in range(2):
                            last = nc.tensor.matmul(PS[:, 2 * c + k, :], w1[:, (2 if m < NCH else 0) + k, :], XNT[:, cs],
                                                    start=True, stop=True)
                    else:
                        last = nc.tensor.matmul(PS[:, m, :], w0[:, 1 if m < NCH else 0, :], XNT[:, cs], start=True, stop=True)
                    last.then_inc(s.projected, 1)
                if rope:
                    pe.wait_ge(s.banks_free, 2 * NCH)
                    for m in range(2 * NCH):
                        cs = slice(m % NCH * CH, m % NCH * CH + CH)
                        pe.wait_ge(s.squared, m + 1)
                        nc.tensor.matmul(PS[:, m, :], G, (t1_, t2_)[m // NCH][:, cs], start=True, stop=True).then_inc(s.head_sums, 1)
                    pe.wait_ge(s.flag, 1)
                else:
                    for m in range(2 * NCH):
                        c = m % NCH
                        pe.wait_ge(s.squared, m + 1)
                        last = nc.tensor.matmul(PS[32 * c:32 * c + 32, m // NCH, :], CST[:, C_SUM:C_SUM + 32],
                                                (t1_, t2_)[m // NCH][:, c * CH:c * CH + CH], start=True, stop=True,
                                                tile_position=(0, 32 * c))
                        if c == NCH - 1:
                            last.then_inc(s.head_sums, 1)
                    for m in range(2 * NCH):
                        c, side = m % NCH, m // NCH
                        if c == 0:
                            pe.wait_ge(s.inverse, side + 1)
                        if side:
                            pe.wait_ge(s.roots, 2)
                        nc.tensor.matmul(PS[:, (NCH if side == 0 else 0) + c, :], CST[:, C_SPREAD + c * P:C_SPREAD + c * P + P],
                                         (t1_, t2_)[side][:, 0:CH], start=True, stop=True).then_inc(s.spread, 1)
                    pe.wait_ge(s.unit, 2 * NCH)
                    pe.wait_ge(s.flag, 1)
                nc.tensor.transpose(PS[0:1, 0, 0:P], km[:, 7:8], ident).then_inc(s.flag_row, 1)
                if rope:
                    pe.wait_ge(s.inverse, NCH)
                pe.wait_ge(s.flag, 2)
                for t in range(NT):
                    last = nc.tensor.matmul(PS[:, t // TPC, P * (t % TPC):P * (t % TPC) + P], XNT[:, P * t:P * t + P],
                                            w[:, 4 if rope else 2, :], start=True, stop=True)
                    if t % TPC == TPC - 1:
                        last.then_inc(s.values, 1)

                def scores(it, g):
                    kt, half = g // 2, g % 2
                    pair = (it // NCH) * 2 + half
                    for k in range(2):
                        j = 2 * half + k
                        last = nc.tensor.matmul(
                            PS[:, 2 * half + k, :],
                            Kt[:, bass.ds(pair, 1), P * kt:P * kt + P].rearrange("p o n -> p (o n)"),
                            Qt[:, bass.ds(it, 1), j, :].rearrange("p o n -> p (o n)"), start=True, stop=True)
                    last.then_inc(s.scores, 1)

                def weigh(b, kt, half):
                    for j in range(4):
                        p0 = CH * (j % 2) + half * (CH // 2)
                        last = nc.tensor.matmul(PS[32 * j:32 * j + VW, 4 + 2 * b + half, 0:CH // 2], VQ[:, b, kt, j, :],
                                                PR[:, (b * CHUNKS + 2 * kt + j // 2) % PRING, p0:p0 + CH // 2],
                                                start=(kt == 0), stop=(kt == NT - 1), tile_position=(0, 32 * j))
                    if kt == NT - 1 and half:
                        last.then_inc(s.out_ready, 1)

                def iteration(it, b, first=False, final=False):
                    for kt in range(NT):
                        for half in range(2):
                            g = 2 * kt + half
                            pe.wait_ge(s.exps, it * CHUNKS + (g + 1))
                            if kt < NT - 1:
                                scores(it, g + 2)
                            elif not final:
                                scores(it + 1, half)
                            if kt == 1 and half == 0:
                                pe.wait_ge(s.v_ready, it + 1)
                            if kt:
                                weigh(b, kt - 1, half)
                            elif not first:
                                weigh(1 - b, NT - 1, half)
                    if final:
                        for half in range(2):
                            weigh(b, NT - 1, half)

                pe.wait_ge(LQ[0], loaded)
                pe.wait_ge(s.v_ready, 2)
                with pe.If(bound_is_large(pe, s)):
                    for l in LQ[1:]:
                        pe.wait_ge(l, loaded)
                    with pe.Fori(0, ITERS) as u:
                        for k in range(4 * TPC):
                            j, t = k // TPC, k % TPC
                            pe.wait_ge(s.maxima, u * (4 * TPC) + (k + 1))
                            for c in range(NCH):
                                last = nc.tensor.matmul(
                                    PS[:, 4 * (k % 2) + c, :],
                                    Qt[:, bass.ds(u, 1), j, P * t:P * t + P].rearrange("p o n -> p (o n)"),
                                    Kt[:, bass.ds((u // NCH) * 2 + j // 2, 1), CH * c:CH * c + CH].rearrange("p o n -> p (o n)"),
                                    start=True, stop=True)
                            last.then_inc(s.max_scores, 1)
                    pe.wait_ge(s.maxima, MAX_STEPS + 2)
                    for k in range(2):
                        last = nc.tensor.transpose(PS[:, 0, P * k:P * k + P], MX[:, P * k:P * k + P], ident)
                    last.then_inc(s.max_scores, 1)
                    pe.wait_ge(s.maxima, MAX_STEPS + 4)
                    pe.wait_ge(s.maxima_in_qt, 16 * (1 + NH))
                scores(0, 0)
                scores(0, 1)
                iteration(0, 0, first=True)
                iteration(1, 1)
                for l in LQ[1:]:
                    pe.wait_ge(l, loaded)
                with pe.Fori(1, ITERS // 2 - 1) as u:
                    for b in range(2):
                        iteration(2 * u + b, b)
                iteration(ITERS - 2, 0)
                iteration(ITERS - 1, 1, final=True)
                pe.wait_ge(s.out_steps, 4 * (ITERS - 1))
                for t in range(NT):
                    if t == NT - TPC:
                        pe.wait_ge(s.heads_done, 1)
                    for q in range(QUADS):
                        last = nc.tensor.matmul(PS[:, t // TPC, P * (t % TPC):P * (t % TPC) + P],
                                                AT[:, NCH * q + t // TPC, P * (t % TPC):P * (t % TPC) + P],
                                                wo[:, 1 if rope else 0, q, :], start=(q == 0), stop=(q == QUADS - 1))
                    if t % TPC == TPC - 1:
                        last.then_inc(s.values, 1)

            def routed(i):
                s, n = MS[i], NS
                W = NG + NE
                for t in range(NT):
                    if t % TPC == 0:
                        pe.wait_ge(n.turned, NCH * i + t // TPC + 1)
                    last = nc.tensor.matmul(PS[:, 4 + t // 8, W * (t % 8):W * (t % 8) + W], XNT[:, P * t:P * t + P], r40[:, :],
                                            start=True, stop=True)
                last.then_inc(s.logits, 1)
                for h in range(2):
                    pe.wait_ge(s.members, h + 1)
                    part = slice(NE * NT // 2 * h, NE * NT // 2 * (h + 1))
                    nc.tensor.matmul(PS[:, 6, part], U16[:, 0, :], M16[:, part], start=True, stop=True)
                    nc.tensor.matmul(PS[:, 7, part], U16[:, 1, :], M16[:, part], start=True, stop=True).then_inc(s.counted, 1)
                pe.wait_ge(s.shared_weights, 48)
                for st_ in range(2 * NCH):
                    c, m = st_ // 2, st_ % 2
                    if c:
                        pe.wait_ge(s.shared_hidden, st_ - 1)
                    for k in range(2):
                        last = nc.tensor.matmul(PS[:, 2 * m + k, :], ws[:, k, P * m:P * m + P], XNT[:, c * CH:c * CH + CH],
                                                start=True, stop=True)
                    last.then_inc(s.gate_up, 1)
                pe.wait_ge(s.slots, 2)
                for t in range(NT):
                    c = t // TPC
                    if t % TPC == 0:
                        pe.wait_ge(s.shared_hidden, 2 * c + 2)
                        if c >= 2:
                            pe.wait_ge(s.shared_added, c - 1)
                    for m in range(2):
                        last = nc.tensor.matmul(PS[:, 6 + c % 2, P * (t % TPC):P * (t % TPC) + P], SH[:, m, P * t:P * t + P],
                                                wsd[:, m, :], start=(m == 0), stop=(m == 1))
                    if t % TPC == TPC - 1:
                        last.then_inc(s.shared_down, 1)
                pe.wait_ge(s.shared_hidden, 2 * NCH)
                pe.wait_ge(s.shared_added, NCH)

                before = 0 if i == 3 else NE // RING

                def turn(u, r, first):
                    b = r % 2
                    pe.wait_ge(LX[r], (u + before) * 16 + 16)
                    if not first:
                        pe.wait_ge(s.rows_taken, u * RING + r)
                    for c in range(RT):
                        n_ = P if c < RT - 1 else TAIL
                        last = nc.tensor.transpose(PS[:, b, P * c:P * c + n_], XE[0:n_, r, c, 0:P], ident[0:n_, 0:n_])
                    last.then_inc(s.turned, 1)

                def up(e, u, r, first=False):
                    b = r % 2
                    pe.wait_ge(s.rows_taken, e + 2)
                    pe.wait_ge(LW[r], (u + before) * 48 + 48)
                    for m in range(2):
                        if not first:
                            pe.wait_ge(s.hidden, e * 2 + (m - 1))
                        for k in range(2):
                            last = nc.tensor.matmul(PS[:, 2 + 2 * m + k, 0:CAP], WRING[:, r, HID * k + P * m:HID * k + P * m + P],
                                                    XET[:, b, :], start=True, stop=True)
                        last.then_inc(s.gate_up, 1)

                def down(e, r, first=False):
                    b = r % 2
                    pe.wait_ge(s.hidden, e * 2 + 2)
                    if not first:
                        pe.wait_ge(s.results, e - 1)
                    for c in range(RT):
                        n_ = P if c < RT - 1 else TAIL
                        for m in range(2):
                            last = nc.tensor.matmul(PS[0:n_, 6 + b, P * c:P * c + P], HT[:, b, m, P * c:P * c + n_],
                                                    WRING[:, r, 2 * HID + P * m:2 * HID + P * m + P],
                                                    start=(m == 0), stop=(m == 1))
                    last.then_inc(s.down, 1)

                for r in range(RING):
                    turn(0, r, r < 2)
                    if r >= 1:
                        up(r - 1, 0, r - 1, first=(r == 1))
                    if r >= 2:
                        down(r - 2, r - 2, first=True)
                with pe.Fori(1, NE // RING) as u:
                    for r in range(RING):
                        turn(u, r, False)
                        up(u * RING + (r - 1), u if r else u - 1, (r - 1) % RING)
                        down(u * RING + (r - 2), (r - 2) % RING)
                up(NE - 1, NE // RING - 1, RING - 1)
                down(NE - 2, RING - 2)
                down(NE - 1, RING - 1)

            setup_ffn0()
            for i in range(stages):
                norm(i, XNA if i in (1, 4) else XN)
                if i in (0, 2):
                    ffn0(i)
                    if i == 0:
                        setup()
                elif i in AS:
                    attention(i)
                else:
                    routed(i)


_INS = ['L0_attn_x', 'L0_attn_Wq', 'L0_attn_bq', 'L0_attn_Wk', 'L0_attn_bk', 'L0_attn_Wv', 'L0_attn_bv', 'L0_attn_Wo',
        'L0_attn_bo', 'L0_attn_qk_scale', 'L0_ffn_gate_W', 'L0_ffn_expert_W', 'L0_ffn_out_W', 'L1_attn_Wqkv',
        'L1_attn_bqkv', 'L1_attn_Wout', 'L1_attn_bout', 'L1_ffn_group_centroids', 'L1_ffn_expert_centroids',
        'L1_ffn_bias', 'L1_ffn_wg', 'L1_ffn_wu', 'L1_ffn_wd', 'L1_ffn_sg', 'L1_ffn_su', 'L1_ffn_sd']


def kernel(**inputs):
    import concourse.bacc as bacc
    from concourse.bass_utils import run_bass_kernel_spmd

    nc = bacc.Bacc("TRN2", target_bir_lowering=False, num_devices=1)
    arrays = {f"in_{n}_dram": np.ascontiguousarray(inputs[n]) for n in _INS}
    arrays.update(zip(("consts_dram", "setup_dram", "cos_dram", "sin_dram"), constants()))
    aps = {n: nc.dram_tensor(n, v.shape, mybir.dt.from_np(v.dtype), kind="ExternalInput").ap()
           for n, v in arrays.items()}
    out = nc.dram_tensor("out_dram", (1, NTOK, P), F32, kind="ExternalOutput").ap()
    build(nc, {n: aps[f"in_{n}_dram"] for n in _INS}, aps["consts_dram"], aps["setup_dram"], aps["cos_dram"], aps["sin_dram"], out)
    r = run_bass_kernel_spmd(nc, [arrays], core_ids=[0])
    return r.results[0]["out_dram"]
```
